# Optimizing a Trainium2 kernel written in Bass

```python
import numpy as np
import jax
import jax.numpy as jnp

def _softmax(x, axis=-1):
    return jax.nn.softmax(x, axis=axis)

def _gelu(x):
    return jax.nn.gelu(x, approximate=True)

def _silu(x):
    return jax.nn.silu(x)

def _sigmoid(x):
    return jax.nn.sigmoid(x)

def _layernorm(x, axis=-1, eps=1e-05):
    m = jnp.mean(x, axis=axis, keepdims=True)
    v = jnp.var(x, axis=axis, keepdims=True)
    return (x - m) / jnp.sqrt(v + eps)

def _scatter_add(tgt, idx, src, axis=0):
    return tgt.at[idx].add(src)

def _segment_sum(src, seg, n):
    return jax.ops.segment_sum(src, seg, n)
kernel_name = 'mk_hybrid_d1_jaxref_r8_c911b9'

def setup_inputs(seed: int=0):
    np.random.seed(seed)
    _w = jnp.asarray

    def _L0_attn_a_setup():
        import jax, jax.numpy as jnp
        import numpy as np
        EPS = 1e-05
        DT_RANK = 64
        N_STATE = 16

        def _rmsnorm(x, w):
            var = jnp.mean(x * x, axis=-1, keepdims=True)
            return x * jax.lax.rsqrt(var + EPS) * w

        def _softplus(x, beta=1.0, threshold=20.0):
            return jnp.where(beta * x > threshold, x, 1.0 / beta * jnp.logaddexp(0.0, beta * x))

        def _silu(x):
            return x * jax.nn.sigmoid(x)

        def _scan_combine(left, right):
            aL, xL = left
            aR, xR = right
            return (aR * aL, aR * xL + xR)
        key = jax.random.key(seed)
        ks = jax.random.split(key, 8)
        B, L, H = (2, 128, 256)
        s = 0.02
        A = jnp.tile(jnp.arange(1.0, N_STATE + 1.0)[None, :], (H, 1))
        return {'x': jax.random.normal(ks[0], (B, L, H), jnp.float32), 'norm_w': jnp.ones((H,), jnp.float32), 'in_proj_w': jax.random.normal(ks[1], (2 * H, H), jnp.float32) * s, 'conv_w': jax.random.normal(ks[2], (4, H, H), jnp.float32) * s, 'conv_b': jnp.zeros((H,), jnp.float32), 'x_proj_w': jax.random.normal(ks[3], (DT_RANK + 2 * N_STATE, H), jnp.float32) * s, 'dt_proj_w': jax.random.normal(ks[4], (H, DT_RANK), jnp.float32) * s, 'dt_proj_b': jnp.zeros((H,), jnp.float32), 'A_log': jnp.log(A), 'D': jnp.ones((H,), jnp.float32), 'out_proj_w': jax.random.normal(ks[5], (H, H), jnp.float32) * s}
    _L0_attn_a_in = _L0_attn_a_setup()

    def _L0_attn_b_setup():
        import jax, jax.numpy as jnp
        import numpy as np
        D_MODEL = 256
        D_STATE = 64
        EXPAND = 2
        N_HEADS = 64
        NGROUPS = 1
        CHUNK = 32
        D_INNER = EXPAND * D_MODEL
        HEAD_DIM = D_INNER // N_HEADS
        BC = NGROUPS * D_STATE
        D_PROJ = 2 * D_INNER + 2 * BC + 2 * N_HEADS + D_STATE // 2
        SCALE = D_STATE ** (-0.5)
        EPS = 1e-06
        BATCH, T = (2, 256)

        def _rms_norm(x):
            return x * jax.lax.rsqrt(jnp.mean(x * x, axis=-1, keepdims=True) + EPS)

        def _rope_pairs(x, cos, sin):
            h = x.shape[-1] // 2
            x1, x2 = (x[..., :h], x[..., h:])
            return jnp.concatenate([x1 * cos - x2 * sin, x1 * sin + x2 * cos], axis=-1)

        def _segsum(v):
            L = v.shape[-1]
            cs = jnp.cumsum(v, axis=-1)
            d = cs[..., :, None] - cs[..., None, :]
            mask = jnp.tril(jnp.ones((L, L), dtype=bool))
            return jnp.where(mask, d, -jnp.inf)

        def _ssd_chunked(x, A, Bm, Cm, dt):
            b, Tt, H, P = x.shape
            rep = H // NGROUPS
            Bh = jnp.repeat(Bm, rep, axis=2)
            Ch = jnp.repeat(Cm, rep, axis=2) * SCALE
            c = Tt // CHUNK
            xd = (x * dt[..., None]).reshape(b, c, CHUNK, H, P)
            Bh = Bh.reshape(b, c, CHUNK, H, D_STATE)
            Ch = Ch.reshape(b, c, CHUNK, H, D_STATE)
            dA = (dt * A).reshape(b, c, CHUNK, H)
            Acs = jnp.cumsum(dA, axis=2)
            Lm = jnp.exp(_segsum(jnp.moveaxis(dA, 3, 2)))
            Y_diag = jnp.einsum('bclhn,bcshn,bchls,bcshp->bclhp', Ch, Bh, Lm, xd)
            decay_states = jnp.exp(Acs[:, :, -1:, :] - Acs)
            states = jnp.einsum('bclhn,bclh,bclhp->bchpn', Bh, decay_states, xd)
            chunk_decay = jnp.exp(Acs[:, :, -1])

            def step(h, inp):
                dec, s = inp
                return (h * dec[:, :, None, None] + s, h)
            h0 = jnp.zeros((b, H, P, D_STATE), x.dtype)
            _, prev = jax.lax.scan(step, h0, (jnp.moveaxis(chunk_decay, 1, 0), jnp.moveaxis(states, 1, 0)))
            prev = jnp.moveaxis(prev, 0, 1)
            Y_off = jnp.einsum('bclhn,bchpn,bclh->bclhp', Ch, prev, jnp.exp(Acs))
            return (Y_diag + Y_off).reshape(b, Tt, H, P)
        key = jax.random.key(seed)
        k = jax.random.split(key, 4)
        x = jax.random.normal(k[0], (BATCH, T, D_MODEL), dtype=jnp.float32)
        W_in = jax.random.normal(k[1], (D_MODEL, D_PROJ), dtype=jnp.float32) * D_MODEL ** (-0.5)
        W_out = jax.random.normal(k[2], (D_INNER, D_MODEL), dtype=jnp.float32) * D_INNER ** (-0.5)
        A_log = jnp.zeros((N_HEADS,), jnp.float32)
        dt_bias = jnp.zeros((N_HEADS,), jnp.float32)
        B_norm_bias = jnp.ones((NGROUPS, D_STATE), jnp.float32)
        C_norm_bias = jnp.ones((NGROUPS, D_STATE), jnp.float32)
        return {'x': x, 'W_in': W_in, 'A_log': A_log, 'dt_bias': dt_bias, 'B_norm_bias': B_norm_bias, 'C_norm_bias': C_norm_bias, 'W_out': W_out}
    _L0_attn_b_in = _L0_attn_b_setup()

    def _L0_ffn_setup():
        import jax, jax.numpy as jnp
        import numpy as np
        TOP_K = 2
        EPS = 1e-06
        key = jax.random.key(seed)
        ks = jax.random.split(key, 5)
        B, S, D, E = (4, 256, 256, 8)
        sd = 1.0 / np.sqrt(D)
        return {'x': jax.random.normal(ks[0], (B, S, D), jnp.float32), 'router_w': jax.random.normal(ks[1], (D, E), jnp.float32) * sd, 'router_b': jnp.zeros((E,), jnp.float32), 'expert_w': jax.random.normal(ks[2], (E, D, D), jnp.float32) * sd, 'expert_b': jnp.zeros((E, D), jnp.float32), 'proj_w': jax.random.normal(ks[3], (D, D), jnp.float32) * sd, 'proj_b': jnp.zeros((D,), jnp.float32), 'norm_w': jnp.ones((D,), jnp.float32)}
    _L0_ffn_in = _L0_ffn_setup()
    _d = {'L0_attn_a_x': _L0_attn_a_in['x'], 'L0_attn_a_norm_w': _L0_attn_a_in['norm_w'], 'L0_attn_a_in_proj_w': _L0_attn_a_in['in_proj_w'], 'L0_attn_a_conv_w': _L0_attn_a_in['conv_w'], 'L0_attn_a_conv_b': _L0_attn_a_in['conv_b'], 'L0_attn_a_x_proj_w': _L0_attn_a_in['x_proj_w'], 'L0_attn_a_dt_proj_w': _L0_attn_a_in['dt_proj_w'], 'L0_attn_a_dt_proj_b': _L0_attn_a_in['dt_proj_b'], 'L0_attn_a_A_log': _L0_attn_a_in['A_log'], 'L0_attn_a_D': _L0_attn_a_in['D'], 'L0_attn_a_out_proj_w': _L0_attn_a_in['out_proj_w'], 'L0_attn_b_W_in': _L0_attn_b_in['W_in'], 'L0_attn_b_A_log': _L0_attn_b_in['A_log'], 'L0_attn_b_dt_bias': _L0_attn_b_in['dt_bias'], 'L0_attn_b_B_norm_bias': _L0_attn_b_in['B_norm_bias'], 'L0_attn_b_C_norm_bias': _L0_attn_b_in['C_norm_bias'], 'L0_attn_b_W_out': _L0_attn_b_in['W_out'], 'L0_ffn_router_w': _L0_ffn_in['router_w'], 'L0_ffn_router_b': _L0_ffn_in['router_b'], 'L0_ffn_expert_w': _L0_ffn_in['expert_w'], 'L0_ffn_expert_b': _L0_ffn_in['expert_b'], 'L0_ffn_proj_w': _L0_ffn_in['proj_w'], 'L0_ffn_proj_b': _L0_ffn_in['proj_b'], 'L0_ffn_norm_w': _L0_ffn_in['norm_w']}
    _x0 = _d['L0_attn_a_x']
    _d['L0_attn_a_x'] = jax.random.normal(jax.random.fold_in(jax.random.key(seed), 1), (4, 512, 256), dtype=_x0.dtype)
    del _x0
    return _d

def reference(L0_attn_a_x, L0_attn_a_norm_w, L0_attn_a_in_proj_w, L0_attn_a_conv_w, L0_attn_a_conv_b, L0_attn_a_x_proj_w, L0_attn_a_dt_proj_w, L0_attn_a_dt_proj_b, L0_attn_a_A_log, L0_attn_a_D, L0_attn_a_out_proj_w, L0_attn_b_W_in, L0_attn_b_A_log, L0_attn_b_dt_bias, L0_attn_b_B_norm_bias, L0_attn_b_C_norm_bias, L0_attn_b_W_out, L0_ffn_router_w, L0_ffn_router_b, L0_ffn_expert_w, L0_ffn_expert_b, L0_ffn_proj_w, L0_ffn_proj_b, L0_ffn_norm_w):

    def _L0_attn_a_ref(x, norm_w, in_proj_w, conv_w, conv_b, x_proj_w, dt_proj_w, dt_proj_b, A_log, D, out_proj_w):
        import jax, jax.numpy as jnp
        import numpy as np
        EPS = 1e-05
        DT_RANK = 64
        N_STATE = 16

        def _rmsnorm(x, w):
            var = jnp.mean(x * x, axis=-1, keepdims=True)
            return x * jax.lax.rsqrt(var + EPS) * w

        def _softplus(x, beta=1.0, threshold=20.0):
            return jnp.where(beta * x > threshold, x, 1.0 / beta * jnp.logaddexp(0.0, beta * x))

        def _silu(x):
            return x * jax.nn.sigmoid(x)

        def _scan_combine(left, right):
            aL, xL = left
            aR, xR = right
            return (aR * aL, aR * xL + xR)
        B, L, H = x.shape
        h = _rmsnorm(x, norm_w)
        xz = h @ in_proj_w.T
        xc, z = jnp.split(xz, 2, axis=-1)
        xc = jax.lax.conv_general_dilated(xc, conv_w, window_strides=(1,), padding=[(3, 0)], dimension_numbers=('NLC', 'LIO', 'NLC')) + conv_b
        xc = _silu(xc)
        A = -jnp.exp(A_log)
        dBC = xc @ x_proj_w.T
        delta = dBC[..., :DT_RANK]
        Bm = dBC[..., DT_RANK:DT_RANK + N_STATE]
        Cm = dBC[..., DT_RANK + N_STATE:]
        delta = _softplus(delta @ dt_proj_w.T + dt_proj_b)
        deltaA = jnp.exp(delta[..., None] * A)
        BX = (delta * xc)[..., None] * Bm[:, :, None, :]
        _, hs = jax.lax.associative_scan(_scan_combine, (deltaA, BX), axis=1)
        y = jnp.einsum('blhn,bln->blh', hs, Cm) + D * xc
        out = y * _silu(z) @ out_proj_w.T
        return x + out

    def _L0_attn_b_ref(x, W_in, A_log, dt_bias, B_norm_bias, C_norm_bias, W_out):
        import jax, jax.numpy as jnp
        import numpy as np
        D_MODEL = 256
        D_STATE = 64
        EXPAND = 2
        N_HEADS = 64
        NGROUPS = 1
        CHUNK = 32
        D_INNER = EXPAND * D_MODEL
        HEAD_DIM = D_INNER // N_HEADS
        BC = NGROUPS * D_STATE
        D_PROJ = 2 * D_INNER + 2 * BC + 2 * N_HEADS + D_STATE // 2
        SCALE = D_STATE ** (-0.5)
        EPS = 1e-06
        BATCH, T = (2, 256)

        def _rms_norm(x):
            return x * jax.lax.rsqrt(jnp.mean(x * x, axis=-1, keepdims=True) + EPS)

        def _rope_pairs(x, cos, sin):
            h = x.shape[-1] // 2
            x1, x2 = (x[..., :h], x[..., h:])
            return jnp.concatenate([x1 * cos - x2 * sin, x1 * sin + x2 * cos], axis=-1)

        def _segsum(v):
            L = v.shape[-1]
            cs = jnp.cumsum(v, axis=-1)
            d = cs[..., :, None] - cs[..., None, :]
            mask = jnp.tril(jnp.ones((L, L), dtype=bool))
            return jnp.where(mask, d, -jnp.inf)

        def _ssd_chunked(x, A, Bm, Cm, dt):
            b, Tt, H, P = x.shape
            rep = H // NGROUPS
            Bh = jnp.repeat(Bm, rep, axis=2)
            Ch = jnp.repeat(Cm, rep, axis=2) * SCALE
            c = Tt // CHUNK
            xd = (x * dt[..., None]).reshape(b, c, CHUNK, H, P)
            Bh = Bh.reshape(b, c, CHUNK, H, D_STATE)
            Ch = Ch.reshape(b, c, CHUNK, H, D_STATE)
            dA = (dt * A).reshape(b, c, CHUNK, H)
            Acs = jnp.cumsum(dA, axis=2)
            Lm = jnp.exp(_segsum(jnp.moveaxis(dA, 3, 2)))
            Y_diag = jnp.einsum('bclhn,bcshn,bchls,bcshp->bclhp', Ch, Bh, Lm, xd)
            decay_states = jnp.exp(Acs[:, :, -1:, :] - Acs)
            states = jnp.einsum('bclhn,bclh,bclhp->bchpn', Bh, decay_states, xd)
            chunk_decay = jnp.exp(Acs[:, :, -1])

            def step(h, inp):
                dec, s = inp
                return (h * dec[:, :, None, None] + s, h)
            h0 = jnp.zeros((b, H, P, D_STATE), x.dtype)
            _, prev = jax.lax.scan(step, h0, (jnp.moveaxis(chunk_decay, 1, 0), jnp.moveaxis(states, 1, 0)))
            prev = jnp.moveaxis(prev, 0, 1)
            Y_off = jnp.einsum('bclhn,bchpn,bclh->bclhp', Ch, prev, jnp.exp(Acs))
            return (Y_diag + Y_off).reshape(b, Tt, H, P)
        b, Tt, _ = x.shape
        proj = x @ W_in
        d, bc, nh = (D_INNER, BC, N_HEADS)
        z = proj[..., :d]
        x_raw = proj[..., d:2 * d]
        B_mat = proj[..., 2 * d:2 * d + bc].reshape(b, Tt, NGROUPS, D_STATE)
        C_mat = proj[..., 2 * d + bc:2 * d + 2 * bc].reshape(b, Tt, NGROUPS, D_STATE)
        dt_raw = proj[..., 2 * d + 2 * bc:2 * d + 2 * bc + nh]
        lambda_raw = proj[..., 2 * d + 2 * bc + nh:2 * d + 2 * bc + 2 * nh]
        theta_raw = proj[..., 2 * d + 2 * bc + 2 * nh:]
        x_raw = jax.nn.silu(x_raw)
        B_mat = _rms_norm(B_mat) * B_norm_bias
        C_mat = _rms_norm(C_mat) * C_norm_bias
        A = -jnp.exp(A_log)
        dt = jnp.clip(jax.nn.softplus(dt_raw + dt_bias), 0.0001, 0.5)
        dt_mean = jnp.mean(dt, axis=-1, keepdims=True)
        cum = -jnp.cumsum(dt_mean * theta_raw, axis=1)
        cos = jnp.cos(cum)[:, :, None, :]
        sin = jnp.sin(cum)[:, :, None, :]
        B_mat = _rope_pairs(B_mat, cos, sin)
        C_mat = _rope_pairs(C_mat, cos, sin)
        xh = x_raw.reshape(b, Tt, N_HEADS, HEAD_DIM)
        lam = jax.nn.sigmoid(lambda_raw)
        alpha = jnp.exp(A * dt)
        x_gamma = xh * lam[..., None]
        x_shift = jnp.pad(xh[:, :-1], ((0, 0), (1, 0), (0, 0), (0, 0)))
        x_beta = x_shift * ((1.0 - lam) * alpha)[..., None]
        B_shift = jnp.pad(B_mat[:, :-1], ((0, 0), (1, 0), (0, 0), (0, 0)))
        y = _ssd_chunked(x_gamma, A, B_mat, C_mat, dt) + _ssd_chunked(x_beta, A, B_shift, C_mat, dt)
        y = y.reshape(b, Tt, D_INNER)
        y = _rms_norm(y) * jax.nn.silu(z)
        return y @ W_out

    def _L0_ffn_ref(x, router_w, router_b, expert_w, expert_b, proj_w, proj_b, norm_w):
        import jax, jax.numpy as jnp
        import numpy as np
        TOP_K = 2
        EPS = 1e-06
        B, S, D = x.shape
        E = router_b.shape[0]
        logits = jnp.einsum('bsd,de->bse', x, router_w) + router_b
        topk_vals, topk_idx = jax.lax.top_k(logits, TOP_K)
        topk_w = jax.nn.softmax(topk_vals, axis=-1)
        full_w = jnp.sum(jax.nn.one_hot(topk_idx, E, dtype=x.dtype) * topk_w[..., None], axis=-2)
        xf = x.reshape(-1, D)
        h = jnp.einsum('td,edf->etf', xf, expert_w) + expert_b[:, None, :]
        expert_out = jax.nn.silu(h)
        combined = jnp.einsum('etf,te->tf', expert_out, full_w.reshape(-1, E)).reshape(B, S, D)
        out = jnp.einsum('bsd,df->bsf', combined, proj_w) + proj_b
        y = x + out
        rms = jnp.sqrt(jnp.mean(y * y, axis=-1, keepdims=True) + EPS)
        return norm_w * (y / rms)
    x = L0_attn_a_x
    x = x + _L0_attn_a_ref(_layernorm(x, axis=-1), L0_attn_a_norm_w, L0_attn_a_in_proj_w, L0_attn_a_conv_w, L0_attn_a_conv_b, L0_attn_a_x_proj_w, L0_attn_a_dt_proj_w, L0_attn_a_dt_proj_b, L0_attn_a_A_log, L0_attn_a_D, L0_attn_a_out_proj_w)
    x = x + _L0_ffn_ref(_layernorm(x, axis=-1), L0_ffn_router_w, L0_ffn_router_b, L0_ffn_expert_w, L0_ffn_expert_b, L0_ffn_proj_w, L0_ffn_proj_b, L0_ffn_norm_w)
    x = x + _L0_attn_b_ref(_layernorm(x, axis=-1), L0_attn_b_W_in, L0_attn_b_A_log, L0_attn_b_dt_bias, L0_attn_b_B_norm_bias, L0_attn_b_C_norm_bias, L0_attn_b_W_out)
    x = x + _L0_ffn_ref(_layernorm(x, axis=-1), L0_ffn_router_w, L0_ffn_router_b, L0_ffn_expert_w, L0_ffn_expert_b, L0_ffn_proj_w, L0_ffn_proj_b, L0_ffn_norm_w)
    return x

_drawn_inputs = setup_inputs


def setup_inputs(seed=0):
    import zlib

    import numpy as np

    out = dict(_drawn_inputs(seed))
    spreads = {'L0_attn_a_norm_w': (1.0, 0.2),
     'L0_attn_a_conv_b': (0.0, 0.1),
     'L0_attn_a_dt_proj_b': (0.0, 0.1),
     'L0_attn_a_D': (1.0, 0.2),
     'L0_attn_b_A_log': (0.0, 0.1),
     'L0_attn_b_dt_bias': (0.0, 0.1),
     'L0_attn_b_B_norm_bias': (1.0, 0.2),
     'L0_attn_b_C_norm_bias': (1.0, 0.2),
     'L0_ffn_router_b': (0.0, 0.1),
     'L0_ffn_expert_b': (0.0, 0.1),
     'L0_ffn_proj_b': (0.0, 0.1),
     'L0_ffn_norm_w': (1.0, 0.2)}
    factors = {}
    for name, (base, spread) in spreads.items():
        noise = np.random.default_rng([zlib.crc32(name.encode()), seed]).standard_normal(out[name].shape)
        drawn = base * np.exp(spread * noise) if base else spread * noise
        out[name] = jnp.asarray(drawn.astype(out[name].dtype))
    for name, factor in factors.items():
        out[name] = (out[name] * factor).astype(out[name].dtype)
    return out
```

```python
from contextlib import ExitStack

import concourse.bass as bass
import numpy as np
from concourse import mybir

F32 = mybir.dt.float32
BF16 = mybir.dt.bfloat16
ALU = mybir.AluOpType
ACT = mybir.ActivationFunctionType
AX = mybir.AxisListType.X

P = 128
NB = 4
T = 512
D = 256
KD = D // P
TB = T // P
NT = NB * TB
LN_EPS = 1e-5


class Chain:

    def __init__(self, eng, sem, per):
        self.eng, self.sem, self.per, self.base, self.k = eng, sem, per, 0, 0

    def begin(self, turn):
        self.base, self.k = turn * self.per, 0

    def link(self, ins):
        self.k += 1
        ins.then_inc(self.sem, 1)
        self.eng.wait_ge(self.sem, self.base + self.k)

    def end(self):
        assert self.k == self.per, (self.k, self.per)


def bc_last(ap, n):
    return ap.unsqueeze(len(ap.shape)).to_broadcast(list(ap.shape) + [n])


def bc_mid(ap, n):
    return ap.unsqueeze(1).to_broadcast([ap.shape[0], n] + list(ap.shape[1:]))


def phase_mamba(nc, x_res, ident, w, x_dram):
    NS, R = 16, 64
    CT = 4
    HT, XC, Z, CV, DBC, DT, NF = 0, 2, 4, 6, 8, 9, 11
    with ExitStack() as ctx:
        def sb(name, shape, dt=F32):
            return ctx.enter_context(nc.sbuf_tensor("m_" + name, shape, dt))

        def ps(name, shape):
            return ctx.enter_context(nc.psum_tensor("m_" + name, shape, F32))

        def sem(name):
            return ctx.enter_context(nc.semaphore("m_" + name))

        w_in = sb("w_in", [P, KD, 2 * D])
        w_conv = sb("w_conv", [P, CT, KD, D])
        w_xp = sb("w_xp", [P, KD, R + 2 * NS])
        w_dt = sb("w_dt", [R, D])
        w_out = sb("w_out", [P, KD, D])
        norm_w = sb("norm_w", [P, KD])
        conv_b = sb("conv_b", [P, KD])
        dt_b = sb("dt_b", [P, KD])
        d_skip = sb("d_skip", [P, KD])
        a_log = sb("a_log", [P, KD, NS])
        a_exp = sb("a_exp", [P, KD, NS])
        a_neg = sb("a_neg", [P, KD, NS])
        sel = sb("sel", [3 * 2 * NS, 2 * NS, P], BF16)

        stats = sb("stats", [P, TB, 6])
        scrap = sb("scrap", [P, 1])
        mv = sb("mv", [P, TB, 2])
        rstd = sb("rstd", [P, TB])
        var = sb("var", [P, TB])
        ms = sb("ms", [P, TB])
        half = sb("half", [P, TB])
        eps = sb("eps", [P, TB])
        r2 = sb("r2", [P, TB])
        xn = sb("xn", [P, TB, D])
        h = sb("h", [P, TB, D])
        hT = sb("hT", [P, KD, T])
        xc = sb("xc", [P, KD, T + CT - 1])
        dlow = sb("dlow", [R, T])
        rest = sb("rest", [2 * 2 * NS, T])
        sp_in = sb("sp_in", [P, KD, T])
        sp_e = sb("sp_e", [P, KD, T])
        sp_l = sb("sp_l", [P, KD, T])
        sz = sb("sz", [P, NB, KD, T])
        xs = sb("xs", [P, NB, KD, T])
        delta = sb("delta", [P, NB, KD, T])
        u = sb("u", [P, NB, KD, T])
        bc3 = sb("bc3", [3 * 2 * NS, NB, T], BF16)
        dA = sb("dA", [P, 3, KD, T])
        bx = sb("bx", [P, 2, KD, T])
        hs = sb("hs", [P, 2, KD, T])
        hc = sb("hc", [P, 3, KD, T])
        y2 = sb("y2", [P, KD, T])
        g = sb("g", [P, KD, T])

        front = [ps(f"front{j}", [P, T]) for j in range(2)]
        yps = ps("yps", [P, KD, T])
        Bps = ps("Bps", [P, 2, T])
        Cps = ps("Cps", [P, 2, T])

        s_x0 = sem("x0_loaded")
        s_x = sem("x_loaded")
        s_w = sem("weights_loaded")
        s_pool = sem("pool_step")
        s_id = sem("ident_ready")
        s_pad = sem("conv_pad_ready")
        s_sel = sem("selectors_ready")
        s_ae = sem("a_exp_ready")
        s_a = sem("a_ready")
        s_vf = sem("vector_front_step")
        s_pf = sem("pool_front_step")
        s_half = sem("half_ready")
        s_var = sem("var_ready")
        s_r2 = sem("r2_ready")
        s_xn = sem("xn_ready")
        s_h = sem("h_ready")
        s_res = sem("residual_added")
        s_full = sem("front_full")
        s_hT = sem("hT_ready")
        s_xc = sem("xc_ready")
        s_sz = sem("sz_ready")
        s_xs = sem("xs_ready")
        s_dlow = sem("dlow_ready")
        s_bc3 = sem("bc3_ready")
        s_spin = sem("sp_in_ready")
        s_spe = sem("sp_e_ready")
        s_spl = sem("sp_l_ready")
        s_delta = sem("delta_ready")
        s_u = sem("u_ready")
        s_B = sem("B_full")
        s_C = sem("C_full")
        s_bx = sem("bx_ready")
        s_dA = sem("dA_ready")
        s_scan = sem("scan_done")
        s_hc = sem("hc_ready")
        s_hcu = sem("hc_used")
        s_y2 = sem("y2_ready")
        s_g = sem("g_ready")
        s_o = sem("out_full")
        s_xo = sem("x_updated")

        NW = 10
        block = ctx.enter_context(nc.Block())

        def full(b, use):
            return b * NF + use + 1

        def is_first(b):
            return isinstance(b, int) and b == 0

        @block.sync
        def _(sp):
            xv = x_dram.rearrange("b (t p) d -> b p t d", p=P)
            sp.dma_start(x_res[:, 0:TB, :], xv[0]).then_inc(s_x0, 16)

            def column(dst, src):
                sp.dma_start(dst[:], src.rearrange("(k p) -> p k", p=P),
                             allow_slow_non_contiguous=True).then_inc(s_w, 16)

            def rows(dst, src):
                sp.dma_start(dst[:], src.rearrange("(k p) n -> p k n", p=P)).then_inc(s_w, 16)

            column(norm_w, w["norm_w"])
            rows(w_in, w["in_proj_w"])
            sp.dma_start(w_conv[:], w["conv_w"].rearrange("j (k p) n -> p j k n", p=P)).then_inc(s_w, 16)
            column(conv_b, w["conv_b"])
            rows(w_xp, w["x_proj_w"])
            sp.dma_start(w_dt[:], w["dt_proj_w"]).then_inc(s_w, 16)
            column(dt_b, w["dt_proj_b"])
            rows(a_log, w["A_log"])
            column(d_skip, w["D"])
            rows(w_out, w["out_proj_w"])
            for b in range(1, NB):
                sp.dma_start(x_res[:, b * TB:(b + 1) * TB, :], xv[b]).then_inc(s_x, 16)

        @block.gpsimd
        def _(pool):
            chain = Chain(pool, s_pool, 4)
            nc.gpsimd.memset(half[:], -0.5).then_inc(s_half, 1)
            nc.gpsimd.memset(eps[:], LN_EPS).then_inc(s_half, 1)
            pool.wait_ge(s_half, 2)
            chain.link(nc.gpsimd.memset(ident[:], 0.0))
            nc.gpsimd.affine_select(out=ident[:], in_=ident[:], compare_op=ALU.not_equal, fill=1.0, base=0,
                                    pattern=[[-1, P]], channel_multiplier=1).then_inc(s_id, 1)
            nc.gpsimd.memset(xc[:, :, 0:CT - 1], 0.0).then_inc(s_pad, 1)
            chain.link(nc.gpsimd.memset(sel[:], 0.0))
            for part in range(3):
                ins = nc.gpsimd.affine_select(out=sel[:], in_=sel[:], compare_op=ALU.not_equal, fill=1.0,
                                              base=-2 * NS * part, pattern=[[-1, 2 * NS], [0, P]],
                                              channel_multiplier=1)
                if part < 2:
                    chain.link(ins)
            ins.then_inc(s_sel, 1)
            chain.end()

            pool_chain = Chain(pool, s_pf, 6)

            def scales(b):
                pool_chain.begin(b)
                pool.wait_ge(s_var, b + 1)
                if not is_first(b):
                    pool.wait_ge(s_h, b)
                pool_chain.link(nc.gpsimd.tensor_tensor(ms[:], var[:], eps[:], ALU.add))
                pool_chain.link(nc.gpsimd.tensor_tensor(rstd[:], ms[:], half[:], ALU.pow))
                pool_chain.link(nc.gpsimd.tensor_tensor(ms[:], var[:], rstd[:], ALU.mult))
                pool_chain.link(nc.gpsimd.tensor_tensor(ms[:], ms[:], rstd[:], ALU.mult))
                pool_chain.link(nc.gpsimd.tensor_tensor(ms[:], ms[:], eps[:], ALU.add))
                pool_chain.link(nc.gpsimd.tensor_tensor(r2[:], ms[:], half[:], ALU.pow))
                nc.gpsimd.tensor_tensor(r2[:], r2[:], rstd[:], ALU.mult).then_inc(s_r2, 1)
                pool_chain.end()

            def residual(b, rows):
                pool.wait_ge(s_xn, b + 1)
                pool.wait_ge(s_h, b + 1)
                nc.gpsimd.tensor_tensor(rows, rows, xn[:], ALU.add).then_inc(s_res, 1)

            scales(0)
            residual(0, x_res[:, 0:TB, :])
            with pool.Fori(1, NB) as b:
                scales(b)
                residual(b, x_res[:, bass.ds(TB * b, TB), :])

        @block.tensor
        def _(pe):
            def transposes(b):
                pe.wait_ge(s_h, b + 1)
                for k in range(KD):
                    if not is_first(b):
                        pe.wait_ge(s_delta, KD * b)
                    for t in range(TB):
                        mm = nc.tensor.transpose(front[(HT + k) % 2][:, t * P:(t + 1) * P],
                                                 h[:, t, k * P:(k + 1) * P], ident[:])
                    mm.then_inc(s_full, 1)

            def in_proj(b, use, read):
                pe.wait_ge(s_hT, KD * (b + 1))
                for m in range(KD):
                    pe.wait_ge(read, KD * b + m + 1)
                    col = (use - XC + m) * P
                    for k in range(KD):
                        mm = nc.tensor.matmul(front[(use + m) % 2][:], w_in[:, k, col:col + P], hT[:, k, :],
                                              start=(k == 0), stop=(k == KD - 1))
                    mm.then_inc(s_full, 1)

            def conv(b, m, half):
                if half == 0:
                    pe.wait_ge(s_xc, KD * (b + 1))
                    pe.wait_ge(s_sz, KD * b + m + 1)
                for j in range(2 * half, 2 * half + 2):
                    for k in range(KD):
                        mm = nc.tensor.matmul(front[(CV + m) % 2][:], w_conv[:, j, k, m * P:(m + 1) * P],
                                              xc[:, k, j:j + T], start=(j == 0 and k == 0),
                                              stop=(j == CT - 1 and k == KD - 1))
                if half == 1:
                    mm.then_inc(s_full, 1)

            def x_proj(b):
                pe.wait_ge(s_xs, KD * (b + 1))
                for k in range(KD):
                    mm = nc.tensor.matmul(front[DBC % 2][0:R + 2 * NS, :], w_xp[:, k, :], xs[:, b, k, :],
                                          start=(k == 0), stop=(k == KD - 1))
                mm.then_inc(s_full, 1)

            def dt_proj(b):
                pe.wait_ge(s_dlow, b + 1)
                for m in range(KD):
                    if (DT + m) % 2 == DBC % 2:
                        pe.wait_ge(s_bc3, b + 1)
                    nc.tensor.matmul(front[(DT + m) % 2][:], w_dt[:, m * P:(m + 1) * P], dlow[:], start=True,
                                     stop=True).then_inc(s_full, 1)

            pieces = {2: transposes,
                      3: lambda b: in_proj(b, XC, s_hT), 4: lambda b: in_proj(b, Z, s_xc),
                      5: lambda b: conv(b, 0, 0), 6: lambda b: conv(b, 0, 1),
                      7: lambda b: conv(b, 1, 0), 8: lambda b: conv(b, 1, 1),
                      10: x_proj, 12: dt_proj}

            def broadcast(b, n):
                step = NS * b + n
                if not (is_first(b) and n < 2):
                    pe.wait_ge(s_bx, step - 1)
                nc.tensor.matmul(Bps[:, n % 2, :], sel[:, n, :], bc3[:, b, :], start=True,
                                 stop=True).then_inc(s_B, 1)
                if not (is_first(b) and n < 2):
                    pe.wait_ge(s_hc, step - 1)
                nc.tensor.matmul(Cps[:, n % 2, :], sel[:, NS + n, :], bc3[:, b, :], start=True,
                                 stop=True).then_inc(s_C, 1)

            def accumulate(b, n):
                step = NS * b + n
                pe.wait_ge(s_hc, step + 1)
                if n == 0 and not is_first(b):
                    pe.wait_ge(s_xo, KD * b)
                for m in range(KD):
                    mm = nc.tensor.matmul(yps[:, m, :], ident[:], hc[:, (step % 3), m, :], start=(n == 0),
                                          stop=(n == NS - 1))
                mm.then_inc(s_hcu, 1)

            def sequence(b, ahead):
                pe.wait_ge(s_bc3, b + 1)
                broadcast(b, 0)
                for n in range(NS):
                    if n + 1 < NS:
                        broadcast(b, n + 1)
                    if n >= 1:
                        accumulate(b, n - 1)
                    if ahead and n in pieces:
                        pieces[n](b + 1)
                accumulate(b, NS - 1)
                pe.wait_ge(s_g, b + 1)
                for t in range(TB):
                    for k in range(KD):
                        mm = nc.tensor.matmul(yps[:, t // 2, (t % 2) * D:(t % 2 + 1) * D],
                                              g[:, k, t * P:(t + 1) * P], w_out[:, k, :],
                                              start=(k == 0), stop=(k == KD - 1))
                    if t % 2:
                        mm.then_inc(s_o, 1)

            pe.wait_ge(s_id, 1)
            pe.wait_ge(s_pad, 1)
            pe.wait_ge(s_w, 16 * NW)
            for piece in pieces.values():
                piece(0)
            pe.wait_ge(s_sel, 1)
            sequence(0, True)
            with pe.Fori(1, NB - 1) as b:
                sequence(b, True)
            sequence(NB - 1, False)

        @block.scalar
        def _(act):
            def take_hT(b):
                for k in range(KD):
                    act.wait_ge(s_full, full(b, HT + k))
                    nc.scalar.activation(hT[:, k, :], front[(HT + k) % 2][:], ACT.Copy,
                                         scale=norm_w[:, k:k + 1]).then_inc(s_hT, 1)

            def take_xc(b):
                for k in range(KD):
                    act.wait_ge(s_full, full(b, XC + k))
                    nc.scalar.activation(xc[:, k, CT - 1:], front[(XC + k) % 2][:], ACT.Copy).then_inc(s_xc, 1)

            def take_z(b):
                for k in range(KD):
                    act.wait_ge(s_full, full(b, Z + k))
                    nc.scalar.activation(sz[:, b, k, :], front[(Z + k) % 2][:], ACT.Silu).then_inc(s_sz, 1)

            def take_conv(b):
                for k in range(KD):
                    act.wait_ge(s_full, full(b, CV + k))
                    nc.scalar.activation(xs[:, b, k, :], front[(CV + k) % 2][:], ACT.Silu,
                                         bias=conv_b[:, k:k + 1]).then_inc(s_xs, 1)

            def take_dlow(b):
                act.wait_ge(s_full, full(b, DBC))
                nc.scalar.activation(dlow[:], front[DBC % 2][0:R, :], ACT.Copy).then_inc(s_dlow, 1)

            def softplus(b):
                act.wait_ge(s_spin, KD * (b + 1))
                nc.scalar.activation(sp_e[:], sp_in[:], ACT.Exp).then_inc(s_spe, 1)
                act.wait_ge(s_spe, b + 1)
                nc.scalar.activation(sp_l[:], sp_e[:], ACT.Ln, bias=1.0).then_inc(s_spl, 1)

            pieces = {3: take_hT, 4: take_xc, 5: take_z, 9: take_conv, 11: take_dlow, 13: softplus}

            def sequence(b, ahead):
                for n in range(NS):
                    step = NS * b + n
                    if n == 0:
                        act.wait_ge(s_delta, KD * (b + 1))
                    if not (is_first(b) and n < 3):
                        act.wait_ge(s_scan, step - 2)
                    for m in range(KD):
                        ins = nc.scalar.activation(dA[:, step % 3, m, :], delta[:, b, m, :], ACT.Exp,
                                                   scale=a_neg[:, m, n:n + 1])
                    ins.then_inc(s_dA, 1)
                    if ahead and n in pieces:
                        pieces[n](b + 1)

            act.wait_ge(s_w, 16 * NW)
            nc.scalar.activation(a_exp[:], a_log[:], ACT.Exp).then_inc(s_ae, 1)
            for piece in pieces.values():
                piece(0)
            act.wait_ge(s_a, 1)
            sequence(0, True)
            with act.Fori(1, NB - 1) as b:
                sequence(b, True)
            sequence(NB - 1, False)

        @block.vector
        def _(dve):
            chain = Chain(dve, s_vf, 5)

            def statistics(b):
                chain.begin(b)
                dve.wait_ge(s_x0 if is_first(b) else s_x, 16 if is_first(b) else 16 * (NB - 1))
                if not is_first(b):
                    dve.wait_ge(s_h, b)
                for t in range(TB):
                    ins = nc.vector.bn_stats(stats[:, t, :], x_res[:, TB * b + t, :])
                    chain.link(ins) if t == TB - 1 else None
                nc.vector.memset(scrap[:], 0.0)
                for t in range(TB):
                    ins = nc.vector.bn_aggr(mv[:, t, :], stats[:, t, :])
                chain.link(ins)
                nc.vector.tensor_copy(var[:], mv[:, :, 1]).then_inc(s_var, 1)

            def normalise(b):
                dve.wait_ge(s_r2, b + 1)
                if not is_first(b):
                    dve.wait_ge(s_res, b)
                for t in range(TB):
                    ins = nc.vector.tensor_scalar(xn[:, t, :], x_res[:, TB * b + t, :], mv[:, t, 0:1],
                                                  rstd[:, t:t + 1], ALU.subtract, ALU.mult)
                ins.then_inc(s_xn, 1)
                if not is_first(b):
                    dve.wait_ge(s_full, full(b - 1, HT + KD - 1))
                for t in range(TB):
                    ins = nc.vector.tensor_scalar(h[:, t, :], x_res[:, TB * b + t, :], mv[:, t, 0:1],
                                                  r2[:, t:t + 1], ALU.subtract, ALU.mult)
                ins.then_inc(s_h, 1)

            def split_bc(b):
                dve.wait_ge(s_full, full(b, DBC))
                n = 2 * NS
                src = front[DBC % 2][R:R + n, :]
                chain.link(nc.vector.tensor_copy(bc3[0:n, b, :], src))
                chain.link(nc.vector.tensor_tensor(rest[n:2 * n, :], src, bc3[0:n, b, :], ALU.subtract))
                chain.link(nc.vector.tensor_copy(bc3[n:2 * n, b, :], rest[n:2 * n, :]))
                nc.vector.tensor_tensor(bc3[2 * n:3 * n, b, :], rest[n:2 * n, :], bc3[n:2 * n, b, :],
                                        ALU.subtract).then_inc(s_bc3, 1)

            def softplus_in(b):
                for m in range(KD):
                    dve.wait_ge(s_full, full(b, DT + m))
                    nc.vector.tensor_scalar(sp_in[:, m, :], front[(DT + m) % 2][:], dt_b[:, m:m + 1], 30.0,
                                            ALU.add, ALU.min).then_inc(s_spin, 1)

            def step_size(b):
                dve.wait_ge(s_spl, b + 1)
                for m in range(KD):
                    nc.vector.scalar_tensor_tensor(delta[:, b, m, :], front[(DT + m) % 2][:], dt_b[:, m:m + 1],
                                                   sp_l[:, m, :], ALU.add, ALU.max).then_inc(s_delta, 1)
                dve.wait_ge(s_delta, KD * (b + 1))
                dve.wait_ge(s_xs, KD * (b + 1))
                nc.vector.tensor_tensor(u[:, b], delta[:, b], xs[:, b], ALU.mult).then_inc(s_u, 1)
                chain.end()

            pieces = {0: statistics, 1: normalise, 11: split_bc, 13: softplus_in, 14: step_size}

            def inject(b, n):
                step = NS * b + n
                dve.wait_ge(s_B, step + 1)
                nc.vector.tensor_tensor(bx[:, n % 2], u[:, b], bc_mid(Bps[:, n % 2, :], KD),
                                        ALU.mult).then_inc(s_bx, 1)

            def sequence(b, ahead):
                dve.wait_ge(s_u, b + 1)
                inject(b, 0)
                for n in range(NS):
                    step = NS * b + n
                    dve.wait_ge(s_dA, step + 1)
                    dve.wait_ge(s_bx, step + 1)
                    for m in range(KD):
                        ins = nc.vector.tensor_tensor_scan(hs[:, n % 2, m, :], dA[:, step % 3, m, :],
                                                           bx[:, n % 2, m, :], 0.0, ALU.mult, ALU.add)
                    ins.then_inc(s_scan, 1)
                    if n + 1 < NS:
                        inject(b, n + 1)
                    dve.wait_ge(s_C, step + 1)
                    dve.wait_ge(s_scan, step + 1)
                    if not (is_first(b) and n < 3):
                        dve.wait_ge(s_hcu, step - 2)
                    nc.vector.tensor_tensor(hc[:, step % 3], hs[:, n % 2], bc_mid(Cps[:, n % 2, :], KD),
                                            ALU.mult).then_inc(s_hc, 1)
                    if ahead and n in pieces:
                        pieces[n](b + 1)
                dve.wait_ge(s_hcu, NS * (b + 1))
                for m in range(KD):
                    ins = nc.vector.scalar_tensor_tensor(y2[:, m, :], xs[:, b, m, :], d_skip[:, m:m + 1],
                                                         yps[:, m, :], ALU.mult, ALU.add)
                ins.then_inc(s_y2, 1)
                dve.wait_ge(s_y2, b + 1)
                dve.wait_ge(s_sz, KD * (b + 1))
                nc.vector.tensor_tensor(g[:], y2[:], sz[:, b], ALU.mult).then_inc(s_g, 1)
                dve.wait_ge(s_res, b + 1)
                for j in range(KD):
                    dve.wait_ge(s_o, KD * b + j + 1)
                    at = TB * b + 2 * j
                    rows = x_res[:, bass.ds(at, 2), :]
                    nc.vector.tensor_tensor(rows, rows, yps[:, j, :].rearrange("p (t d) -> p t d", t=2),
                                            ALU.add).then_inc(s_xo, 1)

            dve.wait_ge(s_w, 16 * NW)
            dve.wait_ge(s_ae, 1)
            nc.vector.tensor_scalar(a_neg[:], a_exp[:], -1.0, None, ALU.mult).then_inc(s_a, 1)
            for piece in pieces.values():
                piece(0)
            sequence(0, True)
            with dve.Fori(1, NB - 1) as b:
                sequence(b, True)
            sequence(NB - 1, False)


def phase_ffn(nc, x_res, ident, w, tag):
    E = w["router_w"].shape[1]
    RMS_EPS = 1e-6
    EB = 2
    NBANK = E // EB
    NBIAS = E * D + D + E
    PB, RB = E * D, E * D + D
    with ExitStack() as ctx:
        def sb(name, shape, dt=F32):
            return ctx.enter_context(nc.sbuf_tensor(tag + name, shape, dt))

        def ps(name, shape):
            return ctx.enter_context(nc.psum_tensor(tag + name, shape, F32))

        def sem(name):
            return ctx.enter_context(nc.semaphore(tag + name))

        w_e = sb("w_e", [P, KD, E, D])
        w_r = sb("w_r", [P, KD, E])
        w_p = sb("w_p", [P, KD, D])
        norm_w = sb("norm_w", [P, D])
        bias = sb("bias", [1, NBIAS])
        bias_rest = sb("bias_rest", [64, NBIAS])
        bias3 = sb("bias3", [96, NBIAS], BF16)
        ones = sb("ones", [96, P], BF16)
        before = sb("before", [P, E, E])
        half = sb("half", [P, TB])
        eps = sb("eps", [P, TB])
        rms_eps = sb("rms_eps", [P, 1])
        per_d = sb("per_d", [P, 1])

        stats = sb("stats", [P, TB, 6])
        scrap = sb("scrap", [P, 1])
        mv = sb("mv", [P, TB, 2])
        ve = sb("ve", [P, TB])
        rstd = sb("rstd", [P, TB])
        z = sb("z", [P, TB, D])
        zT = sb("zT", [P, 2, KD, P])
        lg = sb("lg", [P, 2, E])
        above = sb("above", [P, E, E])
        equal = sb("equal", [P, E, E])
        rank = sb("rank", [P, 2, E])
        picked = sb("picked", [P, E])
        mid = sb("mid", [P, 2])
        th = sb("th", [P, 2, E])
        wt = sb("wt", [P, E])
        gate = sb("gate", [P, 2, E])
        s = sb("s", [P, 2, E, D])
        acc = sb("acc", [P, 2, D])
        cT = sb("cT", [P, 2, KD, P])
        y = sb("y", [P, 2, D])
        sq = sb("sq", [P, D])
        ss = sb("ss", [P, 2])
        ms = sb("ms", [P, 2])
        rr = sb("rr", [P, 2])
        o = sb("o", [P, 2, D])

        hps = ps("hps", [P, NBANK, EB * D])
        zps = ps("zps", [P, KD, P])
        rps = ps("rps", [P, 2, E])
        cps = ps("cps", [P, KD, P])
        ops = ps("ops", [P, D])

        s_w = sem("weights_loaded")
        s_b = sem("bias_step")
        s_const = sem("constants_ready")
        s_var = sem("var_ready")
        s_rstd = sem("rstd_ready")
        s_pool = sem("pool_step")
        s_z = sem("z_ready")
        s_zt = sem("z_turned")
        s_zT = sem("zT_ready")
        s_r = sem("logits_full")
        s_v = sem("vector_step")
        s_mid = sem("mid_ready")
        s_th = sem("tanh_ready")
        s_gate = sem("gate_ready")
        s_h = sem("experts_full")
        s_s = sem("silu_ready")
        s_acc = sem("combined_ready")
        s_ct = sem("combined_turned")
        s_cT = sem("cT_ready")
        s_o = sem("out_full")
        s_y = sem("y_ready")
        s_ss = sem("ss_ready")
        s_rr = sem("rr_ready")
        s_on = sem("o_ready")
        s_x = sem("x_updated")

        NW = 8
        block = ctx.enter_context(nc.Block())

        def is_first(t):
            return isinstance(t, int) and t == 0

        @block.sync
        def _(sp):
            sp.dma_start(bias[:, 0:PB], w["expert_b"].rearrange("e d -> (e d)").unsqueeze(0)).then_inc(s_w, 16)
            sp.dma_start(bias[:, PB:RB], w["proj_b"].unsqueeze(0)).then_inc(s_w, 16)
            sp.dma_start(bias[:, RB:], w["router_b"].unsqueeze(0)).then_inc(s_w, 16)
            sp.dma_start(w_r[:], w["router_w"].rearrange("(k p) e -> p k e", p=P)).then_inc(s_w, 16)
            for k in range(KD):
                sp.dma_start(w_e[:, k], w["expert_w"].rearrange("e (k p) n -> k p e n", p=P)[k]).then_inc(s_w, 16)
            sp.dma_start(w_p[:], w["proj_w"].rearrange("(k p) n -> p k n", p=P)).then_inc(s_w, 16)
            sp.dma_start(norm_w[:], w["norm_w"].partition_broadcast(P)).then_inc(s_w, 16)

        @block.gpsimd
        def _(pool):
            nc.gpsimd.memset(half[:], -0.5).then_inc(s_const, 1)
            nc.gpsimd.memset(eps[:], LN_EPS).then_inc(s_const, 1)
            nc.gpsimd.memset(rms_eps[:], RMS_EPS).then_inc(s_const, 1)
            nc.gpsimd.memset(per_d[:], 1.0 / D).then_inc(s_const, 1)
            nc.gpsimd.memset(ones[:], 1.0).then_inc(s_const, 1)
            nc.gpsimd.memset(bias3[:], 0.0).then_inc(s_const, 1)
            nc.gpsimd.memset(before[:], 1.0).then_inc(s_const, 1)
            pool.wait_ge(s_const, 7)
            nc.gpsimd.affine_select(out=before[:], in_=before[:], compare_op=ALU.is_gt, fill=0.0, base=0,
                                    pattern=[[1, E], [-1, E]], channel_multiplier=0).then_inc(s_const, 1)
            chain = Chain(pool, s_pool, 1 + 2 * TB)

            def scales(g):
                pool.wait_ge(s_var, g + 1)
                chain.link(nc.gpsimd.tensor_tensor(ve[:], mv[:, :, 1], eps[:], ALU.add))
                nc.gpsimd.tensor_tensor(rstd[:], ve[:], half[:], ALU.pow).then_inc(s_rstd, 1)

            def rms(tile, q):
                pool.wait_ge(s_ss, tile + 1)
                chain.link(nc.gpsimd.tensor_tensor(ms[:, q:q + 1], ss[:, q:q + 1], per_d[:], ALU.mult))
                chain.link(nc.gpsimd.tensor_tensor(ms[:, q:q + 1], ms[:, q:q + 1], rms_eps[:], ALU.add))
                nc.gpsimd.tensor_tensor(rr[:, q:q + 1], ms[:, q:q + 1], half[:, 0:1], ALU.pow).then_inc(s_rr, 1)

            def group(g, ahead):
                chain.begin(g)
                chain.base = 1 if is_first(g) else chain.base - 1
                for t in range(TB):
                    rms(TB * g + t - 1, (t - 1) % 2) if not (is_first(g) and t == 0) else None
                    if t == TB - 2 and ahead:
                        scales(g + 1)
                if not ahead:
                    rms(TB * g + t, t % 2)

            chain.begin(0)
            scales(0)
            group(0, True)
            with pool.Fori(1, NB - 1) as g:
                group(g, True)
            group(NB - 1, False)

        @block.tensor
        def _(pe):
            def turn_z(tile, q):
                pe.wait_ge(s_z, tile + 1)
                if not is_first(tile):
                    pe.wait_ge(s_zT, tile)
                for k in range(KD):
                    mm = nc.tensor.transpose(zps[:, k, :], z[:, q, k * P:(k + 1) * P], ident[:])
                mm.then_inc(s_zt, 1)

            def router(tile, q):
                pe.wait_ge(s_zT, tile + 1)
                for k in range(KD):
                    nc.tensor.matmul(rps[:, q, :], zT[:, q, k, :], w_r[:, k, :], start=(k == 0), stop=False)
                nc.tensor.matmul(rps[:, q, :], ones[:], bias3[:, RB:], start=False, stop=True).then_inc(s_r, 1)

            def experts(tile, q, j):
                if not is_first(tile):
                    pe.wait_ge(s_s, NBANK * tile + j - NBANK + 1)
                cols = slice(EB * D * j, EB * D * (j + 1))
                for k in range(KD):
                    nc.tensor.matmul(hps[:, j, :], zT[:, q, k, :],
                                     w_e[:, k, EB * j:EB * (j + 1), :].rearrange("p e n -> p (e n)"),
                                     start=(k == 0), stop=False)
                nc.tensor.matmul(hps[:, j, :], ones[:], bias3[:, cols], start=False, stop=True).then_inc(s_h, 1)

            def turn_combined(tile, q):
                pe.wait_ge(s_acc, tile + 1)
                for k in range(KD):
                    mm = nc.tensor.transpose(cps[:, k, :], acc[:, q, k * P:(k + 1) * P], ident[:])
                mm.then_inc(s_ct, 1)

            def project(tile, q):
                pe.wait_ge(s_cT, tile + 1)
                if not is_first(tile):
                    pe.wait_ge(s_y, tile)
                for k in range(KD):
                    nc.tensor.matmul(ops[:], cT[:, q, k, :], w_p[:, k, :], start=(k == 0), stop=False)
                nc.tensor.matmul(ops[:], ones[:], bias3[:, PB:RB], start=False, stop=True).then_inc(s_o, 1)

            def group(g, last):
                for t in range(TB):
                    tile, q = TB * g + t, t % 2
                    started = not (is_first(g) and t == 0)
                    router(tile, q)
                    for j in range(NBANK):
                        experts(tile, q, j)
                        if j == 1 and not (last and t == TB - 1):
                            turn_z(tile + 1, (t + 1) % TB)
                        if j == 2 and started:
                            turn_combined(tile - 1, (t - 1) % 2)
                        if j == 3 and started:
                            project(tile - 1, (t - 1) % 2)
                if last:
                    turn_combined(tile, q)
                    project(tile, q)

            pe.wait_ge(s_const, 8)
            pe.wait_ge(s_b, 4)
            pe.wait_ge(s_w, 16 * NW)
            turn_z(0, 0)
            group(0, False)
            with pe.Fori(1, NB - 1) as g:
                group(g, False)
            group(NB - 1, True)

        @block.scalar
        def _(act):
            def take_zT(tile, q):
                act.wait_ge(s_zt, tile + 1)
                nc.scalar.activation(zT[:, q], zps[:], ACT.Copy).then_inc(s_zT, 1)

            def tanh(tile, q):
                act.wait_ge(s_mid, tile + 1)
                nc.scalar.activation(th[:, q, :], lg[:, q, :], ACT.Tanh, bias=mid[:, q:q + 1],
                                     scale=-2.0).then_inc(s_th, 1)

            def silu(tile, q, j):
                act.wait_ge(s_h, NBANK * tile + j + 1)
                if not (isinstance(tile, int) and tile < 2):
                    act.wait_ge(s_acc, tile - 1)
                nc.scalar.activation(s[:, q, EB * j:EB * (j + 1), :].rearrange("p e n -> p (e n)"),
                                     hps[:, j, :], ACT.Silu).then_inc(s_s, 1)

            def take_cT(tile, q):
                act.wait_ge(s_ct, tile + 1)
                nc.scalar.activation(cT[:, q], cps[:], ACT.Copy).then_inc(s_cT, 1)

            def square(tile, q):
                act.wait_ge(s_y, tile + 1)
                nc.scalar.activation(sq[:], y[:, q, :], ACT.Square, accum_out=ss[:, q:q + 1]).then_inc(s_ss, 1)

            def group(g, last):
                for t in range(TB):
                    tile, q = TB * g + t, t % 2
                    started = not (is_first(g) and t == 0)
                    for j in range(NBANK):
                        silu(tile, q, j)
                        if j == 0:
                            tanh(tile, q)
                        if j == 1 and not (last and t == TB - 1):
                            take_zT(tile + 1, (t + 1) % 2)
                        if j == 2 and started:
                            take_cT(tile - 1, (t - 1) % 2)
                    if started:
                        square(tile - 1, (t - 1) % 2)
                if last:
                    take_cT(tile, q)
                    square(tile, q)

            take_zT(0, 0)
            group(0, False)
            with act.Fori(1, NB - 1) as g:
                group(g, False)
            group(NB - 1, True)

        @block.vector
        def _(dve):
            dve.wait_ge(s_w, 16 * NW)
            dve.wait_ge(s_const, 6)
            nc.vector.tensor_copy(bias3[0:1], bias[:]).then_inc(s_b, 1)
            dve.wait_ge(s_b, 1)
            nc.vector.tensor_tensor(bias_rest[32:33], bias[:], bias3[0:1], ALU.subtract).then_inc(s_b, 1)
            dve.wait_ge(s_b, 2)
            nc.vector.tensor_copy(bias3[32:33], bias_rest[32:33]).then_inc(s_b, 1)
            dve.wait_ge(s_b, 3)
            nc.vector.tensor_tensor(bias3[64:65], bias_rest[32:33], bias3[32:33], ALU.subtract).then_inc(s_b, 1)
            chain = Chain(dve, s_v, TB * (5 + 1 + E - 1) + 1)

            def statistics(g):
                for t in range(TB):
                    ins = nc.vector.bn_stats(stats[:, t, :], x_res[:, TB * g + t, :])
                chain.link(ins)
                nc.vector.memset(scrap[:], 0.0)
                for t in range(TB):
                    ins = nc.vector.bn_aggr(mv[:, t, :], stats[:, t, :])
                ins.then_inc(s_var, 1)

            def normalise(tile, t, g):
                if t == 0:
                    dve.wait_ge(s_rstd, g + 1)
                nc.vector.tensor_scalar(z[:, t, :], x_res[:, tile, :], mv[:, t, 0:1], rstd[:, t:t + 1],
                                        ALU.subtract, ALU.mult).then_inc(s_z, 1)

            def route(tile, q):
                dve.wait_ge(s_r, tile + 1)
                chain.link(nc.vector.tensor_scalar(lg[:, q, :], rps[:, q, :], -0.5, None, ALU.mult))
                other, own = bc_mid(lg[:, q, :], E), bc_last(lg[:, q, :], E)
                nc.vector.tensor_tensor(above[:], other, own, ALU.is_lt)
                chain.link(nc.vector.tensor_tensor(equal[:], other, own, ALU.is_equal))
                chain.link(nc.vector.tensor_tensor(equal[:], equal[:], before[:], ALU.mult))
                chain.link(nc.vector.tensor_tensor(above[:], above[:], equal[:], ALU.add))
                chain.link(nc.vector.tensor_reduce(rank[:, q, :], above[:], AX, ALU.add))
                nc.vector.scalar_tensor_tensor(picked[:], rank[:, q, :], 2.0, lg[:, q, :], ALU.is_lt, ALU.mult,
                                               accum_out=mid[:, q:q + 1]).then_inc(s_mid, 1)

            def weigh(tile, q):
                dve.wait_ge(s_th, tile + 1)
                chain.link(nc.vector.tensor_scalar(wt[:], th[:, q, :], 0.5, 0.5, ALU.mult, ALU.add))
                nc.vector.scalar_tensor_tensor(gate[:, q, :], rank[:, q, :], 2.0, wt[:], ALU.is_lt,
                                               ALU.mult).then_inc(s_gate, 1)

            def combine(tile, q):
                if not (isinstance(tile, int) and tile < 2):
                    dve.wait_ge(s_ct, tile - 1)
                dve.wait_ge(s_gate, tile + 1)
                for e in range(E):
                    if e % EB == 0:
                        dve.wait_ge(s_s, NBANK * tile + e // EB + 1)
                    if e == 0:
                        ins = nc.vector.tensor_scalar(acc[:, q, :], s[:, q, e, :], gate[:, q, e:e + 1], None,
                                                      ALU.mult)
                    else:
                        ins = nc.vector.scalar_tensor_tensor(acc[:, q, :], s[:, q, e, :], gate[:, q, e:e + 1],
                                                             acc[:, q, :], ALU.mult, ALU.add)
                    if e < E - 1:
                        chain.link(ins)
                ins.then_inc(s_acc, 1)

            def add_input(tile, q, t):
                dve.wait_ge(s_o, tile + 1)
                nc.vector.tensor_tensor(y[:, q, :], ops[:], z[:, t, :], ALU.add).then_inc(s_y, 1)

            def finish(tile, q):
                dve.wait_ge(s_rr, tile + 1)
                nc.vector.scalar_tensor_tensor(o[:, q, :], y[:, q, :], rr[:, q:q + 1], norm_w[:], ALU.mult,
                                               ALU.mult).then_inc(s_on, 1)
                dve.wait_ge(s_on, tile + 1)
                nc.vector.tensor_tensor(x_res[:, tile, :], x_res[:, tile, :], o[:, q, :], ALU.add).then_inc(s_x, 1)

            def group(g, last):
                chain.begin(g)
                chain.base = chain.base + 1
                for t in range(TB):
                    tile, q = TB * g + t, t % 2
                    started = not (is_first(g) and t == 0)
                    if not (last and t == TB - 1):
                        normalise(tile + 1, (t + 1) % TB, g + (t + 1) // TB)
                    if t == TB - 2 and not last:
                        statistics(g + 1)
                    route(tile, q)
                    if not (is_first(g) and t < 2):
                        finish(tile - 2, q)
                    weigh(tile, q)
                    combine(tile, q)
                    if started:
                        add_input(tile - 1, (t - 1) % 2, (t - 1) % TB)
                if last:
                    finish(tile - 1, (t - 1) % 2)
                    add_input(tile, q, t)
                    finish(tile, q)

            chain.begin(0)
            statistics(0)
            normalise(0, 0, 0)
            group(0, False)
            with dve.Fori(1, NB - 1) as g:
                group(g, False)
            group(NB - 1, True)


def phase_ssd(nc, x_res, ident, w):
    H = w["A_log"].shape[0]
    DI = w["W_out"].shape[0]
    HP = DI // H
    NS = w["B_norm_bias"].shape[1]
    NR = NS // 2
    Q = 32
    NC = P // Q
    NQ = P // Q
    HG = H // NQ
    NG = DI // P
    ST = NG
    REST = 2 * NS + 2 * H + NR
    BC, DT, LAM, TH = 0, 2 * NS, 2 * NS + H, 2 * NS + 2 * H
    RMS_EPS = 1e-6
    TWO_PI_HI, ROUND = 6.28125, 12582912.0
    TWO_PI_LO = 2 * np.pi - TWO_PI_HI
    with ExitStack() as ctx:
        def sb(name, shape, dt=F32):
            return ctx.enter_context(nc.sbuf_tensor("s_" + name, shape, dt))

        def ps(name, shape):
            return ctx.enter_context(nc.psum_tensor("s_" + name, shape, F32))

        def sem(name):
            return ctx.enter_context(nc.semaphore("s_" + name))

        w_in = sb("w_in", [P, KD, 2 * DI + REST])
        w_out = sb("w_out", [P, NG, D])
        row = sb("row", [P, 2 * H + 2 * NS])
        a_exp = sb("a_exp", [P, H])
        a_neg = sb("a_neg", [P, H])
        nbias = sb("nbias", [P, 2 * NS])
        half_pi = sb("half_pi", [P, 1])
        half = sb("half", [P, 2 * TB])
        eps = sb("eps", [P, TB])
        rms_eps = sb("rms_eps", [P, 2 * TB])
        per_ns = sb("per_ns", [P, 2 * TB])
        ones = sb("ones", [P, P])
        tri = sb("tri", [P, P])
        tri_c = sb("tri_c", [P, NC, Q])
        after = sb("after", [P, NC, Q])
        shift = sb("shift", [P, P])
        carry = sb("carry", [P, P])
        rep = sb("rep", [H, DI])
        in_chunk = sb("in_chunk", [P, NC])
        mask_rs = sb("mask_rs", [P, Q])
        mask_st = sb("mask_st", [P, Q])

        stats = sb("stats", [P, TB, 6])
        scrap = sb("scrap", [P, 1])
        mv = sb("mv", [P, TB, 2])
        ve = sb("ve", [P, TB])
        rstd = sb("rstd", [P, TB])
        zn = sb("zn", [P, TB, D])
        zT = sb("zT", [P, KD, T])
        rest = sb("rest", [P, TB, REST])
        v = sb("v", [P, TB, H])
        vm = sb("vm", [P, TB, H])
        le = sb("le", [P, TB, H])
        dt = sb("dt", [P, TB, H])
        dtm = sb("dtm", [P, TB])
        th = sb("th", [P, TB, NR])
        pp = sb("pp", [P, TB, H])
        qq = v
        dA = sb("dA", [P, TB, H])
        dA2 = sb("dA2", [P, 2, TB, H])
        bsq = sb("bsq", [P, TB * 2, NS])
        bss = sb("bss", [P, TB * 2])
        bms = sb("bms", [P, TB * 2])
        brr = sb("brr", [P, TB * 2])
        bn = bsq[:].rearrange("p (t a) n -> p t a n", t=TB)
        kk = sb("kk", [P, TB, NR])
        arg = sb("arg", [P, TB, NR])
        aarg = kk
        sn = sb("sn", [P, TB, NR])
        cs = sb("cs", [P, TB, NR])
        rt = zn[:].rearrange("p t (i r) -> p (t i r)", r=NR).rearrange("p (k t a r) -> p k t a r", k=4, t=TB, a=2)
        br = sb("br", [P, TB, 2, NS])
        cbd = sb("cbd", [P, TB])
        bT = sb("bT", [NS, T])
        cT = sb("cT", [NS, 2, T])
        cbm = sb("cbm", [P, 2, T])
        bm = sb("bm", [P, 2, TB, NC, NS])
        gw = sb("gw", [P, 2, TB, H])
        ww = sb("ww", [P, 2, TB, H])
        dl = sb("dl", [P, 2, TB, H])
        xg = sb("xg", [P, 2, TB, DI])
        szT = sb("szT", [P, 2, NG, T])
        ecs = sb("ecs", [P, 2, NG, T])

        mst = sb("mst", [P, 2, H, Q])
        xbd = sb("xbd", [P, 2, NC, HG, NQ, HP])
        xw = sb("xw", [P, 2, DI])
        xdl = sb("xdl", [P, 2, DI])
        e = sb("e", [P, ST, NG, P])
        st = sb("st", [P, NG, 2 * NC, NS])
        pT = sb("pT", [NS, NC, DI])
        y = sb("y", [P, NG, P])
        y2 = sb("y2", [P, NG, P])
        strict = y2[:, 0, :].rearrange("p (c t) -> p c t", t=Q)
        gT = sb("gT", [P, NG, P])
        ms = sb("ms", [P, 1])
        rr = sb("rr", [P, 1])

        dps = ps("dps", [P, 2, NG, P])
        yps = ps("yps", [P, 2, NG, P])
        ops = ps("ops", [P, NG, P])
        sps = ps("sps", [P, 2, NC, NS])
        mps = ps("mps", [P, T])
        fps = ps("fps", [P, T])

        s_w = sem("weights_loaded")
        s_const = sem("constants_ready")
        s_mask = sem("masks_ready")
        s_ae = sem("a_exp_ready")
        s_var = sem("var_ready")
        s_pool = sem("pool_step")
        s_rstd = sem("rstd_ready")
        s_v = sem("vector_front_step")
        s_zn = sem("zn_ready")
        s_f = sem("front_full")
        s_zT = sem("zT_ready")
        s_rest = sem("rest_ready")
        s_vm = sem("vm_ready")
        s_act = sem("scalar_front_step")
        s_vl = sem("vl_ready")
        s_qq = sem("qq_ready")
        s_bss = sem("bss_ready")
        s_brr = sem("brr_ready")
        s_arg = sem("arg_ready")
        s_trig = sem("trig_ready")
        s_g = sem("g_ready")
        s_br = sem("br_ready")
        s_bT = sem("bT_ready")
        s_cbm = sem("cbm_ready")
        s_dcs = sem("dcs_ready")
        s_xg = sem("xg_ready")
        s_hcs = sem("head_decay_ready")
        s_sz = sem("sz_ready")
        s_ecs = sem("ecs_ready")
        s_front = sem("front_weights_ready")
        s_bm = sem("bm_ready")
        s_mst = sem("mst_ready")
        s_prep = sem("x_scaled")
        s_d = sem("d_full")
        s_e = sem("e_ready")
        s_em = sem("e_masked")
        s_Y = sem("y_added")
        s_S = sem("states_full")
        s_rs = sem("state_step")
        s_z0 = sem("state_cleared")
        s_pt = sem("prev_turned")
        s_pT = sem("prev_ready")
        s_yo = sem("y_off_full")
        s_t1 = sem("t1_ready")
        s_y = sem("y_ready")
        s_gT = sem("gT_ready")
        s_y2 = sem("y2_ready")
        s_tail = sem("tail_full")
        s_ms = sem("ms_ready")
        s_rr = sem("rr_ready")
        s_x = sem("x_updated")

        NW, NCONST = 7, 25
        ZT, RE, XP, CUM, QS, WC, ZP, BCT, CBT, HC, EC = 0, 2, 6, 10, 11, 12, 13, 17, 18, 19, 20
        NF = 24
        block = ctx.enter_context(nc.Block())

        def is_first(n):
            return isinstance(n, int) and n == 0

        def full(b, use):
            return b * NF + use + 1

        def heads(ap, n=HP):
            return bc_last(ap, n)

        @block.sync
        def _(sp):
            for n, name in enumerate(("A_log", "dt_bias")):
                sp.dma_start(row[:, n * H:(n + 1) * H], w[name].partition_broadcast(P)).then_inc(s_w, 16)
            for n, name in enumerate(("B_norm_bias", "C_norm_bias")):
                sp.dma_start(row[:, 2 * H + n * NS:2 * H + (n + 1) * NS],
                             w[name].rearrange("g n -> (g n)").partition_broadcast(P)).then_inc(s_w, 16)
            for k in range(KD):
                sp.dma_start(w_in[:, k], w["W_in"][k * P:(k + 1) * P, :]).then_inc(s_w, 16)
            sp.dma_start(w_out[:], w["W_out"].rearrange("(g p) n -> p g n", p=P)).then_inc(s_w, 16)

        @block.gpsimd
        def _(pool):
            done = [0]

            def step(ins):
                done[0] += 1
                ins.then_inc(s_const, 1)

            def select(out, op, base, pattern, channel, fill=0.0):
                pool.wait_ge(s_const, done[0])
                step(nc.gpsimd.affine_select(out=out, in_=out, compare_op=op, fill=fill, base=base,
                                             pattern=pattern, channel_multiplier=channel))

            for tile_, value in ((half, -0.5), (eps, LN_EPS), (rms_eps, RMS_EPS), (per_ns, 1.0 / NS), (half_pi, np.pi / 2), (ones, 1.0),
                                 (tri, 1.0), (tri_c, 1.0), (after, 1.0), (shift, 0.0), (carry, 0.0),
                                 (in_chunk, 1.0), (xbd, 0.0), (rep, 1.0)):
                step(nc.gpsimd.memset(tile_[:], float(value)))
            select(tri[:], ALU.is_ge, 0, [[1, P]], -1)
            select(tri_c[:], ALU.is_ge, 0, [[Q, NC], [1, Q]], -1)
            select(tri_c[:], ALU.is_ge, 0, [[-Q, NC], [0, Q]], 1)
            select(after[:], ALU.is_gt, 0, [[-Q, NC], [-1, Q]], 1)
            select(after[:], ALU.is_gt, Q, [[Q, NC], [0, Q]], -1)
            select(shift[:], ALU.not_equal, 1, [[1, P]], -1, 1.0)
            select(carry[:], ALU.not_equal, 1 - P, [[1, P]], P, 1.0)
            select(in_chunk[:], ALU.is_ge, 0, [[-Q, NC]], 1)
            select(in_chunk[:], ALU.is_ge, Q - 1, [[Q, NC]], -1)
            select(rep[:], ALU.is_ge, 0, [[1, DI]], -HP)
            select(rep[:], ALU.is_ge, HP - 1, [[-1, DI]], HP)
            chain = Chain(pool, s_pool, 3)

            def scales(b):
                chain.begin(b)
                pool.wait_ge(s_var, b + 1)
                chain.link(nc.gpsimd.tensor_tensor(ve[:], mv[:, :, 1], eps[:], ALU.add))
                nc.gpsimd.tensor_tensor(rstd[:], ve[:], half[:, 0:TB], ALU.pow).then_inc(s_rstd, 1)

            def bc_scales(b):
                pool.wait_ge(s_bss, b + 1)
                chain.link(nc.gpsimd.tensor_tensor(bms[:], bss[:], per_ns[:], ALU.mult))
                chain.link(nc.gpsimd.tensor_tensor(bms[:], bms[:], rms_eps[:], ALU.add))
                nc.gpsimd.tensor_tensor(brr[:], bms[:], half[:], ALU.pow).then_inc(s_brr, 1)

            def spread_b(b):
                pool.wait_ge(s_br, b + 1)
                for t in range(TB):
                    ins = nc.gpsimd.tensor_tensor(bm[:, b % 2, t], bc_mid(br[:, t, 0, :], NC),
                                                  bc_last(in_chunk[:], NS), ALU.mult)
                ins.then_inc(s_bm, 1)

            def decay_operand(b, t):
                tile = TB * b + t
                pool.wait_ge(s_qq, b + 1)
                if not (isinstance(tile, int) and tile < 2):
                    pool.wait_ge(s_d, ST * tile - ST)
                nc.gpsimd.tensor_tensor(mst[:, t % 2], bc_last(dA2[:, b % 2, t, :], Q), bc_mid(mask_rs[:], H),
                                        ALU.mult).then_inc(s_mst, 1)

            def rms(tile):
                pool.wait_ge(s_ms, tile + 1)
                nc.gpsimd.tensor_tensor(rr[:], ms[:], half[:, 0:1], ALU.pow).then_inc(s_rr, 1)

            def sequence(b, ahead):
                for t in range(TB):
                    tile = TB * b + t
                    if t + 1 < TB:
                        decay_operand(b, t + 1)
                    if not (is_first(b) and t == 0):
                        if t > 1 or not is_first(b):
                            rms(tile - 2)
                    if ahead and t == 0:
                        scales(b + 1)
                    if ahead and t == 1:
                        bc_scales(b + 1)
                    if ahead and t == 3:
                        spread_b(b + 1)
                        decay_operand(b + 1, 0)
                if not ahead:
                    rms(tile - 1)
                    rms(tile)

            assert done[0] == NCONST, done[0]
            pool.wait_ge(s_const, NCONST)
            pool.wait_ge(s_mask, 3)
            scales(0)
            bc_scales(0)
            spread_b(0)
            decay_operand(0, 0)
            sequence(0, True)
            with pool.Fori(1, NB - 1) as b:
                sequence(b, True)
            sequence(NB - 1, False)

        @block.tensor
        def _(pe):
            def turn_zn(b, k):
                if k == 0:
                    pe.wait_ge(s_zn, b + 1)
                    if not is_first(b):
                        pe.wait_ge(s_ecs, NG * b)
                else:
                    pe.wait_ge(s_zT, KD * b + k)
                for t in range(TB):
                    mm = nc.tensor.transpose(fps[:, t * P:(t + 1) * P], zn[:, t, k * P:(k + 1) * P], ident[:])
                mm.then_inc(s_f, 1)

            def token_proj(b, t, cols, read, count):
                pe.wait_ge(read, count)
                n = cols.stop - cols.start
                for k in range(KD):
                    mm = nc.tensor.matmul(fps[:, 0:n], zT[:, k, t * P:(t + 1) * P], w_in[:, k, cols],
                                          start=(k == 0), stop=(k == KD - 1))
                mm.then_inc(s_f, 1)

            def project_rest(b, ts):
                for t in ts:
                    if t == 0:
                        pe.wait_ge(s_zT, KD * (b + 1))
                    token_proj(b, t, slice(2 * DI, 2 * DI + REST), s_zT if t == 0 else s_rest,
                               KD * (b + 1) if t == 0 else TB * b + t)

            def project_x(b, ts):
                for t in ts:
                    token_proj(b, t, slice(DI, 2 * DI), s_rest if t == 0 else s_xg,
                               TB * (b + 1) if t == 0 else TB * b + t)

            def sums(b):
                pe.wait_ge(s_qq, b + 1)
                pe.wait_ge(s_xg, TB * (b + 1))
                cum = fps[:, 0:TB * NR].rearrange("p (t n) -> p t n", t=TB)
                nc.tensor.matmul(cum, tri[:], th[:], start=True, stop=False, skip_group_check=True)
                for j in range(TB - 1):
                    mm = nc.tensor.matmul(cum[:, j + 1:, :], ones[:], bc_mid(th[:, j, :], TB - 1 - j),
                                          start=False, stop=(j == TB - 2), skip_group_check=True)
                mm.then_inc(s_f, 1)
                pe.wait_ge(s_arg, b + 1)
                nxt = fps[:, 0:TB * H].rearrange("p (t h) -> p t h", t=TB)
                nc.tensor.matmul(nxt, shift[:], qq[:], start=True, stop=False, skip_group_check=True)
                nc.tensor.matmul(nxt[:, 0:TB - 1, :], carry[:], qq[:, 1:TB, :], start=False, stop=True,
                                 skip_group_check=True).then_inc(s_f, 1)
                pe.wait_ge(s_g, b + 1)
                nc.tensor.matmul(fps[:, 0:TB * H], after[:].rearrange("p c t -> p (c t)"),
                                 dA[:].rearrange("p t h -> p (t h)"), start=True, stop=True).then_inc(s_f, 1)

            def project_z(b, gs):
                for g in gs:
                    pe.wait_ge(s_dcs if g == 0 else s_sz, b + 1 if g == 0 else NG * b + g)
                    for k in range(KD):
                        mm = nc.tensor.matmul(fps[:], w_in[:, k, g * P:(g + 1) * P], zT[:, k, :],
                                              start=(k == 0), stop=(k == KD - 1))
                    mm.then_inc(s_f, 1)

            def turn_bc(b):
                pe.wait_ge(s_sz, NG * (b + 1))
                pe.wait_ge(s_br, b + 1)
                for t in range(TB):
                    mm = nc.tensor.transpose(fps[:, t * P:(t + 1) * P], br[:, t].rearrange("p a n -> p (a n)"),
                                             ident[:])
                mm.then_inc(s_f, 1)

            def c_dot_b(b):
                pe.wait_ge(s_bT, 2 * (b + 1))
                for t in range(TB):
                    mm = nc.tensor.matmul(fps[:, t * P:(t + 1) * P], bT[:, t * P:(t + 1) * P],
                                          cT[:, b % 2, t * P:(t + 1) * P], start=(t == 0), stop=(t == TB - 1),
                                          skip_group_check=True)
                mm.then_inc(s_f, 1)

            def running_decay(b):
                pe.wait_ge(s_cbm, b + 1)
                for t in range(TB):
                    mm = nc.tensor.matmul(fps[0:H, t * P:(t + 1) * P], dA[:, t, :],
                                          tri_c[:].rearrange("p c t -> p (c t)"), start=(t == 0),
                                          stop=(t == TB - 1), skip_group_check=True)
                mm.then_inc(s_f, 1)
                pe.wait_ge(s_hcs, b + 1)
                for g in range(NG):
                    if g > 0:
                        pe.wait_ge(s_ecs, NG * b + g)
                    nc.tensor.matmul(fps[:], rep[:, g * P:(g + 1) * P], bT[:], start=True,
                                     stop=True).then_inc(s_f, 1)

            pieces = {2: lambda b: turn_zn(b, 0), 3: lambda b: turn_zn(b, 1),
                      4: lambda b: project_rest(b, (0, 1)), 5: lambda b: project_rest(b, (2, 3)),
                      6: lambda b: project_x(b, (0, 1)), 7: lambda b: project_x(b, (2, 3)), 8: sums,
                      9: lambda b: project_z(b, (0, 1)), 10: lambda b: project_z(b, (2, 3)),
                      12: turn_bc, 13: c_dot_b, 14: running_decay}

            def decays(tile, t, j):
                step = ST * tile + j
                if j == 0:
                    pe.wait_ge(s_mst, tile + 1)
                if not (isinstance(step, int) and step < 2):
                    pe.wait_ge(s_e, step - 1)
                for i in range(NG):
                    hg = NG * j + i
                    mm = nc.tensor.matmul(dps[:, j % 2, i, :],
                                          mst[:, t % 2, hg * NQ:(hg + 1) * NQ, :].rearrange("p h s -> p (h s)"),
                                          tri_c[:].rearrange("p c t -> p (c t)"), start=(i == 0),
                                          stop=(i == NG - 1), skip_group_check=True)
                mm.then_inc(s_d, 1)

            def own_token(tile, t):
                pe.wait_ge(s_prep, tile + 1)
                if not (isinstance(tile, int) and tile < 2):
                    pe.wait_ge(s_y, tile - 1)
                for g in range(NG):
                    nc.tensor.matmul(yps[:, t % 2, g, :], xdl[:, t % 2, g * P:(g + 1) * P], ident[:],
                                     start=(g == 0), stop=False, skip_group_check=True)

            def earlier_tokens(tile, t, j):
                pe.wait_ge(s_em, ST * tile + j + 1)
                for i in range(NG):
                    for c in range(NC):
                        mm = nc.tensor.matmul(yps[i * Q:(i + 1) * Q, t % 2, j, c * Q:(c + 1) * Q],
                                              xbd[:, t % 2, c, NG * j + i].rearrange("p h q -> p (h q)"),
                                              e[:, j, i, c * Q:(c + 1) * Q], start=False,
                                              stop=(j == ST - 1 and c == NC - 1), skip_group_check=True)
                mm.then_inc(s_Y, 1)

            def chunk_states(b, tile, t, pair):
                if pair == 0 and t == 0:
                    pe.wait_ge(s_bm, b + 1)
                if pair == 1 or not is_first(tile):
                    pe.wait_ge(s_rs, 2 * NC * (2 * tile + pair))
                for i in range(2):
                    g = 2 * pair + i
                    mm = nc.tensor.matmul(sps[:, i].rearrange("p c n -> p (c n)"), xw[:, t % 2, g * P:(g + 1) * P],
                                          bm[:, b % 2, t].rearrange("p c n -> p (c n)"), start=(i == 0),
                                          stop=(i == 1), skip_group_check=True)
                mm.then_inc(s_S, 1)

            def turn_prev(tile, t, cs_):
                for c in cs_:
                    if c == 0:
                        pe.wait_ge(s_rs, 4 * NC * (tile + 1))
                        if not (isinstance(tile, int) and tile < 2):
                            pe.wait_ge(s_x, tile - 1)
                    else:
                        pe.wait_ge(s_pT, NC * tile + c)
                    for g in range(NG):
                        mm = nc.tensor.matmul(mps[0:NS, g * P:(g + 1) * P], st[:, g, NC * (t % 2) + c, :],
                                              ident[:], start=True, stop=True, is_transpose=(g > 0))
                    mm.then_inc(s_pt, 1)

            def earlier_chunks(b, tile, t):
                pe.wait_ge(s_pT, NC * (tile + 1))
                if not is_first(tile):
                    pe.wait_ge(s_t1, tile)
                for g in range(NG):
                    for c in range(NC):
                        at = (t * NC + c) * Q
                        mm = nc.tensor.matmul(ops[:, g, c * Q:(c + 1) * Q], pT[:, c, g * P:(g + 1) * P],
                                              cT[:, b % 2, at:at + Q], start=(g == 0 and c == 0),
                                              stop=(g == NG - 1 and c == NC - 1), skip_group_check=True)
                mm.then_inc(s_yo, 1)

            def tail(tile):
                pe.wait_ge(s_y2, tile + 1)
                for g in range(NG):
                    nc.tensor.matmul(mps[:, D:D + 1], y2[:, g, :], ones[:, 0:1], start=(g == 0), stop=(g == NG - 1))
                pe.wait_ge(s_gT, tile + 1)
                for g in range(NG):
                    mm = nc.tensor.matmul(mps[:, 0:D], gT[:, g, :], w_out[:, g, :], start=(g == 0),
                                          stop=(g == NG - 1))
                mm.then_inc(s_tail, 1)

            def sequence(b, ahead):
                for t in range(TB):
                    tile = TB * b + t
                    started = not (is_first(b) and t == 0)
                    for j in range(ST):
                        if j + 1 < ST:
                            decays(tile, t, j + 1)
                        elif t + 1 < TB or ahead:
                            decays(tile + 1, t + 1, 0) if t + 1 < TB else None
                        if j == 0:
                            own_token(tile, t)
                            chunk_states(b, tile, t, 0)
                        if j == 1:
                            chunk_states(b, tile, t, 1)
                            if started:
                                earlier_chunks(b if t else b - 1, tile - 1, (t - 1) % TB)
                        if j == 2:
                            turn_prev(tile, t, (0, 1))
                        if j == 3:
                            turn_prev(tile, t, (2, 3))
                        earlier_tokens(tile, t, j)
                        if j == 3:
                            if started:
                                pe.wait_ge(s_pT, NC * (tile + 1))
                                tail(tile - 1)
                        if ahead and ST * t + j in pieces:
                            pieces[ST * t + j](b + 1)
                if ahead:
                    decays(tile + 1, 0, 0)
                else:
                    earlier_chunks(b, tile, t)
                    tail(tile)

            pe.wait_ge(s_w, 16 * NW)
            pe.wait_ge(s_const, NCONST)
            for piece in pieces.values():
                piece(0)
            decays(0, 0, 0)
            sequence(0, True)
            with pe.Fori(1, NB - 1) as b:
                sequence(b, True)
            sequence(NB - 1, False)

        @block.scalar
        def _(act):
            chain = Chain(act, s_act, 2)

            def take_zT(b, k):
                act.wait_ge(s_f, full(b, ZT + k))
                nc.scalar.activation(zT[:, k, :], fps[:], ACT.Copy).then_inc(s_zT, 1)

            def take_rest(b, ts):
                for t in ts:
                    act.wait_ge(s_f, full(b, RE + t))
                    if t == 0 and not is_first(b):
                        act.wait_ge(s_trig, b)
                    nc.scalar.activation(rest[:, t, :], fps[:, 0:REST], ACT.Copy).then_inc(s_rest, 1)

            def exps(b):
                chain.begin(b)
                act.wait_ge(s_vm, b + 1)
                nc.scalar.activation(le[:], rest[:, :, LAM:LAM + H], ACT.Exp, scale=-1.0)
                chain.link(nc.scalar.activation(vm[:], vm[:], ACT.Exp))
                nc.scalar.activation(vm[:], vm[:], ACT.Ln, bias=1.0).then_inc(s_vl, 1)

            def take_x(b, ts):
                for t in ts:
                    act.wait_ge(s_f, full(b, XP + t))
                    nc.scalar.activation(xg[:, b % 2, t, :], fps[:], ACT.Silu).then_inc(s_xg, 1)

            def trig(b):
                act.wait_ge(s_arg, b + 1)
                nc.scalar.activation(sn[:], arg[:], ACT.Sin)
                chain.link(nc.scalar.activation(aarg[:], arg[:], ACT.Abs))
                nc.scalar.activation(cs[:], aarg[:], ACT.Sin, bias=half_pi[:], scale=-1.0).then_inc(s_trig, 1)

            def chunk_decay(b):
                act.wait_ge(s_f, full(b, WC))
                nc.scalar.activation(ww[:, b % 2].rearrange("p t h -> p (t h)"), fps[:, 0:TB * H],
                                     ACT.Exp).then_inc(s_dcs, 1)

            def take_z(b, gs):
                for g in gs:
                    act.wait_ge(s_f, full(b, ZP + g))
                    nc.scalar.activation(szT[:, b % 2, g, :], fps[:], ACT.Silu).then_inc(s_sz, 1)

            def take_bc(b):
                act.wait_ge(s_f, full(b, BCT))
                nc.scalar.activation(bT[:], fps[0:NS, :], ACT.Copy).then_inc(s_bT, 1)
                nc.scalar.activation(cT[:, b % 2, :], fps[NS:2 * NS, :], ACT.Copy).then_inc(s_bT, 1)

            def take_decay(b):
                act.wait_ge(s_f, full(b, HC))
                nc.scalar.activation(bT[0:H, :], fps[0:H, :], ACT.Exp).then_inc(s_hcs, 1)
                for g in range(NG):
                    act.wait_ge(s_f, full(b, EC + g))
                    nc.scalar.activation(ecs[:, b % 2, g, :], fps[:], ACT.Copy).then_inc(s_ecs, 1)

            pieces = {2: lambda b: take_zT(b, 0), 3: lambda b: take_zT(b, 1),
                      4: lambda b: take_rest(b, (0, 1)), 5: lambda b: take_rest(b, (2, 3)),
                      6: lambda b: (exps(b), take_x(b, (0, 1))), 7: lambda b: take_x(b, (2, 3)),
                      8: lambda b: chunk_decay(b), 9: lambda b: (trig(b), take_z(b, (0, 1))),
                      10: lambda b: take_z(b, (2, 3)), 12: take_bc, 14: take_decay}

            def decay(tile, j):
                step = ST * tile + j
                act.wait_ge(s_d, step + 1)
                if not is_first(tile):
                    act.wait_ge(s_Y, step - ST + 1)
                nc.scalar.activation(e[:, j].rearrange("p g t -> p (g t)"),
                                     dps[:, j % 2].rearrange("p g t -> p (g t)"), ACT.Exp).then_inc(s_e, 1)

            def take_prev(tile, cs_):
                for c in cs_:
                    act.wait_ge(s_pt, NC * tile + c + 1)
                    if c == 0 and not is_first(tile):
                        act.wait_ge(s_yo, tile)
                    nc.scalar.activation(pT[:, c, :], mps[0:NS, :], ACT.Copy).then_inc(s_pT, 1)

            def square(tile):
                act.wait_ge(s_y, tile + 1)
                if not is_first(tile):
                    act.wait_ge(s_tail, tile)
                nc.scalar.activation(y2[:], y[:], ACT.Square).then_inc(s_y2, 1)

            def sequence(b, ahead):
                for t in range(TB):
                    tile = TB * b + t
                    started = not (is_first(b) and t == 0)
                    for j in range(ST):
                        decay(tile, j)
                        if j == 2:
                            take_prev(tile, (0, 1))
                            if started:
                                square(tile - 1)
                        if j == 3:
                            take_prev(tile, (2, 3))
                        if ahead and ST * t + j in pieces:
                            pieces[ST * t + j](b + 1)
                if not ahead:
                    square(tile)

            act.wait_ge(s_w, 16 * NW)
            act.wait_ge(s_const, NCONST)
            nc.scalar.activation(a_exp[:], row[:, 0:H], ACT.Exp).then_inc(s_ae, 1)
            for piece in pieces.values():
                piece(0)
            sequence(0, True)
            with act.Fori(1, NB - 1) as b:
                sequence(b, True)
            sequence(NB - 1, False)

        @block.vector
        def _(dve):
            chain = Chain(dve, s_v, 16)

            def statistics(b):
                chain.begin(b)
                for t in range(TB):
                    ins = nc.vector.bn_stats(stats[:, t, :], x_res[:, TB * b + t, :])
                chain.link(ins)
                nc.vector.memset(scrap[:], 0.0)
                for t in range(TB):
                    ins = nc.vector.bn_aggr(mv[:, t, :], stats[:, t, :])
                ins.then_inc(s_var, 1)

            def normalise(b):
                dve.wait_ge(s_rstd, b + 1)
                for t in range(TB):
                    ins = nc.vector.tensor_scalar(zn[:, t, :], x_res[:, TB * b + t, :], mv[:, t, 0:1],
                                                  rstd[:, t:t + 1], ALU.subtract, ALU.mult)
                ins.then_inc(s_zn, 1)

            def raw(b):
                dve.wait_ge(s_rest, TB * (b + 1))
                chain.link(nc.vector.tensor_tensor(v[:], rest[:, :, DT:DT + H], bc_mid(row[:, H:2 * H], TB), ALU.add))
                nc.vector.tensor_scalar(vm[:], v[:], 30.0, None, ALU.min).then_inc(s_vm, 1)
                bc = rest[:, :, 0:2 * NS]
                chain.link(nc.vector.tensor_tensor(bsq[:].rearrange("p (t a) n -> p t (a n)", t=TB), bc, bc, ALU.mult))
                nc.vector.tensor_reduce(bss[:], bsq[:], AX, ALU.add).then_inc(s_bss, 1)

            def rates(b):
                dve.wait_ge(s_vl, b + 1)
                nc.vector.tensor_tensor(dt[:], v[:], vm[:], ALU.max)
                chain.link(nc.vector.tensor_scalar(le[:], le[:], 1.0, None, ALU.add))
                nc.vector.tensor_scalar(dt[:], dt[:], 1e-4, 0.5, ALU.max, ALU.min)
                chain.link(nc.vector.reciprocal(le[:], le[:]))
                nc.vector.tensor_tensor(dA[:], dt[:], bc_mid(a_neg[:], TB), ALU.mult)
                nc.vector.tensor_reduce(dtm[:], dt[:], AX, ALU.add)
                chain.link(nc.vector.tensor_tensor(pp[:], dt[:], le[:], ALU.mult))
                nc.vector.tensor_scalar(dtm[:], dtm[:], -1.0 / H, None, ALU.mult)
                chain.link(nc.vector.tensor_copy(dA2[:, b % 2], dA[:]))
                nc.vector.tensor_tensor(th[:], rest[:, :, TH:TH + NR], bc_last(dtm[:], NR), ALU.mult)
                nc.vector.tensor_tensor(qq[:], dt[:], pp[:], ALU.subtract).then_inc(s_qq, 1)
                dve.wait_ge(s_brr, b + 1)
                chain.link(nc.vector.tensor_tensor(
                    bn, rest[:, :, 0:2 * NS].rearrange("p t (a n) -> p t a n", a=2),
                    brr[:].rearrange("p (t a) -> p t a", t=TB).unsqueeze(3).to_broadcast([P, TB, 2, NS]), ALU.mult))
                chain.link(nc.vector.tensor_tensor(
                    bn.rearrange("p t a n -> p t (a n)"), bn.rearrange("p t a n -> p t (a n)"),
                    bc_mid(nbias[:], TB), ALU.mult))

            def angles(b):
                dve.wait_ge(s_f, full(b, CUM))
                cum = fps[:, 0:TB * NR].rearrange("p (t n) -> p t n", t=TB)
                chain.link(nc.vector.tensor_scalar(kk[:], cum, float(1 / (2 * np.pi)), ROUND, ALU.mult, ALU.add))
                chain.link(nc.vector.tensor_scalar(kk[:], kk[:], ROUND, None, ALU.subtract))
                chain.link(nc.vector.scalar_tensor_tensor(arg[:], kk[:], -TWO_PI_HI, cum, ALU.mult, ALU.add))
                chain.link(nc.vector.scalar_tensor_tensor(arg[:], kk[:], -TWO_PI_LO, arg[:], ALU.mult, ALU.add))
                nc.vector.tensor_scalar(arg[:], arg[:], 3.1415925, -3.1415925, ALU.min, ALU.max).then_inc(s_arg, 1)
                dve.wait_ge(s_f, full(b, QS))
                nc.vector.tensor_tensor(gw[:, b % 2], pp[:], fps[:, 0:TB * H].rearrange("p (t h) -> p t h", t=TB),
                                        ALU.add).then_inc(s_g, 1)

            def rotate(b):
                dve.wait_ge(s_trig, b + 1)
                x1, x2 = bn[:, :, :, 0:NR], bn[:, :, :, NR:]
                cosb = cs[:].unsqueeze(2).to_broadcast([P, TB, 2, NR])
                sinb = sn[:].unsqueeze(2).to_broadcast([P, TB, 2, NR])
                nc.vector.tensor_tensor(rt[:, 0], x1, cosb, ALU.mult)
                nc.vector.tensor_tensor(rt[:, 1], x2, sinb, ALU.mult)
                nc.vector.tensor_tensor(rt[:, 2], x1, sinb, ALU.mult)
                chain.link(nc.vector.tensor_tensor(rt[:, 3], x2, cosb, ALU.mult))
                nc.vector.tensor_tensor(br[:, :, :, 0:NR], rt[:, 0], rt[:, 1], ALU.subtract)
                nc.vector.tensor_tensor(br[:, :, :, NR:], rt[:, 2], rt[:, 3], ALU.add).then_inc(s_br, 1)
                dve.wait_ge(s_br, b + 1)
                dve.wait_ge(s_dcs, b + 1)
                nc.vector.tensor_tensor(ww[:, b % 2], ww[:, b % 2], gw[:, b % 2], ALU.mult)
                chain.link(nc.vector.tensor_tensor(bsq[:, 0:TB, :], br[:, :, 0, :], br[:, :, 1, :], ALU.mult))
                chain.link(nc.vector.tensor_reduce(cbd[:], bsq[:, 0:TB, :], AX, ALU.add))
                nc.vector.tensor_tensor(dl[:, b % 2], pp[:], bc_last(cbd[:], H), ALU.mult).then_inc(s_front, 1)

            def mask_cb(b):
                dve.wait_ge(s_f, full(b, CBT))
                for c in range(NC):
                    rows = slice(c * Q, (c + 1) * Q)
                    for i in range(NQ):
                        ins = nc.vector.tensor_tensor(
                            cbm[i * Q:(i + 1) * Q, b % 2, :].rearrange("p (k t) -> p k t", t=P)[:, :, rows],
                            fps[rows, :].rearrange("p (k t) -> p k t", t=P)[:, :, rows],
                            bc_mid(mask_st[rows], TB), ALU.mult)
                ins.then_inc(s_cbm, 1)
                chain.end()

            def prepare(b, tile, t):
                if t == 0:
                    dve.wait_ge(s_front, b + 1)
                    dve.wait_ge(s_xg, TB * (b + 1))
                if not (isinstance(tile, int) and tile < 2):
                    dve.wait_ge(s_Y, ST * tile - ST)
                x = xg[:, b % 2, t, :].rearrange("p (h q) -> p h q", q=HP)
                for c in range(NC):
                    for i in range(NQ):
                        src = slice(c * Q, (c + 1) * Q)
                        nc.vector.tensor_tensor(
                            xbd[i * Q:(i + 1) * Q, t % 2, c, :, i, :],
                            x[src].rearrange("p (g i) q -> p i g q", i=NQ)[:, i],
                            heads(gw[src, b % 2, t, :].rearrange("p (g i) -> p i g", i=NQ)[:, i]), ALU.mult)
                nc.vector.tensor_tensor(xw[:, t % 2, :].rearrange("p (h q) -> p h q", q=HP), x,
                                        heads(ww[:, b % 2, t, :]), ALU.mult)
                nc.vector.tensor_tensor(xdl[:, t % 2, :].rearrange("p (h q) -> p h q", q=HP), x,
                                        heads(dl[:, b % 2, t, :]), ALU.mult).then_inc(s_prep, 1)

            def mask(b, tile, t, j):
                dve.wait_ge(s_e, ST * tile + j + 1)
                if t == 0 and j == 0:
                    dve.wait_ge(s_cbm, b + 1)
                nc.vector.tensor_tensor(e[:, j], e[:, j], bc_mid(cbm[:, b % 2, t * P:(t + 1) * P], NG),
                                        ALU.mult).then_inc(s_em, 1)

            def carry_states(b, tile, t, pair):
                if t == 0 and pair == 0:
                    if not is_first(b):
                        dve.wait_ge(s_pt, NC * tile)
                    nc.vector.memset(st[:, :, 0, :], 0.0).then_inc(s_z0, 1)
                    dve.wait_ge(s_z0, b + 1)
                    dve.wait_ge(s_ecs, NG * (b + 1))
                elif pair == 0:
                    dve.wait_ge(s_pt, NC * tile)
                dve.wait_ge(s_S, 2 * tile + pair + 1)
                base = 4 * NC * tile + 2 * NC * pair
                for c in range(NC):
                    for i in range(2):
                        g, n = 2 * pair + i, 2 * c + i
                        if c > 0:
                            dve.wait_ge(s_rs, base + n - 1)
                        slot = NC * (t % 2) + c
                        at = t * P + c * Q + Q - 1
                        nc.vector.scalar_tensor_tensor(st[:, g, (slot + 1) % (2 * NC), :], st[:, g, slot, :],
                                                       ecs[:, b % 2, g, at:at + 1], sps[:, i, c, :], ALU.mult,
                                                       ALU.add).then_inc(s_rs, 1)

            def combine(b, tile, t):
                dve.wait_ge(s_yo, tile + 1)
                nc.vector.tensor_tensor(y[:], ops[:], ecs[:, b % 2, :, t * P:(t + 1) * P],
                                        ALU.mult).then_inc(s_t1, 1)
                dve.wait_ge(s_t1, tile + 1)
                dve.wait_ge(s_Y, ST * (tile + 1))
                if not is_first(tile):
                    dve.wait_ge(s_tail, tile)
                nc.vector.tensor_tensor(y[:], yps[:, t % 2], y[:], ALU.add).then_inc(s_y, 1)
                dve.wait_ge(s_y, tile + 1)
                dve.wait_ge(s_sz, NG * (b + 1))
                nc.vector.tensor_tensor(gT[:], y[:], szT[:, b % 2, :, t * P:(t + 1) * P], ALU.mult).then_inc(s_gT, 1)

            def mean_square(tile):
                dve.wait_ge(s_tail, tile + 1)
                nc.vector.tensor_scalar(ms[:], mps[:, D:D + 1], 1.0 / DI, RMS_EPS, ALU.mult, ALU.add).then_inc(s_ms, 1)

            def update(tile):
                dve.wait_ge(s_rr, tile + 1)
                nc.vector.scalar_tensor_tensor(x_res[:, tile, :], mps[:, 0:D], rr[:], x_res[:, tile, :], ALU.mult,
                                               ALU.add).then_inc(s_x, 1)

            pieces = {0: statistics, 1: normalise, 6: raw, 7: rates, 8: angles, 11: rotate, 13: mask_cb}

            def sequence(b, ahead):
                for t in range(TB):
                    tile = TB * b + t
                    for j in range(ST):
                        mask(b, tile, t, j)
                        if j < 2:
                            carry_states(b, tile, t, j)
                        two_back = not (is_first(b) and t < 2)
                        if j == 0 and two_back:
                            mean_square(tile - 2)
                        if j == 1 and two_back:
                            update(tile - 2)
                        if j == 2 and not (is_first(b) and t == 0):
                            combine(b if t else b - 1, tile - 1, (t - 1) % TB)
                        if ahead and ST * t + j in pieces:
                            pieces[ST * t + j](b + 1)
                        if j == 3 and (t + 1 < TB or ahead):
                            prepare(b if t + 1 < TB else b + 1, tile + 1, (t + 1) % TB)
                if not ahead:
                    mean_square(tile - 1)
                    update(tile - 1)
                    combine(b, tile, t)
                    mean_square(tile)
                    update(tile)

            dve.wait_ge(s_w, 16 * NW)
            dve.wait_ge(s_const, NCONST)
            nc.vector.tensor_tensor(strict.rearrange("p c t -> p (c t)"), tri_c[:].rearrange("p c t -> p (c t)"),
                                    ident[:], ALU.subtract).then_inc(s_mask, 1)
            dve.wait_ge(s_mask, 1)
            nc.vector.tensor_reduce(mask_st[:], strict.rearrange("p c t -> p t c"), AX, ALU.add).then_inc(s_mask, 1)
            nc.vector.tensor_reduce(mask_rs[:], after[:].rearrange("p c t -> p t c"), AX, ALU.add).then_inc(s_mask, 1)
            nc.vector.tensor_copy(nbias[:, 0:NS], row[:, 2 * H:2 * H + NS])
            nc.vector.tensor_scalar(nbias[:, NS:], row[:, 2 * H + NS:], float(NS) ** -0.5, None, ALU.mult)
            dve.wait_ge(s_ae, 1)
            nc.vector.tensor_scalar(a_neg[:], a_exp[:], -1.0, None, ALU.mult).then_inc(s_mask, 1)
            dve.wait_ge(s_mask, 4)
            for piece in pieces.values():
                piece(0)
            prepare(0, 0, 0)
            sequence(0, True)
            with dve.Fori(1, NB - 1) as b:
                sequence(b, True)
            sequence(NB - 1, False)


def hybrid_block(nc, ins, out):
    with ExitStack() as ctx:
        x_res = ctx.enter_context(nc.sbuf_tensor("x_res", [P, NT, D], F32))
        ident = ctx.enter_context(nc.sbuf_tensor("ident", [P, P], F32))
        a = {n[len("L0_attn_a_"):]: v for n, v in ins.items() if n.startswith("L0_attn_a_")}
        s = {n[len("L0_attn_b_"):]: v for n, v in ins.items() if n.startswith("L0_attn_b_")}
        f = {n[len("L0_ffn_"):]: v for n, v in ins.items() if n.startswith("L0_ffn_")}
        phase_mamba(nc, x_res, ident, a, a["x"])
        phase_ffn(nc, x_res, ident, f, "f1_")
        phase_ssd(nc, x_res, ident, s)
        phase_ffn(nc, x_res, ident, f, "f2_")
        stored = ctx.enter_context(nc.semaphore("stored"))
        block = ctx.enter_context(nc.Block())

        @block.sync
        def _(sp):
            sp.dma_start(out.rearrange("b (t p) d -> p (b t) d", p=P), x_res[:]).then_inc(stored, 16)
            sp.wait_ge(stored, 16)


_TURNED = ("L0_attn_a_in_proj_w", "L0_attn_a_x_proj_w", "L0_attn_a_dt_proj_w", "L0_attn_a_out_proj_w")


def kernel(**inputs):
    import numpy as np
    import concourse.bacc as bacc
    from concourse import mybir as mb
    from concourse.bass_utils import run_bass_kernel_spmd

    nc = bacc.Bacc("TRN2", target_bir_lowering=False, num_devices=1)
    arrays, aps = {}, {}
    for name, value in inputs.items():
        a = np.asarray(value)
        a = np.ascontiguousarray(a.T if name in _TURNED else a)
        arrays["in_" + name] = a
        aps[name] = nc.dram_tensor("in_" + name, a.shape, mb.dt.from_np(a.dtype), kind="ExternalInput").ap()
    out = nc.dram_tensor("out_x", (NB, T, D), F32, kind="ExternalOutput").ap()
    hybrid_block(nc, aps, out)
    r = run_bass_kernel_spmd(nc, [arrays], core_ids=[0])
    return r.results[0]["out_x"]
```

```python
from contextlib import ExitStack

import concourse.bass as bass
import numpy as np
from concourse import mybir

F32 = mybir.dt.float32
BF16 = mybir.dt.bfloat16
ALU = mybir.AluOpType
ACT = mybir.ActivationFunctionType
AX = mybir.AxisListType.X

P = 128
NB = 4
T = 512
D = 256
KD = D // P
TB = T // P
NT = NB * TB
LN_EPS = 1e-5


class Chain:

    def __init__(self, eng, sem, per):
        self.eng, self.sem, self.per, self.base, self.k = eng, sem, per, 0, 0

    def begin(self, turn):
        self.base, self.k = turn * self.per, 0

    def link(self, ins):
        self.k += 1
        ins.then_inc(self.sem, 1)
        self.eng.wait_ge(self.sem, self.base + self.k)

    def end(self):
        assert self.k == self.per, (self.k, self.per)


def bc_last(ap, n):
    return ap.unsqueeze(len(ap.shape)).to_broadcast(list(ap.shape) + [n])


def bc_mid(ap, n):
    return ap.unsqueeze(1).to_broadcast([ap.shape[0], n] + list(ap.shape[1:]))


def phase_mamba(nc, x_res, ident, w, x_dram, load_later, bias):
    NS, R = 16, 64
    CT = 4
    HT, XC, CV, DBC, DT, NF = 0, 2, 4, 7, 8, 11
    Z = (6, 10)
    with ExitStack() as ctx:
        def sb(name, shape, dt=F32):
            return ctx.enter_context(nc.sbuf_tensor("m_" + name, shape, dt))

        def ps(name, shape):
            return ctx.enter_context(nc.psum_tensor("m_" + name, shape, F32))

        def sem(name):
            return ctx.enter_context(nc.semaphore("m_" + name))

        w_in = sb("w_in", [P, KD, 2 * D])
        w_conv = sb("w_conv", [P, CT, KD, D])
        w_xp = sb("w_xp", [P, KD, R + 2 * NS])
        w_dt = sb("w_dt", [R, D])
        w_out = sb("w_out", [P, KD, D])
        norm_w = sb("norm_w", [P, KD])
        conv_b = sb("conv_b", [P, KD])
        dt_b = sb("dt_b", [P, KD])
        d_skip = sb("d_skip", [P, KD])
        a_log = sb("a_log", [P, KD, NS])
        a_exp = sb("a_exp", [P, KD, NS])
        a_neg = sb("a_neg", [P, KD, NS])
        sel = sb("sel", [3 * 2 * NS, 2 * NS, P], BF16)

        stats = sb("stats", [P, TB, 6])
        scrap = sb("scrap", [P, 1])
        mv = sb("mv", [P, TB, 2])
        rstd = sb("rstd", [P, TB])
        var = sb("var", [P, TB])
        ms = sb("ms", [P, TB])
        half = sb("half", [P, TB])
        eps = sb("eps", [P, TB])
        r2 = sb("r2", [P, TB])
        xn = sb("xn", [P, TB, D])
        h = sb("h", [P, TB, D])
        hT = sb("hT", [P, KD, T])
        xc = sb("xc", [P, KD, T + CT - 1])
        dlow = sb("dlow", [R, T])
        rest = sb("rest", [2 * 2 * NS, T])
        sp_in = sb("sp_in", [P, KD, T])
        sp_e = sb("sp_e", [P, KD, T])
        sp_l = sb("sp_l", [P, KD, T])
        sz = sb("sz", [P, 2, KD, T])
        xs = sb("xs", [P, 2, KD, T])
        delta = sb("delta", [P, 2, KD, T])
        u = sb("u", [P, 2, KD, T])
        bc3 = sb("bc3", [3 * 2 * NS, 2, T], BF16)
        dA = sb("dA", [P, 3, KD, T])
        bx = sb("bx", [P, 2, KD, T])
        hs = sb("hs", [P, 2, KD, T])
        hc = sb("hc", [P, 3, KD, T])
        y2 = sb("y2", [P, KD, T])
        g = sb("g", [P, KD, T])

        bias.whole = sb("bias_whole", [33, bias.n])

        front = [ps(f"front{j}", [P, T]) for j in range(2)]
        yps = ps("yps", [P, KD, T])
        Bps = ps("Bps", [P, 2, T])
        Cps = ps("Cps", [P, 2, T])

        s_x0 = sem("x0_loaded")
        s_x = sem("x_loaded")
        s_wn = sem("norm_w_loaded")
        s_wi = sem("in_proj_loaded")
        s_wc = sem("conv_loaded")
        s_wx = sem("x_proj_loaded")
        s_wd = sem("dt_proj_loaded")
        s_wa = sem("a_log_loaded")
        s_wo = sem("out_proj_loaded")
        s_bs = sem("bias_step")
        s_pool = sem("pool_step")
        s_id = sem("ident_ready")
        s_pad = sem("conv_pad_ready")
        s_sel = sem("selectors_ready")
        s_ae = sem("a_exp_ready")
        s_a = sem("a_ready")
        s_vf = sem("vector_front_step")
        s_pf = sem("pool_front_step")
        s_half = sem("half_ready")
        s_var = sem("var_ready")
        s_r2 = sem("r2_ready")
        s_xn = sem("xn_ready")
        s_h = sem("h_ready")
        s_res = sem("residual_added")
        s_full = sem("front_full")
        s_hT = sem("hT_ready")
        s_xc = sem("xc_ready")
        s_sz = sem("sz_ready")
        s_xs = sem("xs_ready")
        s_dlow = sem("dlow_ready")
        s_bc3 = sem("bc3_ready")
        s_spin = sem("sp_in_ready")
        s_spe = sem("sp_e_ready")
        s_spl = sem("sp_l_ready")
        s_delta = sem("delta_ready")
        s_u = sem("u_ready")
        s_B = sem("B_full")
        s_C = sem("C_full")
        s_bx = sem("bx_ready")
        s_dA = sem("dA_ready")
        s_scan = sem("scan_done")
        s_hc = sem("hc_ready")
        s_hcu = sem("hc_used")
        s_y2 = sem("y2_ready")
        s_g = sem("g_ready")
        s_o = sem("out_full")
        s_xo = sem("x_updated")

        block = ctx.enter_context(nc.Block())

        def full(b, use):
            return b * NF + use + 1

        def is_first(b):
            return isinstance(b, int) and b == 0

        def is_second(b):
            return isinstance(b, int) and b == 1

        @block.sync
        def _(sp):
            xv = x_dram.rearrange("b (t p) d -> b p t d", p=P)
            sp.dma_start(x_res[:, 0:TB, :], xv[0]).then_inc(s_x0, 16)

            def column(dst, src, sem):
                sp.dma_start(dst[:], src.rearrange("(k p) -> p k", p=P),
                             allow_slow_non_contiguous=True).then_inc(sem, 16)

            def rows(dst, src, sem):
                sp.dma_start(dst[:], src.rearrange("(k p) n -> p k n", p=P)).then_inc(sem, 16)

            column(norm_w, w["norm_w"], s_wn)
            rows(w_in, w["in_proj_w"], s_wi)
            sp.dma_start(w_conv[:], w["conv_w"].rearrange("j (k p) n -> p j k n", p=P)).then_inc(s_wc, 16)
            column(conv_b, w["conv_b"], s_wc)
            rows(w_xp, w["x_proj_w"], s_wx)
            sp.dma_start(w_dt[:], w["dt_proj_w"]).then_inc(s_wd, 16)
            column(dt_b, w["dt_proj_b"], s_wd)
            rows(a_log, w["A_log"], s_wa)
            column(d_skip, w["D"], s_wa)
            for b in range(1, NB):
                sp.dma_start(x_res[:, b * TB:(b + 1) * TB, :], xv[b]).then_inc(s_x, 16)
            rows(w_out, w["out_proj_w"], s_wo)
            bias.load(sp)
            load_later(sp)

        @block.gpsimd
        def _(pool):
            chain = Chain(pool, s_pool, 4)
            nc.gpsimd.memset(half[:], -0.5).then_inc(s_half, 1)
            nc.gpsimd.memset(eps[:], LN_EPS).then_inc(s_half, 1)
            pool.wait_ge(s_half, 2)
            chain.link(nc.gpsimd.memset(ident[:], 0.0))
            nc.gpsimd.affine_select(out=ident[:], in_=ident[:], compare_op=ALU.not_equal, fill=1.0, base=0,
                                    pattern=[[-1, P]], channel_multiplier=1).then_inc(s_id, 1)
            nc.gpsimd.memset(xc[:, :, 0:CT - 1], 0.0).then_inc(s_pad, 1)
            pool_chain = Chain(pool, s_pf, 6)

            def scales(b):
                pool_chain.begin(b)
                pool.wait_ge(s_var, b + 1)
                if not is_first(b):
                    pool.wait_ge(s_h, b)
                pool_chain.link(nc.gpsimd.tensor_tensor(ms[:], var[:], eps[:], ALU.add))
                pool_chain.link(nc.gpsimd.tensor_tensor(rstd[:], ms[:], half[:], ALU.pow))
                pool_chain.link(nc.gpsimd.tensor_tensor(ms[:], var[:], rstd[:], ALU.mult))
                pool_chain.link(nc.gpsimd.tensor_tensor(ms[:], ms[:], rstd[:], ALU.mult))
                pool_chain.link(nc.gpsimd.tensor_tensor(ms[:], ms[:], eps[:], ALU.add))
                pool_chain.link(nc.gpsimd.tensor_tensor(r2[:], ms[:], half[:], ALU.pow))
                nc.gpsimd.tensor_tensor(r2[:], r2[:], rstd[:], ALU.mult).then_inc(s_r2, 1)
                pool_chain.end()

            def residual(b, rows):
                pool.wait_ge(s_xn, b + 1)
                pool.wait_ge(s_h, b + 1)
                nc.gpsimd.tensor_tensor(rows, rows, xn[:], ALU.add).then_inc(s_res, 1)

            scales(0)
            residual(0, x_res[:, 0:TB, :])
            nc.gpsimd.memset(bias.parts[:], 0.0).then_inc(bias.ready, 1)
            chain.link(nc.gpsimd.memset(sel[:], 0.0))
            for part in range(3):
                ins = nc.gpsimd.affine_select(out=sel[:], in_=sel[:], compare_op=ALU.not_equal, fill=1.0,
                                              base=-2 * NS * part, pattern=[[-1, 2 * NS], [0, P]],
                                              channel_multiplier=1)
                if part < 2:
                    chain.link(ins)
            ins.then_inc(s_sel, 1)
            chain.end()
            with pool.Fori(1, NB) as b:
                scales(b)
                residual(b, x_res[:, bass.ds(TB * b, TB), :])

        @block.tensor
        def _(pe):
            def transposes(b):
                pe.wait_ge(s_h, b + 1)
                for k in range(KD):
                    if is_first(b):
                        pass
                    elif is_second(b):
                        pe.wait_ge(s_spin, b)
                        pe.wait_ge(s_sz, KD * b)
                    else:
                        pe.wait_ge(s_xo, KD * (b - 1))
                    for t in range(TB):
                        mm = nc.tensor.transpose(front[(HT + k) % 2][:, t * P:(t + 1) * P],
                                                 h[:, t, k * P:(k + 1) * P], ident[:])
                    mm.then_inc(s_full, 1)

            def in_proj(b, m, use, col, read, count):
                pe.wait_ge(s_hT, KD * (b + 1))
                pe.wait_ge(read, count)
                if is_first(b):
                    pe.wait_ge(s_wi, 16)
                for k in range(KD):
                    mm = nc.tensor.matmul(front[use % 2][:], w_in[:, k, (col + m) * P:(col + m + 1) * P],
                                          hT[:, k, :], start=(k == 0), stop=(k == KD - 1))
                mm.then_inc(s_full, 1)

            def conv(b, m, half):
                if half == 0:
                    pe.wait_ge(s_xc, KD * (b + 1))
                if is_first(b):
                    pe.wait_ge(s_wc, 32)
                for j in range(2 * half, 2 * half + 2):
                    for k in range(KD):
                        mm = nc.tensor.matmul(front[(CV + m) % 2][:], w_conv[:, j, k, m * P:(m + 1) * P],
                                              xc[:, k, j:j + T], start=(j == 0 and k == 0),
                                              stop=(j == CT - 1 and k == KD - 1))
                if half == 1:
                    mm.then_inc(s_full, 1)

            def x_proj(b):
                pe.wait_ge(s_xs, KD * (b + 1))
                if is_first(b):
                    pe.wait_ge(s_wx, 16)
                for k in range(KD):
                    mm = nc.tensor.matmul(front[DBC % 2][0:R + 2 * NS, :], w_xp[:, k, :], xs[:, b % 2, k, :],
                                          start=(k == 0), stop=(k == KD - 1))
                mm.then_inc(s_full, 1)

            def dt_proj(b):
                pe.wait_ge(s_dlow, b + 1)
                pe.wait_ge(s_sz, KD * b + 1)
                if is_first(b):
                    pe.wait_ge(s_wd, 32)
                for m in range(KD):
                    if m == 1:
                        pe.wait_ge(s_bc3, b + 1)
                    nc.tensor.matmul(front[(DT + m) % 2][:], w_dt[:, m * P:(m + 1) * P], dlow[:], start=True,
                                     stop=True).then_inc(s_full, 1)

            pieces = {3: transposes,
                      4: lambda b: in_proj(b, 0, XC, 0, s_hT, KD * b + 1),
                      5: lambda b: in_proj(b, 1, XC + 1, 0, s_hT, KD * b + 2),
                      6: lambda b: conv(b, 0, 0), 7: lambda b: conv(b, 0, 1),
                      8: lambda b: conv(b, 1, 0), 9: lambda b: conv(b, 1, 1),
                      10: lambda b: in_proj(b, 0, Z[0], KD, s_xs, KD * b + 1), 11: x_proj, 13: dt_proj,
                      14: lambda b: in_proj(b, 1, Z[1], KD, s_spin, b + 1)}

            def broadcast_B(b, n):
                step = NS * b + n
                if not (is_first(b) and n < 2):
                    pe.wait_ge(s_bx, step - 1)
                nc.tensor.matmul(Bps[:, n % 2, :], sel[:, n, :], bc3[:, b % 2, :], start=True,
                                 stop=True).then_inc(s_B, 1)

            def broadcast_C(b, n):
                step = NS * b + n
                if not (is_first(b) and n < 2):
                    pe.wait_ge(s_hc, step - 1)
                nc.tensor.matmul(Cps[:, n % 2, :], sel[:, NS + n, :], bc3[:, b % 2, :], start=True,
                                 stop=True).then_inc(s_C, 1)

            def accumulate(b, n):
                step = NS * b + n
                pe.wait_ge(s_hc, step + 1)
                if n == 0 and not is_first(b):
                    pe.wait_ge(s_y2, b)
                for m in range(KD):
                    mm = nc.tensor.matmul(yps[:, m, :], ident[:], hc[:, (step % 3), m, :], start=(n == 0),
                                          stop=(n == NS - 1))
                mm.then_inc(s_hcu, 1)

            def out_proj(b, fronts):
                pe.wait_ge(s_g, b + 1)
                pe.wait_ge(s_spin, fronts)
                pe.wait_ge(s_sz, KD * fronts)
                for j in range(KD):
                    for t in range(2 * j, 2 * j + 2):
                        for k in range(KD):
                            mm = nc.tensor.matmul(front[1 - j][:, (t % 2) * D:(t % 2 + 1) * D],
                                                  g[:, k, t * P:(t + 1) * P], w_out[:, k, :],
                                                  start=(k == 0), stop=(k == KD - 1))
                    mm.then_inc(s_o, 1)

            def sequence(b, ahead):
                for n in range(NS):
                    if n + 2 < NS:
                        broadcast_B(b, n + 2)
                    elif ahead:
                        if n + 2 == NS:
                            pe.wait_ge(s_bc3, b + 2)
                        broadcast_B(b + 1, n + 2 - NS)
                    if n + 1 < NS:
                        broadcast_C(b, n + 1)
                    elif ahead:
                        broadcast_C(b + 1, 0)
                    if n >= 1:
                        accumulate(b, n - 1)
                    elif not is_first(b):
                        accumulate(b - 1, NS - 1)
                    if n == 1 and not is_first(b):
                        out_proj(b - 1, b + 1)
                    if ahead and n in pieces:
                        pieces[n](b + 1)
                if not ahead:
                    accumulate(b, NS - 1)
                    out_proj(b, NB)

            pe.wait_ge(s_id, 1)
            pe.wait_ge(s_pad, 1)
            for piece in pieces.values():
                piece(0)
            pe.wait_ge(s_sel, 1)
            broadcast_B(0, 0)
            broadcast_B(0, 1)
            broadcast_C(0, 0)
            pe.wait_ge(s_wo, 16)
            sequence(0, True)
            with pe.Fori(1, NB - 1) as b:
                sequence(b, True)
            sequence(NB - 1, False)

        @block.scalar
        def _(act):
            def take_hT(b):
                if is_first(b):
                    act.wait_ge(s_wn, 16)
                for k in range(KD):
                    act.wait_ge(s_full, full(b, HT + k))
                    nc.scalar.activation(hT[:, k, :], front[(HT + k) % 2][:], ACT.Copy,
                                         scale=norm_w[:, k:k + 1]).then_inc(s_hT, 1)

            def take_xc(b, k):
                act.wait_ge(s_full, full(b, XC + k))
                nc.scalar.activation(xc[:, k, CT - 1:], front[(XC + k) % 2][:], ACT.Copy).then_inc(s_xc, 1)

            def take_z(b, k):
                act.wait_ge(s_full, full(b, Z[k]))
                nc.scalar.activation(sz[:, b % 2, k, :], front[Z[k] % 2][:], ACT.Silu).then_inc(s_sz, 1)

            def take_conv(b, k):
                if is_first(b):
                    act.wait_ge(s_wc, 32)
                act.wait_ge(s_full, full(b, CV + k))
                nc.scalar.activation(xs[:, b % 2, k, :], front[(CV + k) % 2][:], ACT.Silu,
                                     bias=conv_b[:, k:k + 1]).then_inc(s_xs, 1)

            def take_dlow(b):
                act.wait_ge(s_full, full(b, DBC))
                nc.scalar.activation(dlow[:], front[DBC % 2][0:R, :], ACT.Copy).then_inc(s_dlow, 1)

            def softplus(b):
                act.wait_ge(s_spin, b + 1)
                nc.scalar.activation(sp_e[:], sp_in[:], ACT.Exp).then_inc(s_spe, 1)
                act.wait_ge(s_spe, b + 1)
                nc.scalar.activation(sp_l[:], sp_e[:], ACT.Ln, bias=1.0).then_inc(s_spl, 1)

            pieces = {5: take_hT, 6: lambda b: take_xc(b, 0), 7: lambda b: take_xc(b, 1),
                      9: lambda b: take_conv(b, 0), 11: lambda b: (take_conv(b, 1), take_z(b, 0)),
                      13: take_dlow, 15: softplus}

            def sequence(b, ahead):
                for n in range(NS):
                    step = NS * b + n
                    if n == 0:
                        act.wait_ge(s_delta, b + 1)
                    if not (is_first(b) and n < 3):
                        act.wait_ge(s_scan, step - 2)
                    for m in range(KD):
                        ins = nc.scalar.activation(dA[:, step % 3, m, :], delta[:, b % 2, m, :], ACT.Exp,
                                                   scale=a_neg[:, m, n:n + 1])
                    ins.then_inc(s_dA, 1)
                    if n == 1:
                        take_z(b, 1)
                    if ahead and n in pieces:
                        pieces[n](b + 1)

            for piece in pieces.values():
                piece(0)
            act.wait_ge(s_wa, 32)
            nc.scalar.activation(a_exp[:], a_log[:], ACT.Exp).then_inc(s_ae, 1)
            act.wait_ge(s_a, 1)
            sequence(0, True)
            with act.Fori(1, NB - 1) as b:
                sequence(b, True)
            sequence(NB - 1, False)

        @block.vector
        def _(dve):
            chain = Chain(dve, s_vf, 6)

            def statistics(b):
                chain.begin(b)
                dve.wait_ge(s_x0 if is_first(b) else s_x, 16 if is_first(b) else 16 * (NB - 1))
                if not is_first(b):
                    dve.wait_ge(s_h, b)
                for t in range(TB):
                    ins = nc.vector.bn_stats(stats[:, t, :], x_res[:, TB * b + t, :])
                    chain.link(ins) if t == TB - 1 else None
                nc.vector.memset(scrap[:], 0.0)
                for t in range(TB):
                    ins = nc.vector.bn_aggr(mv[:, t, :], stats[:, t, :])
                chain.link(ins)
                nc.vector.tensor_copy(var[:], mv[:, :, 1]).then_inc(s_var, 1)

            def normalise(b):
                dve.wait_ge(s_r2, b + 1)
                if not is_first(b):
                    dve.wait_ge(s_res, b)
                for t in range(TB):
                    ins = nc.vector.tensor_scalar(xn[:, t, :], x_res[:, TB * b + t, :], mv[:, t, 0:1],
                                                  rstd[:, t:t + 1], ALU.subtract, ALU.mult)
                ins.then_inc(s_xn, 1)
                if not is_first(b):
                    dve.wait_ge(s_full, full(b - 1, HT + KD - 1))
                for t in range(TB):
                    ins = nc.vector.tensor_scalar(h[:, t, :], x_res[:, TB * b + t, :], mv[:, t, 0:1],
                                                  r2[:, t:t + 1], ALU.subtract, ALU.mult)
                ins.then_inc(s_h, 1)

            def split_bc(b):
                dve.wait_ge(s_full, full(b, DBC))
                n = 2 * NS
                src = front[DBC % 2][R:R + n, :]
                chain.link(nc.vector.tensor_copy(bc3[0:n, b % 2, :], src))
                chain.link(nc.vector.tensor_tensor(rest[n:2 * n, :], src, bc3[0:n, b % 2, :], ALU.subtract))
                chain.link(nc.vector.tensor_copy(bc3[n:2 * n, b % 2, :], rest[n:2 * n, :]))
                nc.vector.tensor_tensor(bc3[2 * n:3 * n, b % 2, :], rest[n:2 * n, :], bc3[n:2 * n, b % 2, :],
                                        ALU.subtract).then_inc(s_bc3, 1)

            def softplus_in(b):
                if is_first(b):
                    dve.wait_ge(s_wd, 32)
                for m in range(KD):
                    dve.wait_ge(s_full, full(b, DT + m))
                    ins = nc.vector.tensor_scalar(delta[:, b % 2, m, :], front[(DT + m) % 2][:], dt_b[:, m:m + 1],
                                                  None, ALU.add)
                chain.link(ins)
                nc.vector.tensor_scalar(sp_in[:], delta[:, b % 2], 30.0, None, ALU.min).then_inc(s_spin, 1)

            def step_size(b):
                dve.wait_ge(s_spl, b + 1)
                nc.vector.tensor_tensor(delta[:, b % 2], delta[:, b % 2], sp_l[:], ALU.max).then_inc(s_delta, 1)
                dve.wait_ge(s_delta, b + 1)
                dve.wait_ge(s_xs, KD * (b + 1))
                nc.vector.tensor_tensor(u[:, b % 2], delta[:, b % 2], xs[:, b % 2], ALU.mult).then_inc(s_u, 1)
                chain.end()

            pieces = {0: statistics, 2: normalise, 12: split_bc, 13: softplus_in}

            def inject(b, n):
                step = NS * b + n
                if n == 0:
                    dve.wait_ge(s_u, b + 1)
                dve.wait_ge(s_B, step + 1)
                nc.vector.tensor_tensor(bx[:, n % 2], u[:, b % 2], bc_mid(Bps[:, n % 2, :], KD),
                                        ALU.mult).then_inc(s_bx, 1)

            def gate(b):
                dve.wait_ge(s_hcu, NS * (b + 1))
                for m in range(KD):
                    ins = nc.vector.scalar_tensor_tensor(y2[:, m, :], xs[:, b % 2, m, :], d_skip[:, m:m + 1],
                                                         yps[:, m, :], ALU.mult, ALU.add)
                ins.then_inc(s_y2, 1)
                dve.wait_ge(s_y2, b + 1)
                dve.wait_ge(s_sz, KD * (b + 1))
                nc.vector.tensor_tensor(g[:], y2[:], sz[:, b % 2], ALU.mult).then_inc(s_g, 1)

            def add_output(b):
                dve.wait_ge(s_res, b + 1)
                for j in range(KD):
                    dve.wait_ge(s_o, KD * b + j + 1)
                    rows = x_res[:, bass.ds(TB * b + 2 * j, 2), :]
                    nc.vector.tensor_tensor(rows, rows, front[1 - j][:].rearrange("p (t d) -> p t d", t=2),
                                            ALU.add).then_inc(s_xo, 1)

            def sequence(b, ahead):
                for n in range(NS):
                    step = NS * b + n
                    dve.wait_ge(s_dA, step + 1)
                    dve.wait_ge(s_bx, step + 1)
                    for m in range(KD):
                        ins = nc.vector.tensor_tensor_scan(hs[:, n % 2, m, :], dA[:, step % 3, m, :],
                                                           bx[:, n % 2, m, :], 0.0, ALU.mult, ALU.add)
                    ins.then_inc(s_scan, 1)
                    if n + 1 < NS:
                        inject(b, n + 1)
                    elif ahead:
                        step_size(b + 1)
                        inject(b + 1, 0)
                    dve.wait_ge(s_C, step + 1)
                    dve.wait_ge(s_scan, step + 1)
                    if not (is_first(b) and n < 3):
                        dve.wait_ge(s_hcu, step - 2)
                    nc.vector.tensor_tensor(hc[:, step % 3], hs[:, n % 2], bc_mid(Cps[:, n % 2, :], KD),
                                            ALU.mult).then_inc(s_hc, 1)
                    if n == 0 and not is_first(b):
                        gate(b - 1)
                    if n == 2 and not is_first(b):
                        add_output(b - 1)
                    if ahead and n in pieces:
                        pieces[n](b + 1)
                if not ahead:
                    gate(b)
                    add_output(b)

            statistics(0)
            normalise(0)
            split_bias(nc, dve, bias, s_bs)
            split_bc(0)
            softplus_in(0)
            step_size(0)
            inject(0, 0)
            dve.wait_ge(s_ae, 1)
            nc.vector.tensor_scalar(a_neg[:], a_exp[:], -1.0, None, ALU.mult).then_inc(s_a, 1)
            dve.wait_ge(s_wa, 32)
            sequence(0, True)
            with dve.Fori(1, NB - 1) as b:
                sequence(b, True)
            sequence(NB - 1, False)

class FfnBiases:

    def __init__(self, nc, ctx, w):
        E = w["router_w"].shape[1]
        self.w, self.E = w, E
        self.PB, self.RB = E * D, E * D + D
        self.n = E * D + D + E
        self.parts = ctx.enter_context(nc.sbuf_tensor("bias_parts", [96, self.n], BF16))
        self.loaded = ctx.enter_context(nc.semaphore("biases_loaded"))
        self.ready = ctx.enter_context(nc.semaphore("bias_parts_cleared"))
        self.whole = None

    def load(self, sp):
        w, PB, RB = self.w, self.PB, self.RB
        sp.dma_start(self.whole[0:1, 0:PB], w["expert_b"].rearrange("e d -> (e d)").unsqueeze(0)).then_inc(self.loaded, 16)
        sp.dma_start(self.whole[0:1, PB:RB], w["proj_b"].unsqueeze(0)).then_inc(self.loaded, 16)
        sp.dma_start(self.whole[0:1, RB:], w["router_b"].unsqueeze(0)).then_inc(self.loaded, 16)


def split_bias(nc, dve, bias, step):
    whole, parts = bias.whole, bias.parts
    dve.wait_ge(bias.loaded, 48)
    dve.wait_ge(bias.ready, 1)
    nc.vector.tensor_copy(parts[0:1], whole[0:1]).then_inc(step, 1)
    dve.wait_ge(step, 1)
    nc.vector.tensor_tensor(whole[32:33], whole[0:1], parts[0:1], ALU.subtract).then_inc(step, 1)
    dve.wait_ge(step, 2)
    nc.vector.tensor_copy(parts[32:33], whole[32:33]).then_inc(step, 1)
    dve.wait_ge(step, 3)
    nc.vector.tensor_tensor(parts[64:65], whole[32:33], parts[32:33], ALU.subtract)


class FfnSignals:
    EB = 2

    def __init__(self, nc, ctx, w):
        E = w["router_w"].shape[1]
        self.experts = [ctx.enter_context(nc.semaphore(f"experts_{j}_loaded")) for j in range(E // self.EB)]
        self.router = ctx.enter_context(nc.semaphore("router_loaded"))
        self.proj = ctx.enter_context(nc.semaphore("proj_loaded"))
        self.norm = ctx.enter_context(nc.semaphore("norm_loaded"))


class FfnWeights:

    def __init__(self, nc, ctx, w, signals, turn):
        E = w["router_w"].shape[1]
        self.w, self.signals, self.turn = w, signals, turn

        def sb(name, shape):
            return ctx.enter_context(nc.sbuf_tensor(f"f{turn}_{name}", shape, F32))

        self.w_e = sb("w_e", [P, KD, E, D])
        self.w_r = sb("w_r", [P, KD, E])
        self.w_p = sb("w_p", [P, KD, D])
        self.norm_w = sb("norm_w", [P, D])

    def load(self, sp):
        w, signals, EB = self.w, self.signals, self.signals.EB
        sp.dma_start(self.w_r[:], w["router_w"].rearrange("(k p) e -> p k e", p=P)).then_inc(signals.router, 16)
        for j, loaded in enumerate(signals.experts):
            for k in range(KD):
                sp.dma_start(self.w_e[:, k, EB * j:EB * (j + 1)],
                             w["expert_w"].rearrange("e (k p) n -> k p e n", p=P)[k, :, EB * j:EB * (j + 1)]
                             ).then_inc(loaded, 16)
        sp.dma_start(self.w_p[:], w["proj_w"].rearrange("(k p) n -> p k n", p=P)).then_inc(signals.proj, 16)
        sp.dma_start(self.norm_w[:], w["norm_w"].partition_broadcast(P)).then_inc(signals.norm, 16)


def phase_ffn(nc, x_res, ident, bias, weights, load_now, tag):
    RMS_EPS = 1e-6
    E, EB = bias.E, weights.signals.EB
    signals, LOADED = weights.signals, 16 * weights.turn
    NBANK = E // EB
    PB, RB, bias3 = bias.PB, bias.RB, bias.parts
    w_e, w_r, w_p, norm_w = weights.w_e, weights.w_r, weights.w_p, weights.norm_w
    with ExitStack() as ctx:
        def sb(name, shape, dt=F32):
            return ctx.enter_context(nc.sbuf_tensor(tag + name, shape, dt))

        def ps(name, shape):
            return ctx.enter_context(nc.psum_tensor(tag + name, shape, F32))

        def sem(name):
            return ctx.enter_context(nc.semaphore(tag + name))

        ones = sb("ones", [96, P], BF16)
        before = sb("before", [P, E, E])
        half = sb("half", [P, TB])
        eps = sb("eps", [P, TB])
        rms_eps = sb("rms_eps", [P, 1])
        per_d = sb("per_d", [P, 1])

        stats = sb("stats", [P, TB, 6])
        scrap = sb("scrap", [P, 1])
        mv = sb("mv", [P, TB, 2])
        ve = sb("ve", [P, TB])
        rstd = sb("rstd", [P, TB])
        z = sb("z", [P, TB, D])
        zT = sb("zT", [P, 2, KD, P])
        lg = sb("lg", [P, 2, E])
        above = sb("above", [P, E, E])
        equal = sb("equal", [P, E, E])
        rank = sb("rank", [P, 2, E])
        picked = sb("picked", [P, E])
        mid = sb("mid", [P, 2])
        th = sb("th", [P, 2, E])
        wt = sb("wt", [P, E])
        gate = sb("gate", [P, 2, E])
        s = sb("s", [P, 2, E, D])
        acc = sb("acc", [P, 2, D])
        cT = sb("cT", [P, 2, KD, P])
        y = sb("y", [P, 2, D])
        sq = sb("sq", [P, D])
        ss = sb("ss", [P, 2])
        ms = sb("ms", [P, 2])
        rr = sb("rr", [P, 2])
        o = sb("o", [P, 2, D])

        hps = ps("hps", [P, NBANK, EB * D])
        zps = ps("zps", [P, KD, P])
        rps = ps("rps", [P, 2, E])
        cps = ps("cps", [P, KD, P])
        ops = ps("ops", [P, D])

        s_const = sem("constants_ready")
        s_var = sem("var_ready")
        s_rstd = sem("rstd_ready")
        s_pool = sem("pool_step")
        s_z = sem("z_ready")
        s_zt = sem("z_turned")
        s_zT = sem("zT_ready")
        s_r = sem("logits_full")
        s_v = sem("vector_step")
        s_mid = sem("mid_ready")
        s_th = sem("tanh_ready")
        s_gate = sem("gate_ready")
        s_h = sem("experts_full")
        s_s = sem("silu_ready")
        s_acc = sem("combined_ready")
        s_ct = sem("combined_turned")
        s_cT = sem("cT_ready")
        s_o = sem("out_full")
        s_y = sem("y_ready")
        s_ss = sem("ss_ready")
        s_rr = sem("rr_ready")
        s_on = sem("o_ready")
        s_x = sem("x_updated")

        block = ctx.enter_context(nc.Block())

        def is_first(t):
            return isinstance(t, int) and t == 0

        @block.sync
        def _(sp):
            if load_now:
                weights.load(sp)

        @block.gpsimd
        def _(pool):
            nc.gpsimd.memset(half[:], -0.5).then_inc(s_const, 1)
            nc.gpsimd.memset(eps[:], LN_EPS).then_inc(s_const, 1)
            nc.gpsimd.memset(rms_eps[:], RMS_EPS).then_inc(s_const, 1)
            nc.gpsimd.memset(per_d[:], 1.0 / D).then_inc(s_const, 1)
            nc.gpsimd.memset(ones[:], 1.0).then_inc(s_const, 1)
            nc.gpsimd.memset(before[:], 1.0).then_inc(s_const, 1)
            pool.wait_ge(s_const, 6)
            nc.gpsimd.affine_select(out=before[:], in_=before[:], compare_op=ALU.is_gt, fill=0.0, base=0,
                                    pattern=[[1, E], [-1, E]], channel_multiplier=0).then_inc(s_const, 1)
            chain = Chain(pool, s_pool, 1 + 2 * TB)

            def scales(g):
                pool.wait_ge(s_var, g + 1)
                chain.link(nc.gpsimd.tensor_tensor(ve[:], mv[:, :, 1], eps[:], ALU.add))
                nc.gpsimd.tensor_tensor(rstd[:], ve[:], half[:], ALU.pow).then_inc(s_rstd, 1)

            def rms(tile, q):
                pool.wait_ge(s_ss, tile + 1)
                chain.link(nc.gpsimd.tensor_tensor(ms[:, q:q + 1], ss[:, q:q + 1], per_d[:], ALU.mult))
                chain.link(nc.gpsimd.tensor_tensor(ms[:, q:q + 1], ms[:, q:q + 1], rms_eps[:], ALU.add))
                nc.gpsimd.tensor_tensor(rr[:, q:q + 1], ms[:, q:q + 1], half[:, 0:1], ALU.pow).then_inc(s_rr, 1)

            def group(g, ahead):
                chain.begin(g)
                chain.base = 1 if is_first(g) else chain.base - 1
                for t in range(TB):
                    rms(TB * g + t - 1, (t - 1) % 2) if not (is_first(g) and t == 0) else None
                    if t == TB - 2 and ahead:
                        scales(g + 1)
                if not ahead:
                    rms(TB * g + t, t % 2)

            chain.begin(0)
            scales(0)
            group(0, True)
            with pool.Fori(1, NB - 1) as g:
                group(g, True)
            group(NB - 1, False)

        @block.tensor
        def _(pe):
            def turn_z(tile, q):
                pe.wait_ge(s_z, tile + 1)
                if not is_first(tile):
                    pe.wait_ge(s_zT, tile)
                for k in range(KD):
                    mm = nc.tensor.transpose(zps[:, k, :], z[:, q, k * P:(k + 1) * P], ident[:])
                mm.then_inc(s_zt, 1)

            def router(tile, q):
                pe.wait_ge(s_zT, tile + 1)
                if is_first(tile):
                    pe.wait_ge(signals.router, LOADED)
                for k in range(KD):
                    nc.tensor.matmul(rps[:, q, :], zT[:, q, k, :], w_r[:, k, :], start=(k == 0), stop=False)
                nc.tensor.matmul(rps[:, q, :], ones[:], bias3[:, RB:], start=False, stop=True).then_inc(s_r, 1)

            def experts(tile, q, j):
                if not is_first(tile):
                    pe.wait_ge(s_s, NBANK * tile + j - NBANK + 1)
                else:
                    pe.wait_ge(signals.experts[j], LOADED * KD)
                cols = slice(EB * D * j, EB * D * (j + 1))
                for k in range(KD):
                    nc.tensor.matmul(hps[:, j, :], zT[:, q, k, :],
                                     w_e[:, k, EB * j:EB * (j + 1), :].rearrange("p e n -> p (e n)"),
                                     start=(k == 0), stop=False)
                nc.tensor.matmul(hps[:, j, :], ones[:], bias3[:, cols], start=False, stop=True).then_inc(s_h, 1)

            def turn_combined(tile, q):
                pe.wait_ge(s_acc, tile + 1)
                for k in range(KD):
                    mm = nc.tensor.transpose(cps[:, k, :], acc[:, q, k * P:(k + 1) * P], ident[:])
                mm.then_inc(s_ct, 1)

            def project(tile, q):
                pe.wait_ge(s_cT, tile + 1)
                if not is_first(tile):
                    pe.wait_ge(s_y, tile)
                else:
                    pe.wait_ge(signals.proj, LOADED)
                for k in range(KD):
                    nc.tensor.matmul(ops[:], cT[:, q, k, :], w_p[:, k, :], start=(k == 0), stop=False)
                nc.tensor.matmul(ops[:], ones[:], bias3[:, PB:RB], start=False, stop=True).then_inc(s_o, 1)

            def group(g, last):
                for t in range(TB):
                    tile, q = TB * g + t, t % 2
                    started = not (is_first(g) and t == 0)
                    router(tile, q)
                    for j in range(NBANK):
                        experts(tile, q, j)
                        if j == 1 and not (last and t == TB - 1):
                            turn_z(tile + 1, (t + 1) % TB)
                        if j == 2 and started:
                            turn_combined(tile - 1, (t - 1) % 2)
                        if j == 3 and started:
                            project(tile - 1, (t - 1) % 2)
                if last:
                    turn_combined(tile, q)
                    project(tile, q)

            pe.wait_ge(s_const, 7)
            turn_z(0, 0)
            group(0, False)
            with pe.Fori(1, NB - 1) as g:
                group(g, False)
            group(NB - 1, True)

        @block.scalar
        def _(act):
            def take_zT(tile, q):
                act.wait_ge(s_zt, tile + 1)
                nc.scalar.activation(zT[:, q], zps[:], ACT.Copy).then_inc(s_zT, 1)

            def tanh(tile, q):
                act.wait_ge(s_mid, tile + 1)
                nc.scalar.activation(th[:, q, :], lg[:, q, :], ACT.Tanh, bias=mid[:, q:q + 1],
                                     scale=-2.0).then_inc(s_th, 1)

            def silu(tile, q, j):
                act.wait_ge(s_h, NBANK * tile + j + 1)
                if not (isinstance(tile, int) and tile < 2):
                    act.wait_ge(s_acc, tile - 1)
                nc.scalar.activation(s[:, q, EB * j:EB * (j + 1), :].rearrange("p e n -> p (e n)"),
                                     hps[:, j, :], ACT.Silu).then_inc(s_s, 1)

            def take_cT(tile, q):
                act.wait_ge(s_ct, tile + 1)
                nc.scalar.activation(cT[:, q], cps[:], ACT.Copy).then_inc(s_cT, 1)

            def square(tile, q):
                act.wait_ge(s_y, tile + 1)
                nc.scalar.activation(sq[:], y[:, q, :], ACT.Square, accum_out=ss[:, q:q + 1]).then_inc(s_ss, 1)

            def group(g, last):
                for t in range(TB):
                    tile, q = TB * g + t, t % 2
                    started = not (is_first(g) and t == 0)
                    for j in range(NBANK):
                        silu(tile, q, j)
                        if j == 0:
                            tanh(tile, q)
                        if j == 1 and not (last and t == TB - 1):
                            take_zT(tile + 1, (t + 1) % 2)
                        if j == 2 and started:
                            take_cT(tile - 1, (t - 1) % 2)
                    if started:
                        square(tile - 1, (t - 1) % 2)
                if last:
                    take_cT(tile, q)
                    square(tile, q)

            take_zT(0, 0)
            group(0, False)
            with act.Fori(1, NB - 1) as g:
                group(g, False)
            group(NB - 1, True)

        @block.vector
        def _(dve):
            chain = Chain(dve, s_v, TB * (5 + 1 + E - 1) + 1)

            def statistics(g):
                for t in range(TB):
                    ins = nc.vector.bn_stats(stats[:, t, :], x_res[:, TB * g + t, :])
                chain.link(ins)
                nc.vector.memset(scrap[:], 0.0)
                for t in range(TB):
                    ins = nc.vector.bn_aggr(mv[:, t, :], stats[:, t, :])
                ins.then_inc(s_var, 1)

            def normalise(tile, t, g):
                if t == 0:
                    dve.wait_ge(s_rstd, g + 1)
                nc.vector.tensor_scalar(z[:, t, :], x_res[:, tile, :], mv[:, t, 0:1], rstd[:, t:t + 1],
                                        ALU.subtract, ALU.mult).then_inc(s_z, 1)

            def route(tile, q):
                dve.wait_ge(s_r, tile + 1)
                chain.link(nc.vector.tensor_scalar(lg[:, q, :], rps[:, q, :], -0.5, None, ALU.mult))
                other, own = bc_mid(lg[:, q, :], E), bc_last(lg[:, q, :], E)
                nc.vector.tensor_tensor(above[:], other, own, ALU.is_lt)
                chain.link(nc.vector.tensor_tensor(equal[:], other, own, ALU.is_equal))
                chain.link(nc.vector.tensor_tensor(equal[:], equal[:], before[:], ALU.mult))
                chain.link(nc.vector.tensor_tensor(above[:], above[:], equal[:], ALU.add))
                chain.link(nc.vector.tensor_reduce(rank[:, q, :], above[:], AX, ALU.add))
                nc.vector.scalar_tensor_tensor(picked[:], rank[:, q, :], 2.0, lg[:, q, :], ALU.is_lt, ALU.mult,
                                               accum_out=mid[:, q:q + 1]).then_inc(s_mid, 1)

            def weigh(tile, q):
                dve.wait_ge(s_th, tile + 1)
                chain.link(nc.vector.tensor_scalar(wt[:], th[:, q, :], 0.5, 0.5, ALU.mult, ALU.add))
                nc.vector.scalar_tensor_tensor(gate[:, q, :], rank[:, q, :], 2.0, wt[:], ALU.is_lt,
                                               ALU.mult).then_inc(s_gate, 1)

            def combine(tile, q):
                if not (isinstance(tile, int) and tile < 2):
                    dve.wait_ge(s_ct, tile - 1)
                dve.wait_ge(s_gate, tile + 1)
                for e in range(E):
                    if e % EB == 0:
                        dve.wait_ge(s_s, NBANK * tile + e // EB + 1)
                    if e == 0:
                        ins = nc.vector.tensor_scalar(acc[:, q, :], s[:, q, e, :], gate[:, q, e:e + 1], None,
                                                      ALU.mult)
                    else:
                        ins = nc.vector.scalar_tensor_tensor(acc[:, q, :], s[:, q, e, :], gate[:, q, e:e + 1],
                                                             acc[:, q, :], ALU.mult, ALU.add)
                    if e < E - 1:
                        chain.link(ins)
                ins.then_inc(s_acc, 1)

            def add_input(tile, q, t):
                dve.wait_ge(s_o, tile + 1)
                nc.vector.tensor_tensor(y[:, q, :], ops[:], z[:, t, :], ALU.add).then_inc(s_y, 1)

            def finish(tile, q):
                dve.wait_ge(s_rr, tile + 1)
                if is_first(tile):
                    dve.wait_ge(signals.norm, LOADED)
                nc.vector.scalar_tensor_tensor(o[:, q, :], y[:, q, :], rr[:, q:q + 1], norm_w[:], ALU.mult,
                                               ALU.mult).then_inc(s_on, 1)
                dve.wait_ge(s_on, tile + 1)
                nc.vector.tensor_tensor(x_res[:, tile, :], x_res[:, tile, :], o[:, q, :], ALU.add).then_inc(s_x, 1)

            def group(g, last):
                chain.begin(g)
                chain.base = chain.base + 1
                for t in range(TB):
                    tile, q = TB * g + t, t % 2
                    started = not (is_first(g) and t == 0)
                    if not (last and t == TB - 1):
                        normalise(tile + 1, (t + 1) % TB, g + (t + 1) // TB)
                    if t == TB - 2 and not last:
                        statistics(g + 1)
                    route(tile, q)
                    if not (is_first(g) and t < 2):
                        finish(tile - 2, q)
                    weigh(tile, q)
                    combine(tile, q)
                    if started:
                        add_input(tile - 1, (t - 1) % 2, (t - 1) % TB)
                if last:
                    finish(tile - 1, (t - 1) % 2)
                    add_input(tile, q, t)
                    finish(tile, q)

            chain.begin(0)
            statistics(0)
            normalise(0, 0, 0)
            group(0, False)
            with dve.Fori(1, NB - 1) as g:
                group(g, False)
            group(NB - 1, True)


class SsdWeights:

    def __init__(self, nc, ctx, w):
        self.w = w
        H, DI, NS = w["A_log"].shape[0], w["W_out"].shape[0], w["B_norm_bias"].shape[1]
        self.w_in = ctx.enter_context(nc.sbuf_tensor("s_w_in", [P, KD, w["W_in"].shape[1]], F32))
        self.w_out = ctx.enter_context(nc.sbuf_tensor("s_w_out", [P, DI // P, D], F32))
        self.row = ctx.enter_context(nc.sbuf_tensor("s_row", [P, 2 * H + 2 * NS], F32))
        self.H, self.NS = H, NS
        self.loaded = ctx.enter_context(nc.semaphore("s_weights_loaded"))
        self.n_loads = 5 + KD

    def load(self, sp):
        w, row, H, NS, loaded = self.w, self.row, self.H, self.NS, self.loaded
        for n, name in enumerate(("A_log", "dt_bias")):
            sp.dma_start(row[:, n * H:(n + 1) * H], w[name].partition_broadcast(P)).then_inc(loaded, 16)
        for n, name in enumerate(("B_norm_bias", "C_norm_bias")):
            sp.dma_start(row[:, 2 * H + n * NS:2 * H + (n + 1) * NS],
                         w[name].rearrange("g n -> (g n)").partition_broadcast(P)).then_inc(loaded, 16)
        for k in range(KD):
            sp.dma_start(self.w_in[:, k], w["W_in"][k * P:(k + 1) * P, :]).then_inc(loaded, 16)
        sp.dma_start(self.w_out[:], w["W_out"].rearrange("(g p) n -> p g n", p=P)).then_inc(loaded, 16)


def phase_ssd(nc, x_res, ident, weights):
    w, w_in, w_out, row = weights.w, weights.w_in, weights.w_out, weights.row
    H = w["A_log"].shape[0]
    DI = w["W_out"].shape[0]
    HP = DI // H
    NS = w["B_norm_bias"].shape[1]
    NR = NS // 2
    Q = 32
    NC = P // Q
    NQ = P // Q
    HG = H // NQ
    NG = DI // P
    ST = NG
    REST = 2 * NS + 2 * H + NR
    BC, DT, LAM, TH = 0, 2 * NS, 2 * NS + H, 2 * NS + 2 * H
    RMS_EPS = 1e-6
    TWO_PI_HI, ROUND = 6.28125, 12582912.0
    TWO_PI_LO = 2 * np.pi - TWO_PI_HI
    with ExitStack() as ctx:
        def sb(name, shape, dt=F32):
            return ctx.enter_context(nc.sbuf_tensor("s_" + name, shape, dt))

        def ps(name, shape):
            return ctx.enter_context(nc.psum_tensor("s_" + name, shape, F32))

        def sem(name):
            return ctx.enter_context(nc.semaphore("s_" + name))

        a_exp = sb("a_exp", [P, H])
        a_neg = sb("a_neg", [P, H])
        nbias = row[:, 2 * H:]
        half_pi = sb("half_pi", [P, 1])
        half = sb("half", [P, 2 * TB])
        eps = sb("eps", [P, TB])
        rms_eps = sb("rms_eps", [P, 2 * TB])
        per_ns = sb("per_ns", [P, 2 * TB])
        ones = sb("ones", [P, P])
        tri = sb("tri", [P, P])
        tri_c = sb("tri_c", [P, NC, Q])
        after = sb("after", [P, NC, Q])
        shift = sb("shift", [P, P])
        carry = sb("carry", [P, P])
        rep = sb("rep", [H, DI])
        in_chunk = sb("in_chunk", [P, NC])
        mask_rs = sb("mask_rs", [P, Q])
        mask_st = sb("mask_st", [P, Q])

        stats = sb("stats", [P, TB, 6])
        scrap = sb("scrap", [P, 1])
        mv = sb("mv", [P, TB, 2])
        ve = sb("ve", [P, TB])
        rstd = sb("rstd", [P, TB])
        zn = sb("zn", [P, TB, D])
        zT = sb("zT", [P, KD, T])
        rest = sb("rest", [P, TB, REST])
        v = sb("v", [P, TB, H])
        vm = sb("vm", [P, TB, H])
        le = sb("le", [P, TB, H])
        dt = sb("dt", [P, TB, H])
        dtm = sb("dtm", [P, TB])
        th = sb("th", [P, TB, NR])
        pp = sb("pp", [P, TB, H])
        qq = v
        dA = sb("dA", [P, TB, H])
        dA2 = sb("dA2", [P, 2, TB, H])
        bsq = sb("bsq", [P, TB * 2, NS])
        bss = sb("bss", [P, TB * 2])
        bms = sb("bms", [P, TB * 2])
        brr = sb("brr", [P, TB * 2])
        bn = bsq[:].rearrange("p (t a) n -> p t a n", t=TB)
        kk = sb("kk", [P, TB, NR])
        arg = sb("arg", [P, TB, NR])
        aarg = kk
        sn = sb("sn", [P, TB, NR])
        cs = sb("cs", [P, TB, NR])
        rt = zn[:].rearrange("p t (i r) -> p (t i r)", r=NR).rearrange("p (k t a r) -> p k t a r", k=4, t=TB, a=2)
        br = sb("br", [P, TB, 2, NS])
        cbd = sb("cbd", [P, TB])
        bT = sb("bT", [P, T])
        cT = sb("cT", [P, 2, T])
        cbm = sb("cbm", [P, 2, T])
        bm = sb("bm", [P, 2, TB, NC, NS])
        gw = sb("gw", [P, 2, TB, H])
        ww = sb("ww", [P, 2, TB, H])
        dl = sb("dl", [P, 2, TB, H])
        xg = sb("xg", [P, 2, TB, DI])
        szT = sb("szT", [P, 2, NG, T])
        ecs = sb("ecs", [P, 2, NG, T])

        mst = sb("mst", [P, 2, H, Q])
        xbd = sb("xbd", [P, 2, NC, HG, NQ, HP])
        xw = sb("xw", [P, 2, DI])
        xdl = sb("xdl", [P, 2, DI])
        e = sb("e", [P, ST, NG, P])
        st = sb("st", [P, NG, 2 * NC, NS])
        pT = sb("pT", [P, NC // 2, DI])
        y = sb("y", [P, NG, P])
        y2 = sb("y2", [P, NG, P])
        strict = y2[:, 0, :].rearrange("p (c t) -> p c t", t=Q)
        gT = sb("gT", [P, NG, P])
        ms = sb("ms", [P, 1])
        rr = sb("rr", [P, 1])

        dps = ps("dps", [P, 2, NG, P])
        yps = ps("yps", [P, 2, NG, P])
        ops = ps("ops", [P, NG, P])
        sps = ps("sps", [P, 2, NC, NS])
        mps = ps("mps", [P, T])
        fps = ps("fps", [P, T])

        s_const = sem("constants_ready")
        s_mask = sem("masks_ready")
        s_ae = sem("a_exp_ready")
        s_var = sem("var_ready")
        s_pool = sem("pool_step")
        s_rstd = sem("rstd_ready")
        s_v = sem("vector_front_step")
        s_zn = sem("zn_ready")
        s_f = sem("front_full")
        s_zT = sem("zT_ready")
        s_rest = sem("rest_ready")
        s_vm = sem("vm_ready")
        s_act = sem("scalar_front_step")
        s_vl = sem("vl_ready")
        s_qq = sem("qq_ready")
        s_bss = sem("bss_ready")
        s_brr = sem("brr_ready")
        s_arg = sem("arg_ready")
        s_trig = sem("trig_ready")
        s_g = sem("g_ready")
        s_br = sem("br_ready")
        s_bT = sem("bT_ready")
        s_cbm = sem("cbm_ready")
        s_dcs = sem("dcs_ready")
        s_xg = sem("xg_ready")
        s_hcs = sem("head_decay_ready")
        s_sz = sem("sz_ready")
        s_ecs = sem("ecs_ready")
        s_front = sem("front_weights_ready")
        s_bm = sem("bm_ready")
        s_mst = sem("mst_ready")
        s_prep = sem("x_scaled")
        s_d = sem("d_full")
        s_e = sem("e_ready")
        s_em = sem("e_masked")
        s_Y = sem("y_added")
        s_S = sem("states_full")
        s_rs = sem("state_step")
        s_z0 = sem("state_cleared")
        s_pt = sem("prev_turned")
        s_pT = sem("prev_ready")
        s_yo = sem("y_off_full")
        s_t1 = sem("t1_ready")
        s_y = sem("y_ready")
        s_gT = sem("gT_ready")
        s_y2 = sem("y2_ready")
        s_tail = sem("tail_full")
        s_ms = sem("ms_ready")
        s_rr = sem("rr_ready")
        s_x = sem("x_updated")

        NCONST = 26
        ZT, RE, XP, CUM, QS, WC, BCT, CBT, HC, EC = 0, 2, 6, 11, 12, 13, 17, 18, 19, 20
        ZP = (10, 14, 15, 16)
        NF = 24
        was_read = ([(s_zT, KD, k + 1) for k in range(KD)] + [(s_rest, TB, t + 1) for t in range(TB)] +
                    [(s_xg, TB, t + 1) for t in range(TB)] + [(s_sz, NG, 1), (s_arg, 1, 1), (s_g, 1, 1), (s_dcs, 1, 1)] +
                    [(s_sz, NG, g + 1) for g in range(1, NG)] + [(s_bT, 4, 4), (s_cbm, 1, 1), (s_hcs, 1, 1)] +
                    [(s_ecs, NG, g + 1) for g in range(NG)])
        assert len(was_read) == NF
        block = ctx.enter_context(nc.Block())

        def is_first(n):
            return isinstance(n, int) and n == 0

        def full(b, use):
            return b * NF + use + 1

        def front(b, use):
            return mps if is_first(b) and use % 2 else fps

        def heads(ap, n=HP):
            return bc_last(ap, n)

        @block.gpsimd
        def _(pool):
            done = [0]

            def step(ins):
                done[0] += 1
                ins.then_inc(s_const, 1)

            def select(out, op, base, pattern, channel, fill=0.0):
                pool.wait_ge(s_const, done[0])
                step(nc.gpsimd.affine_select(out=out, in_=out, compare_op=op, fill=fill, base=base,
                                             pattern=pattern, channel_multiplier=channel))

            for tile_, value in ((half, -0.5), (eps, LN_EPS), (rms_eps, RMS_EPS), (per_ns, 1.0 / NS), (half_pi, np.pi / 2), (ones, 1.0),
                                 (tri, 1.0), (tri_c, 1.0), (after, 1.0), (shift, 0.0), (carry, 0.0),
                                 (in_chunk, 1.0), (xbd, 0.0), (rep, 1.0), (cT, 0.0)):
                step(nc.gpsimd.memset(tile_[:], float(value)))
            select(tri[:], ALU.is_ge, 0, [[1, P]], -1)
            select(tri_c[:], ALU.is_ge, 0, [[Q, NC], [1, Q]], -1)
            select(tri_c[:], ALU.is_ge, 0, [[-Q, NC], [0, Q]], 1)
            select(after[:], ALU.is_gt, 0, [[-Q, NC], [-1, Q]], 1)
            select(after[:], ALU.is_gt, Q, [[Q, NC], [0, Q]], -1)
            select(shift[:], ALU.not_equal, 1, [[1, P]], -1, 1.0)
            select(carry[:], ALU.not_equal, 1 - P, [[1, P]], P, 1.0)
            select(in_chunk[:], ALU.is_ge, 0, [[-Q, NC]], 1)
            select(in_chunk[:], ALU.is_ge, Q - 1, [[Q, NC]], -1)
            select(rep[:], ALU.is_ge, 0, [[1, DI]], -HP)
            select(rep[:], ALU.is_ge, HP - 1, [[-1, DI]], HP)
            chain = Chain(pool, s_pool, 3)

            def scales(b):
                chain.begin(b)
                pool.wait_ge(s_var, b + 1)
                chain.link(nc.gpsimd.tensor_tensor(ve[:], mv[:, :, 1], eps[:], ALU.add))
                nc.gpsimd.tensor_tensor(rstd[:], ve[:], half[:, 0:TB], ALU.pow).then_inc(s_rstd, 1)

            def bc_scales(b):
                pool.wait_ge(s_bss, b + 1)
                chain.link(nc.gpsimd.tensor_tensor(bms[:], bss[:], per_ns[:], ALU.mult))
                chain.link(nc.gpsimd.tensor_tensor(bms[:], bms[:], rms_eps[:], ALU.add))
                nc.gpsimd.tensor_tensor(brr[:], bms[:], half[:], ALU.pow).then_inc(s_brr, 1)

            def spread_b(b):
                pool.wait_ge(s_br, b + 1)
                for t in range(TB):
                    ins = nc.gpsimd.tensor_tensor(bm[:, b % 2, t], bc_mid(br[:, t, 0, :], NC),
                                                  bc_last(in_chunk[:], NS), ALU.mult)
                ins.then_inc(s_bm, 1)

            def decay_operand(b, t):
                tile = TB * b + t
                pool.wait_ge(s_qq, b + 1)
                if not (isinstance(tile, int) and tile < 2):
                    pool.wait_ge(s_d, ST * tile - ST)
                nc.gpsimd.tensor_tensor(mst[:, t % 2], bc_last(dA2[:, b % 2, t, :], Q), bc_mid(mask_rs[:], H),
                                        ALU.mult).then_inc(s_mst, 1)

            def rms(tile):
                pool.wait_ge(s_ms, tile + 1)
                nc.gpsimd.tensor_tensor(rr[:], ms[:], half[:, 0:1], ALU.pow).then_inc(s_rr, 1)

            def sequence(b, ahead):
                for t in range(TB):
                    tile = TB * b + t
                    if t > 1 or not is_first(b):
                        rms(tile - 2)
                    if t + 1 < TB:
                        decay_operand(b, t + 1)
                    if ahead and t == 0:
                        scales(b + 1)
                    if ahead and t == 1:
                        bc_scales(b + 1)
                    if ahead and t == 3:
                        spread_b(b + 1)
                        decay_operand(b + 1, 0)
                if not ahead:
                    rms(tile - 1)
                    rms(tile)

            assert done[0] == NCONST, done[0]
            pool.wait_ge(s_const, NCONST)
            pool.wait_ge(s_mask, 3)
            scales(0)
            bc_scales(0)
            spread_b(0)
            decay_operand(0, 0)
            sequence(0, True)
            with pool.Fori(1, NB - 1) as b:
                sequence(b, True)
            sequence(NB - 1, False)

        @block.tensor
        def _(pe):
            def claim(b, use):
                last = use - 2 if is_first(b) else use - 1
                if last >= 0:
                    read, per, count = was_read[last]
                    pe.wait_ge(read, per * b + count)
                elif not is_first(b):
                    pe.wait_ge(s_ecs, NG * b)
                return front(b, use)

            def turn_zn(b, k):
                pe.wait_ge(s_zn, b + 1)
                bank = claim(b, ZT + k)
                for t in range(TB):
                    mm = nc.tensor.transpose(bank[:, t * P:(t + 1) * P], zn[:, t, k * P:(k + 1) * P], ident[:])
                mm.then_inc(s_f, 1)

            def token_proj(b, t, use, cols):
                bank = claim(b, use)
                for k in range(KD):
                    mm = nc.tensor.matmul(bank[:, 0:cols.stop - cols.start], zT[:, k, t * P:(t + 1) * P],
                                          w_in[:, k, cols], start=(k == 0), stop=(k == KD - 1))
                mm.then_inc(s_f, 1)

            def project_rest(b, t):
                if t == 0:
                    pe.wait_ge(s_zT, KD * (b + 1))
                token_proj(b, t, RE + t, slice(2 * DI, 2 * DI + REST))

            def project_x(b, t):
                token_proj(b, t, XP + t, slice(DI, 2 * DI))

            def project_z(b, g):
                bank = claim(b, ZP[g])
                for k in range(KD):
                    mm = nc.tensor.matmul(bank[:], w_in[:, k, g * P:(g + 1) * P], zT[:, k, :],
                                          start=(k == 0), stop=(k == KD - 1))
                mm.then_inc(s_f, 1)

            def sum_angles(b):
                pe.wait_ge(s_qq, b + 1)
                cum = claim(b, CUM)[:, 0:TB * NR].rearrange("p (t n) -> p t n", t=TB)
                nc.tensor.matmul(cum, tri[:], th[:], start=True, stop=False, skip_group_check=True)
                for j in range(TB - 1):
                    mm = nc.tensor.matmul(cum[:, j + 1:, :], ones[:], bc_mid(th[:, j, :], TB - 1 - j),
                                          start=False, stop=(j == TB - 2), skip_group_check=True)
                mm.then_inc(s_f, 1)

            def next_token(b):
                nxt = claim(b, QS)[:, 0:TB * H].rearrange("p (t h) -> p t h", t=TB)
                nc.tensor.matmul(nxt, shift[:], qq[:], start=True, stop=False, skip_group_check=True)
                nc.tensor.matmul(nxt[:, 0:TB - 1, :], carry[:], qq[:, 1:TB, :], start=False, stop=True,
                                 skip_group_check=True).then_inc(s_f, 1)

            def following_decay(b):
                nc.tensor.matmul(claim(b, WC)[:, 0:TB * H], after[:].rearrange("p c t -> p (c t)"),
                                 dA[:].rearrange("p t h -> p (t h)"), start=True, stop=True).then_inc(s_f, 1)

            def turn_bc(b):
                pe.wait_ge(s_br, b + 1)
                bank = claim(b, BCT)
                for t in range(TB):
                    mm = nc.tensor.transpose(bank[:, t * P:(t + 1) * P], br[:, t].rearrange("p a n -> p (a n)"),
                                             ident[:])
                mm.then_inc(s_f, 1)

            def c_dot_b(b):
                pe.wait_ge(s_bT, 4 * (b + 1))
                bank = claim(b, CBT)
                for t in range(TB):
                    mm = nc.tensor.matmul(bank[:, t * P:(t + 1) * P], bT[:, t * P:(t + 1) * P],
                                          cT[:, b % 2, t * P:(t + 1) * P], start=(t == 0), stop=(t == TB - 1),
                                          skip_group_check=True)
                mm.then_inc(s_f, 1)

            def running_decay(b):
                bank = claim(b, HC)
                for t in range(TB):
                    mm = nc.tensor.matmul(bank[0:H, t * P:(t + 1) * P], dA[:, t, :],
                                          tri_c[:].rearrange("p c t -> p (c t)"), start=(t == 0),
                                          stop=(t == TB - 1), skip_group_check=True)
                mm.then_inc(s_f, 1)

            def spread_decay(b, g):
                if g == 0:
                    pe.wait_ge(s_hcs, b + 1)
                nc.tensor.matmul(claim(b, EC + g)[:], rep[:, g * P:(g + 1) * P], bT[0:H, :], start=True,
                                 stop=True).then_inc(s_f, 1)

            pieces = {(2, 0): lambda b: turn_zn(b, 0), (2, 1): lambda b: turn_zn(b, 1),
                      (3, 0): lambda b: project_rest(b, 0), (3, 1): lambda b: project_rest(b, 1),
                      (4, 0): lambda b: project_rest(b, 2), (4, 1): lambda b: project_rest(b, 3),
                      (5, 0): lambda b: project_x(b, 0), (5, 1): lambda b: project_x(b, 1),
                      (6, 1): lambda b: project_x(b, 2), (7, 0): lambda b: project_x(b, 3),
                      (7, 1): lambda b: project_z(b, 0), (8, 0): sum_angles, (8, 1): next_token,
                      (9, 0): following_decay, (9, 1): lambda b: project_z(b, 1),
                      (10, 0): lambda b: project_z(b, 2), (10, 1): lambda b: project_z(b, 3),
                      (12, 0): turn_bc, (12, 1): c_dot_b, (13, 0): running_decay,
                      (13, 1): lambda b: spread_decay(b, 0), (14, 0): lambda b: spread_decay(b, 1),
                      (14, 1): lambda b: spread_decay(b, 2), (15, 0): lambda b: spread_decay(b, 3)}

            def decays(tile, t, j):
                step = ST * tile + j
                if j == 0:
                    pe.wait_ge(s_mst, tile + 1)
                if not (isinstance(step, int) and step < 2):
                    pe.wait_ge(s_e, step - 1)
                for i in range(NG):
                    hg = NG * j + i
                    mm = nc.tensor.matmul(dps[:, j % 2, i, :],
                                          mst[:, t % 2, hg * NQ:(hg + 1) * NQ, :].rearrange("p h s -> p (h s)"),
                                          tri_c[:].rearrange("p c t -> p (c t)"), start=(i == 0),
                                          stop=(i == NG - 1), skip_group_check=True)
                mm.then_inc(s_d, 1)

            def own_token(tile, t):
                pe.wait_ge(s_prep, tile + 1)
                if not (isinstance(tile, int) and tile < 2):
                    pe.wait_ge(s_y, tile - 1)
                for g in range(NG):
                    nc.tensor.matmul(yps[:, t % 2, g, :], xdl[:, t % 2, g * P:(g + 1) * P], ident[:],
                                     start=(g == 0), stop=False, skip_group_check=True)

            def earlier_tokens(tile, t, j):
                pe.wait_ge(s_em, ST * tile + j + 1)
                for i in range(NG):
                    for c in range(NC):
                        mm = nc.tensor.matmul(yps[i * Q:(i + 1) * Q, t % 2, j, c * Q:(c + 1) * Q],
                                              xbd[:, t % 2, c, NG * j + i].rearrange("p h q -> p (h q)"),
                                              e[:, j, i, c * Q:(c + 1) * Q], start=False,
                                              stop=(j == ST - 1 and c == NC - 1), skip_group_check=True)
                mm.then_inc(s_Y, 1)

            def chunk_states(b, tile, t, pair):
                if pair == 0 and t == 0:
                    pe.wait_ge(s_bm, b + 1)
                if pair == 1 or not is_first(tile):
                    pe.wait_ge(s_rs, 2 * NC * (2 * tile + pair))
                for i in range(2):
                    g = 2 * pair + i
                    mm = nc.tensor.matmul(sps[:, i].rearrange("p c n -> p (c n)"), xw[:, t % 2, g * P:(g + 1) * P],
                                          bm[:, b % 2, t].rearrange("p c n -> p (c n)"), start=(i == 0),
                                          stop=(i == 1), skip_group_check=True)
                mm.then_inc(s_S, 1)

            def turn_prev(tile, t, pair):
                if pair == 0:
                    pe.wait_ge(s_rs, 4 * NC * (tile + 1))
                    if is_first(tile):
                        pe.wait_ge(s_ecs, NG)
                    if not (isinstance(tile, int) and tile < 2):
                        pe.wait_ge(s_x, tile - 1)
                elif not is_first(tile):
                    pe.wait_ge(s_t1, tile)
                out = (mps, ops[:].rearrange("p g t -> p (g t)"))[pair]
                slot = NC * (t % 2) + 2 * pair
                for g in range(NG):
                    mm = nc.tensor.transpose(out[:, g * P:(g + 1) * P],
                                             st[:, g, slot:slot + 2, :].rearrange("p c n -> p (c n)"), ident[:])
                mm.then_inc(s_pt, 1)

            def earlier_chunks(b, tile, t):
                pe.wait_ge(s_pT, 2 * (tile + 1))
                for g in range(NG):
                    for pair in range(2):
                        at, n = t * P + pair * 2 * Q, 2 * Q
                        mm = nc.tensor.matmul(ops[:, g, pair * n:(pair + 1) * n], pT[:, pair, g * P:(g + 1) * P],
                                              cT[:, b % 2, at:at + n], start=(g == 0 and pair == 0),
                                              stop=(g == NG - 1 and pair == 1), skip_group_check=True)
                mm.then_inc(s_yo, 1)

            def tail(tile):
                pe.wait_ge(s_y2, tile + 1)
                for g in range(NG):
                    nc.tensor.matmul(mps[:, D:D + 1], y2[:, g, :], ones[:, 0:1], start=(g == 0), stop=(g == NG - 1))
                pe.wait_ge(s_gT, tile + 1)
                for g in range(NG):
                    mm = nc.tensor.matmul(mps[:, 0:D], gT[:, g, :], w_out[:, g, :], start=(g == 0),
                                          stop=(g == NG - 1))
                mm.then_inc(s_tail, 1)

            def sequence(b, ahead):
                for t in range(TB):
                    tile = TB * b + t
                    started = not (is_first(b) and t == 0)
                    for j in range(ST):
                        piece = [pieces.get((ST * t + j, i)) if ahead else None for i in range(2)]
                        if j + 1 < ST:
                            decays(tile, t, j + 1)
                        elif t + 1 < TB or ahead:
                            decays(tile + 1, (t + 1) % TB, 0)
                        if j == 0:
                            own_token(tile, t)
                            chunk_states(b, tile, t, 0)
                            if started:
                                earlier_chunks(b if t else b - 1, tile - 1, (t - 1) % TB)
                        if j == 1:
                            chunk_states(b, tile, t, 1)
                        if j >= 2:
                            turn_prev(tile, t, j - 2)
                        if piece[0]:
                            piece[0](b + 1)
                        if j > 0:
                            earlier_tokens(tile, t, j - 1)
                        elif started:
                            earlier_tokens(tile - 1, (t - 1) % TB, ST - 1)
                        if j == 3 and started:
                            pe.wait_ge(s_pT, 2 * tile + 1)
                            tail(tile - 1)
                        if piece[1]:
                            piece[1](b + 1)
                if not ahead:
                    earlier_tokens(tile, t, ST - 1)
                    earlier_chunks(b, tile, t)
                    tail(tile)

            pe.wait_ge(weights.loaded, 16 * weights.n_loads)
            pe.wait_ge(s_const, NCONST)
            for piece in pieces.values():
                piece(0)
            decays(0, 0, 0)
            sequence(0, True)
            with pe.Fori(1, NB - 1) as b:
                sequence(b, True)
            sequence(NB - 1, False)

        @block.scalar
        def _(act):
            chain = Chain(act, s_act, 2)

            def take_zT(b, k):
                act.wait_ge(s_f, full(b, ZT + k))
                nc.scalar.activation(zT[:, k, :], front(b, ZT + k)[:], ACT.Copy).then_inc(s_zT, 1)

            def take_rest(b, t):
                act.wait_ge(s_f, full(b, RE + t))
                if t == 0 and not is_first(b):
                    act.wait_ge(s_trig, b)
                nc.scalar.activation(rest[:, t, :], front(b, RE + t)[:, 0:REST], ACT.Copy).then_inc(s_rest, 1)

            def exps(b):
                act.wait_ge(s_vm, b + 1)
                chain.link(nc.scalar.activation(vm[:], vm[:], ACT.Exp))
                nc.scalar.activation(vm[:], vm[:], ACT.Ln, bias=1.0).then_inc(s_vl, 1)

            def tanh(b):
                chain.begin(b)
                act.wait_ge(s_rest, TB * (b + 1))
                nc.scalar.activation(le[:], rest[:, :, LAM:LAM + H], ACT.Tanh, scale=0.5)

            def take_x(b, t):
                act.wait_ge(s_f, full(b, XP + t))
                nc.scalar.activation(xg[:, b % 2, t, :], front(b, XP + t)[:], ACT.Silu).then_inc(s_xg, 1)

            def trig(b):
                act.wait_ge(s_arg, b + 1)
                nc.scalar.activation(sn[:], arg[:], ACT.Sin)
                chain.link(nc.scalar.activation(aarg[:], arg[:], ACT.Abs))
                nc.scalar.activation(cs[:], aarg[:], ACT.Sin, bias=half_pi[:], scale=-1.0).then_inc(s_trig, 1)

            def chunk_decay(b):
                act.wait_ge(s_f, full(b, WC))
                nc.scalar.activation(ww[:, b % 2].rearrange("p t h -> p (t h)"), front(b, WC)[:, 0:TB * H],
                                     ACT.Exp).then_inc(s_dcs, 1)

            def take_z(b, g):
                act.wait_ge(s_f, full(b, ZP[g]))
                nc.scalar.activation(szT[:, b % 2, g, :], front(b, ZP[g])[:], ACT.Silu).then_inc(s_sz, 1)

            def take_bc(b):
                act.wait_ge(s_f, full(b, BCT))
                bank = front(b, BCT)
                for i in range(2):
                    half_ = slice(i * NS, (i + 1) * NS)
                    nc.scalar.activation(bT[half_, :], bank[0:NS, :], ACT.Copy).then_inc(s_bT, 1)
                    nc.scalar.activation(cT[half_, b % 2, :].rearrange("p (c i t) -> p c i t", i=2, t=Q)[:, :, i],
                                         bank[NS:2 * NS, :].rearrange("p (c i t) -> p c i t", i=2, t=Q)[:, :, i],
                                         ACT.Copy).then_inc(s_bT, 1)

            def take_head_decay(b):
                act.wait_ge(s_f, full(b, HC))
                nc.scalar.activation(bT[0:H, :], front(b, HC)[0:H, :], ACT.Exp).then_inc(s_hcs, 1)

            def take_decay(b, g):
                act.wait_ge(s_f, full(b, EC + g))
                nc.scalar.activation(ecs[:, b % 2, g, :], front(b, EC + g)[:], ACT.Copy).then_inc(s_ecs, 1)

            pieces = {(2, 0): lambda b: take_zT(b, 0), (2, 1): lambda b: take_zT(b, 1),
                      (3, 0): lambda b: take_rest(b, 0), (3, 1): lambda b: take_rest(b, 1),
                      (4, 0): lambda b: take_rest(b, 2), (4, 1): lambda b: take_rest(b, 3),
                      (5, 0): lambda b: (tanh(b), take_x(b, 0)), (5, 1): lambda b: take_x(b, 1),
                      (6, 0): exps, (6, 1): lambda b: take_x(b, 2), (7, 0): lambda b: take_x(b, 3),
                      (7, 1): lambda b: take_z(b, 0), (9, 0): chunk_decay,
                      (9, 1): lambda b: (trig(b), take_z(b, 1)),
                      (10, 0): lambda b: take_z(b, 2), (10, 1): lambda b: take_z(b, 3),
                      (12, 0): take_bc, (13, 0): take_head_decay,
                      (13, 1): lambda b: take_decay(b, 0), (14, 0): lambda b: take_decay(b, 1),
                      (14, 1): lambda b: take_decay(b, 2), (15, 0): lambda b: take_decay(b, 3)}

            def decay(tile, j):
                step = ST * tile + j
                act.wait_ge(s_d, step + 1)
                if not is_first(tile):
                    act.wait_ge(s_Y, step - ST + 1)
                nc.scalar.activation(e[:, j].rearrange("p g t -> p (g t)"),
                                     dps[:, j % 2].rearrange("p g t -> p (g t)"), ACT.Exp).then_inc(s_e, 1)

            def take_prev(tile, pair):
                act.wait_ge(s_pt, 2 * tile + pair + 1)
                if pair == 0 and not is_first(tile):
                    act.wait_ge(s_yo, tile)
                src = (mps, ops[:].rearrange("p g t -> p (g t)"))[pair]
                nc.scalar.activation(pT[:, pair, :], src[:], ACT.Copy).then_inc(s_pT, 1)

            def square(tile):
                act.wait_ge(s_y, tile + 1)
                if not is_first(tile):
                    act.wait_ge(s_tail, tile)
                nc.scalar.activation(y2[:], y[:], ACT.Square).then_inc(s_y2, 1)

            def sequence(b, ahead):
                for t in range(TB):
                    tile = TB * b + t
                    started = not (is_first(b) and t == 0)
                    for j in range(ST):
                        piece = [pieces.get((ST * t + j, i)) if ahead else None for i in range(2)]
                        decay(tile, j)
                        if j >= 2:
                            take_prev(tile, j - 2)
                        if j == 2 and started:
                            square(tile - 1)
                        for p in piece:
                            if p:
                                p(b + 1)
                if not ahead:
                    square(tile)

            act.wait_ge(weights.loaded, 16 * weights.n_loads)
            act.wait_ge(s_const, NCONST)
            nc.scalar.activation(a_exp[:], row[:, 0:H], ACT.Exp).then_inc(s_ae, 1)
            for piece in pieces.values():
                piece(0)
            sequence(0, True)
            with act.Fori(1, NB - 1) as b:
                sequence(b, True)
            sequence(NB - 1, False)

        @block.vector
        def _(dve):
            chain = Chain(dve, s_v, 16)

            def statistics(b):
                chain.begin(b)
                for t in range(TB):
                    ins = nc.vector.bn_stats(stats[:, t, :], x_res[:, TB * b + t, :])
                chain.link(ins)
                nc.vector.memset(scrap[:], 0.0)
                for t in range(TB):
                    ins = nc.vector.bn_aggr(mv[:, t, :], stats[:, t, :])
                ins.then_inc(s_var, 1)

            def normalise(b):
                dve.wait_ge(s_rstd, b + 1)
                for t in range(TB):
                    ins = nc.vector.tensor_scalar(zn[:, t, :], x_res[:, TB * b + t, :], mv[:, t, 0:1],
                                                  rstd[:, t:t + 1], ALU.subtract, ALU.mult)
                ins.then_inc(s_zn, 1)

            def raw(b):
                dve.wait_ge(s_rest, TB * (b + 1))
                chain.link(nc.vector.tensor_tensor(v[:], rest[:, :, DT:DT + H], bc_mid(row[:, H:2 * H], TB), ALU.add))
                nc.vector.tensor_scalar(vm[:], v[:], 30.0, None, ALU.min).then_inc(s_vm, 1)
                bc = rest[:, :, 0:2 * NS]
                chain.link(nc.vector.tensor_tensor(bsq[:].rearrange("p (t a) n -> p t (a n)", t=TB), bc, bc, ALU.mult))
                nc.vector.tensor_reduce(bss[:], bsq[:], AX, ALU.add).then_inc(s_bss, 1)

            def rates(b):
                dve.wait_ge(s_vl, b + 1)
                nc.vector.tensor_tensor(dt[:], v[:], vm[:], ALU.max)
                chain.link(nc.vector.tensor_scalar(le[:], le[:], 0.5, 0.5, ALU.mult, ALU.add))
                chain.link(nc.vector.tensor_scalar(dt[:], dt[:], 1e-4, 0.5, ALU.max, ALU.min))
                nc.vector.tensor_tensor(dA[:], dt[:], bc_mid(a_neg[:], TB), ALU.mult)
                nc.vector.tensor_reduce(dtm[:], dt[:], AX, ALU.add)
                chain.link(nc.vector.tensor_tensor(pp[:], dt[:], le[:], ALU.mult))
                nc.vector.tensor_scalar(dtm[:], dtm[:], -1.0 / H, None, ALU.mult)
                chain.link(nc.vector.tensor_copy(dA2[:, b % 2], dA[:]))
                nc.vector.tensor_tensor(th[:], rest[:, :, TH:TH + NR], bc_last(dtm[:], NR), ALU.mult)
                nc.vector.tensor_tensor(qq[:], dt[:], pp[:], ALU.subtract).then_inc(s_qq, 1)
                dve.wait_ge(s_brr, b + 1)
                chain.link(nc.vector.tensor_tensor(
                    bn, rest[:, :, 0:2 * NS].rearrange("p t (a n) -> p t a n", a=2),
                    brr[:].rearrange("p (t a) -> p t a", t=TB).unsqueeze(3).to_broadcast([P, TB, 2, NS]), ALU.mult))
                chain.link(nc.vector.tensor_tensor(
                    bn.rearrange("p t a n -> p t (a n)"), bn.rearrange("p t a n -> p t (a n)"),
                    bc_mid(nbias, TB), ALU.mult))

            def angles(b):
                dve.wait_ge(s_f, full(b, CUM))
                cum = front(b, CUM)[:, 0:TB * NR].rearrange("p (t n) -> p t n", t=TB)
                chain.link(nc.vector.tensor_scalar(kk[:], cum, float(1 / (2 * np.pi)), ROUND, ALU.mult, ALU.add))
                chain.link(nc.vector.tensor_scalar(kk[:], kk[:], ROUND, None, ALU.subtract))
                chain.link(nc.vector.scalar_tensor_tensor(arg[:], kk[:], -TWO_PI_HI, cum, ALU.mult, ALU.add))
                chain.link(nc.vector.scalar_tensor_tensor(arg[:], kk[:], -TWO_PI_LO, arg[:], ALU.mult, ALU.add))
                nc.vector.tensor_scalar(arg[:], arg[:], 3.1415925, -3.1415925, ALU.min, ALU.max).then_inc(s_arg, 1)

            def seen_later(b):
                dve.wait_ge(s_f, full(b, QS))
                nc.vector.tensor_tensor(gw[:, b % 2], pp[:],
                                        front(b, QS)[:, 0:TB * H].rearrange("p (t h) -> p t h", t=TB), ALU.add).then_inc(s_g, 1)

            def rotate(b):
                dve.wait_ge(s_trig, b + 1)
                x1, x2 = bn[:, :, :, 0:NR], bn[:, :, :, NR:]
                cosb = cs[:].unsqueeze(2).to_broadcast([P, TB, 2, NR])
                sinb = sn[:].unsqueeze(2).to_broadcast([P, TB, 2, NR])
                nc.vector.tensor_tensor(rt[:, 0], x1, cosb, ALU.mult)
                nc.vector.tensor_tensor(rt[:, 1], x2, sinb, ALU.mult)
                nc.vector.tensor_tensor(rt[:, 2], x1, sinb, ALU.mult)
                chain.link(nc.vector.tensor_tensor(rt[:, 3], x2, cosb, ALU.mult))
                nc.vector.tensor_tensor(br[:, :, :, 0:NR], rt[:, 0], rt[:, 1], ALU.subtract)
                nc.vector.tensor_tensor(br[:, :, :, NR:], rt[:, 2], rt[:, 3], ALU.add).then_inc(s_br, 1)
                dve.wait_ge(s_br, b + 1)
                dve.wait_ge(s_dcs, b + 1)
                nc.vector.tensor_tensor(ww[:, b % 2], ww[:, b % 2], gw[:, b % 2], ALU.mult)
                chain.link(nc.vector.tensor_tensor(bsq[:, 0:TB, :], br[:, :, 0, :], br[:, :, 1, :], ALU.mult))
                chain.link(nc.vector.tensor_reduce(cbd[:], bsq[:, 0:TB, :], AX, ALU.add))
                nc.vector.tensor_tensor(dl[:, b % 2], pp[:], bc_last(cbd[:], H), ALU.mult).then_inc(s_front, 1)

            def mask_cb(b):
                dve.wait_ge(s_f, full(b, CBT))
                for c in range(NC):
                    rows = slice(c * Q, (c + 1) * Q)
                    for i in range(NQ):
                        ins = nc.vector.tensor_tensor(
                            cbm[i * Q:(i + 1) * Q, b % 2, :].rearrange("p (k t) -> p k t", t=P)[:, :, rows],
                            front(b, CBT)[rows, :].rearrange("p (k t) -> p k t", t=P)[:, :, rows],
                            bc_mid(mask_st[rows], TB), ALU.mult)
                ins.then_inc(s_cbm, 1)
                chain.end()

            def prepare(b, tile, t):
                if t == 0:
                    dve.wait_ge(s_front, b + 1)
                    dve.wait_ge(s_xg, TB * (b + 1))
                if not (isinstance(tile, int) and tile < 2):
                    dve.wait_ge(s_Y, ST * tile - ST)
                x = xg[:, b % 2, t, :].rearrange("p (h q) -> p h q", q=HP)
                for c in range(NC):
                    for i in range(NQ):
                        src = slice(c * Q, (c + 1) * Q)
                        nc.vector.tensor_tensor(
                            xbd[i * Q:(i + 1) * Q, t % 2, c, :, i, :],
                            x[src].rearrange("p (g i) q -> p i g q", i=NQ)[:, i],
                            heads(gw[src, b % 2, t, :].rearrange("p (g i) -> p i g", i=NQ)[:, i]), ALU.mult)
                nc.vector.tensor_tensor(xw[:, t % 2, :].rearrange("p (h q) -> p h q", q=HP), x,
                                        heads(ww[:, b % 2, t, :]), ALU.mult)
                nc.vector.tensor_tensor(xdl[:, t % 2, :].rearrange("p (h q) -> p h q", q=HP), x,
                                        heads(dl[:, b % 2, t, :]), ALU.mult).then_inc(s_prep, 1)

            def mask(b, tile, t, j):
                dve.wait_ge(s_e, ST * tile + j + 1)
                if t == 0 and j == 0:
                    dve.wait_ge(s_cbm, b + 1)
                nc.vector.tensor_tensor(e[:, j], e[:, j], bc_mid(cbm[:, b % 2, t * P:(t + 1) * P], NG),
                                        ALU.mult).then_inc(s_em, 1)

            def carry_states(b, tile, t, pair):
                if t == 0 and pair == 0:
                    if not is_first(b):
                        dve.wait_ge(s_pt, 2 * tile)
                    nc.vector.memset(st[:, :, 0, :], 0.0).then_inc(s_z0, 1)
                    dve.wait_ge(s_z0, b + 1)
                    dve.wait_ge(s_ecs, NG * (b + 1))
                elif pair == 0:
                    dve.wait_ge(s_pt, 2 * tile)
                dve.wait_ge(s_S, 2 * tile + pair + 1)
                base = 4 * NC * tile + 2 * NC * pair
                for c in range(NC):
                    for i in range(2):
                        g, n = 2 * pair + i, 2 * c + i
                        if c > 0:
                            dve.wait_ge(s_rs, base + n - 1)
                        slot = NC * (t % 2) + c
                        at = t * P + c * Q + Q - 1
                        nc.vector.scalar_tensor_tensor(st[:, g, (slot + 1) % (2 * NC), :], st[:, g, slot, :],
                                                       ecs[:, b % 2, g, at:at + 1], sps[:, i, c, :], ALU.mult,
                                                       ALU.add).then_inc(s_rs, 1)

            def combine(b, tile, t):
                dve.wait_ge(s_yo, tile + 1)
                nc.vector.tensor_tensor(y[:], ops[:], ecs[:, b % 2, :, t * P:(t + 1) * P],
                                        ALU.mult).then_inc(s_t1, 1)
                dve.wait_ge(s_t1, tile + 1)
                dve.wait_ge(s_Y, ST * (tile + 1))
                if not is_first(tile):
                    dve.wait_ge(s_tail, tile)
                nc.vector.tensor_tensor(y[:], yps[:, t % 2], y[:], ALU.add).then_inc(s_y, 1)
                dve.wait_ge(s_y, tile + 1)
                dve.wait_ge(s_sz, NG * (b + 1))
                nc.vector.tensor_tensor(gT[:], y[:], szT[:, b % 2, :, t * P:(t + 1) * P], ALU.mult).then_inc(s_gT, 1)

            def mean_square(tile):
                dve.wait_ge(s_tail, tile + 1)
                nc.vector.tensor_scalar(ms[:], mps[:, D:D + 1], 1.0 / DI, RMS_EPS, ALU.mult, ALU.add).then_inc(s_ms, 1)

            def update(tile):
                dve.wait_ge(s_rr, tile + 1)
                nc.vector.scalar_tensor_tensor(x_res[:, tile, :], mps[:, 0:D], rr[:], x_res[:, tile, :], ALU.mult,
                                               ALU.add).then_inc(s_x, 1)

            pieces = {(0, 1): statistics, (1, 0): normalise, (5, 0): raw, (7, 1): rates,
                      (8, 1): lambda b: (angles(b), seen_later(b)), (11, 1): rotate, (12, 1): mask_cb}

            def sequence(b, ahead):
                for t in range(TB):
                    tile = TB * b + t
                    for j in range(ST):
                        piece = [pieces.get((ST * t + j, i)) if ahead else None for i in range(2)]
                        two_back = not (is_first(b) and t < 2)
                        if j == 0 and two_back:
                            mean_square(tile - 2)
                        if j == 1 and two_back:
                            update(tile - 2)
                        if piece[0]:
                            piece[0](b + 1)
                        if j < 2:
                            carry_states(b, tile, t, j)
                        mask(b, tile, t, j)
                        if j == 1 and not (is_first(b) and t == 0):
                            combine(b if t else b - 1, tile - 1, (t - 1) % TB)
                        if piece[1]:
                            piece[1](b + 1)
                        if j == 2 and (t + 1 < TB or ahead):
                            prepare(b if t + 1 < TB else b + 1, tile + 1, (t + 1) % TB)
                if not ahead:
                    mean_square(tile - 1)
                    update(tile - 1)
                    combine(b, tile, t)
                    mean_square(tile)
                    update(tile)

            dve.wait_ge(weights.loaded, 16 * weights.n_loads)
            dve.wait_ge(s_const, NCONST)
            nc.vector.tensor_tensor(strict.rearrange("p c t -> p (c t)"), tri_c[:].rearrange("p c t -> p (c t)"),
                                    ident[:], ALU.subtract).then_inc(s_mask, 1)
            dve.wait_ge(s_mask, 1)
            nc.vector.tensor_reduce(mask_st[:], strict.rearrange("p c t -> p t c"), AX, ALU.add).then_inc(s_mask, 1)
            nc.vector.tensor_reduce(mask_rs[:], after[:].rearrange("p c t -> p t c"), AX, ALU.add).then_inc(s_mask, 1)
            nc.vector.tensor_scalar(nbias[:, NS:], nbias[:, NS:], float(NS) ** -0.5, None, ALU.mult)
            dve.wait_ge(s_ae, 1)
            nc.vector.tensor_scalar(a_neg[:], a_exp[:], -1.0, None, ALU.mult).then_inc(s_mask, 1)
            dve.wait_ge(s_mask, 4)
            for piece in pieces.values():
                piece(0)
            prepare(0, 0, 0)
            sequence(0, True)
            with dve.Fori(1, NB - 1) as b:
                sequence(b, True)
            sequence(NB - 1, False)


def hybrid_block(nc, ins, out):
    with ExitStack() as ctx:
        x_res = ctx.enter_context(nc.sbuf_tensor("x_res", [P, NT, D], F32))
        ident = ctx.enter_context(nc.sbuf_tensor("ident", [P, P], F32))
        a = {n[len("L0_attn_a_"):]: v for n, v in ins.items() if n.startswith("L0_attn_a_")}
        s = {n[len("L0_attn_b_"):]: v for n, v in ins.items() if n.startswith("L0_attn_b_")}
        f = {n[len("L0_ffn_"):]: v for n, v in ins.items() if n.startswith("L0_ffn_")}
        bias = FfnBiases(nc, ctx, f)
        signals = FfnSignals(nc, ctx, f)
        with ExitStack() as before_ffn2:
            ssd = SsdWeights(nc, before_ffn2, s)
            with ExitStack() as before_ssd:
                ffn1 = FfnWeights(nc, before_ssd, f, signals, 1)

                def load_later(sp):
                    ffn1.load(sp)
                    ssd.load(sp)

                phase_mamba(nc, x_res, ident, a, a["x"], load_later, bias)
                phase_ffn(nc, x_res, ident, bias, ffn1, False, "f1_")
            phase_ssd(nc, x_res, ident, ssd)
        ffn2 = FfnWeights(nc, ctx, f, signals, 2)
        phase_ffn(nc, x_res, ident, bias, ffn2, True, "f2_")
        stored = ctx.enter_context(nc.semaphore("stored"))
        block = ctx.enter_context(nc.Block())

        @block.sync
        def _(sp):
            sp.dma_start(out.rearrange("b (t p) d -> p (b t) d", p=P), x_res[:]).then_inc(stored, 16)
            sp.wait_ge(stored, 16)


_TURNED = ("L0_attn_a_in_proj_w", "L0_attn_a_x_proj_w", "L0_attn_a_dt_proj_w", "L0_attn_a_out_proj_w")


def kernel(**inputs):
    import numpy as np
    import concourse.bacc as bacc
    from concourse import mybir as mb
    from concourse.bass_utils import run_bass_kernel_spmd

    nc = bacc.Bacc("TRN2", target_bir_lowering=False, num_devices=1)
    arrays, aps = {}, {}
    for name, value in inputs.items():
        a = np.asarray(value)
        a = np.ascontiguousarray(a.T if name in _TURNED else a)
        arrays["in_" + name] = a
        aps[name] = nc.dram_tensor("in_" + name, a.shape, mb.dt.from_np(a.dtype), kind="ExternalInput").ap()
    out = nc.dram_tensor("out_x", (NB, T, D), F32, kind="ExternalOutput").ap()
    hybrid_block(nc, aps, out)
    r = run_bass_kernel_spmd(nc, [arrays], core_ids=[0])
    return r.results[0]["out_x"]
```

```python
from contextlib import ExitStack

import concourse.bass as bass
import numpy as np
from concourse import mybir

F32 = mybir.dt.float32
BF16 = mybir.dt.bfloat16
F16 = mybir.dt.float16
ALU = mybir.AluOpType
ACT = mybir.ActivationFunctionType
AX = mybir.AxisListType.X

P = 128
NB = 4
T = 512
D = 256
KD = D // P
TB = T // P
NT = NB * TB
LN_EPS = 1e-5


class Chain:

    def __init__(self, eng, sem, per):
        self.eng, self.sem, self.per, self.base, self.k = eng, sem, per, 0, 0

    def begin(self, turn):
        self.base, self.k = turn * self.per, 0

    def mark(self, ins):
        self.k += 1
        ins.then_inc(self.sem, 1)

    def wait(self):
        self.eng.wait_ge(self.sem, self.base + self.k)

    def link(self, ins):
        self.mark(ins)
        self.wait()

    def end(self):
        assert self.k == self.per, (self.k, self.per)


def bc_last(ap, n):
    return ap.unsqueeze(len(ap.shape)).to_broadcast(list(ap.shape) + [n])


def bc_mid(ap, n):
    return ap.unsqueeze(1).to_broadcast([ap.shape[0], n] + list(ap.shape[1:]))


def phase_mamba(nc, x_res, ident, w, x_dram, load_later, bias, split):
    NS, R = 16, 64
    CT = 4
    HT, XC, CV, DBC, DT, NF = 0, 2, 4, 7, 8, 11
    Z = (6, 10)
    with ExitStack() as ctx:
        def sb(name, shape, dt=F32):
            return ctx.enter_context(nc.sbuf_tensor("m_" + name, shape, dt))

        def ps(name, shape):
            return ctx.enter_context(nc.psum_tensor("m_" + name, shape, F32))

        def sem(name):
            return ctx.enter_context(nc.semaphore("m_" + name))

        w_in = sb("w_in", [P, KD, 2 * D])
        w_conv = sb("w_conv", [P, CT, KD, D])
        w_xp = sb("w_xp", [P, KD, R + 2 * NS])
        w_dt = sb("w_dt", [R, D])
        w_out = sb("w_out", [P, KD, D])
        norm_w = sb("norm_w", [P, KD])
        conv_b = sb("conv_b", [P, KD])
        dt_b = sb("dt_b", [P, KD])
        d_skip = sb("d_skip", [P, KD])
        a_log = sb("a_log", [P, KD, NS])
        a_exp = sb("a_exp", [P, KD, NS])
        a_neg = sb("a_neg", [P, KD, NS])
        sel = sb("sel", [3 * 2 * NS, 2 * NS, P], BF16)

        stats = sb("stats", [P, TB, 6])
        scrap = sb("scrap", [P, 1])
        mv = sb("mv", [P, TB, 2])
        rstd = sb("rstd", [P, TB])
        var = sb("var", [P, TB])
        ms = sb("ms", [P, TB])
        half = sb("half", [P, TB])
        eps = sb("eps", [P, TB])
        r2 = sb("r2", [P, TB])
        xn = sb("xn", [P, TB, D])
        h = sb("h", [P, TB, D])
        hT = sb("hT", [P, KD, T])
        xc = sb("xc", [P, KD, T + CT - 1])
        dlow = sb("dlow", [R, T])
        rest = sb("rest", [2 * 2 * NS, T])
        sp_in = sb("sp_in", [P, KD, T])
        sp_e = sb("sp_e", [P, KD, T])
        sp_l = sb("sp_l", [P, KD, T])
        sz = sb("sz", [P, 2, KD, T])
        xs = sb("xs", [P, 2, KD, T])
        delta = sb("delta", [P, 2, KD, T])
        u = sb("u", [P, 2, KD, T])
        bc3 = sb("bc3", [3 * 2 * NS, 2, T], BF16)
        dA = sb("dA", [P, 3, KD, T])
        bx = sb("bx", [P, 2, KD, T])
        hs = sb("hs", [P, 2, KD, T])
        place = split.whole[:].rearrange("p j k e n -> p (j k e n)")
        hc = place[:, 0:3 * KD * T].rearrange("p (i k t) -> p i k t", i=3, k=KD)
        y2 = sb("y2", [P, KD, T])
        g = place[:, 3 * KD * T:4 * KD * T].rearrange("p (k t) -> p k t", k=KD)

        bias.whole = dA[0:33].rearrange("p i k t -> p (i k t)")[:, 0:bias.n]

        front = [ps(f"front{j}", [P, T]) for j in range(2)]
        yps = ps("yps", [P, KD, T])
        Bps = ps("Bps", [P, 2, T])
        Cps = ps("Cps", [P, 2, T])

        s_x0 = sem("x0_loaded")
        s_x = sem("x_loaded")
        s_wn = sem("norm_w_loaded")
        s_wi = sem("in_proj_loaded")
        s_wc = sem("conv_loaded")
        s_wx = sem("x_proj_loaded")
        s_wd = sem("dt_proj_loaded")
        s_wa = sem("a_log_loaded")
        s_wo = sem("out_proj_loaded")
        s_bs = sem("bias_step")
        s_pool = sem("pool_step")
        s_id = sem("ident_ready")
        s_pad = sem("conv_pad_ready")
        s_sel = sem("selectors_ready")
        s_ae = sem("a_exp_ready")
        s_a = sem("a_ready")
        s_vf = sem("vector_front_step")
        s_pf = sem("pool_front_step")
        s_half = sem("half_ready")
        s_var = sem("var_ready")
        s_r2 = sem("r2_ready")
        s_xn = sem("xn_ready")
        s_h = sem("h_ready")
        s_res = sem("residual_added")
        s_full = sem("front_full")
        s_hT = sem("hT_ready")
        s_xc = sem("xc_ready")
        s_sz = sem("sz_ready")
        s_xs = sem("xs_ready")
        s_dlow = sem("dlow_ready")
        s_bc3 = sem("bc3_ready")
        s_spin = sem("sp_in_ready")
        s_spe = sem("sp_e_ready")
        s_spl = sem("sp_l_ready")
        s_delta = sem("delta_ready")
        s_u = sem("u_ready")
        s_B = sem("B_full")
        s_C = sem("C_full")
        s_bx = sem("bx_ready")
        s_dA = sem("dA_ready")
        s_scan = sem("scan_done")
        s_hc = sem("hc_ready")
        s_hcu = sem("hc_used")
        s_y2 = sem("y2_ready")
        s_g = sem("g_ready")
        s_o = sem("out_full")
        s_xo = sem("x_updated")

        block = ctx.enter_context(nc.Block())

        def full(b, use):
            return b * NF + use + 1

        def is_first(b):
            return isinstance(b, int) and b == 0

        def is_second(b):
            return isinstance(b, int) and b == 1

        @block.sync
        def _(sp):
            xv = x_dram.rearrange("b (t p) d -> b p t d", p=P)
            sp.dma_start(x_res[:, 0:TB, :], xv[0]).then_inc(s_x0, 16)

            def column(dst, src, sem):
                sp.dma_start(dst[:], src.rearrange("(k p) -> p k", p=P),
                             allow_slow_non_contiguous=True).then_inc(sem, 16)

            def rows(dst, src, sem):
                sp.dma_start(dst[:], src.rearrange("(k p) n -> p k n", p=P)).then_inc(sem, 16)

            column(norm_w, w["norm_w"], s_wn)
            rows(w_in, w["in_proj_w"], s_wi)
            sp.dma_start(w_conv[:], w["conv_w"].rearrange("j (k p) n -> p j k n", p=P)).then_inc(s_wc, 16)
            column(conv_b, w["conv_b"], s_wc)
            rows(w_xp, w["x_proj_w"], s_wx)
            sp.dma_start(w_dt[:], w["dt_proj_w"]).then_inc(s_wd, 16)
            column(dt_b, w["dt_proj_b"], s_wd)
            rows(a_log, w["A_log"], s_wa)
            column(d_skip, w["D"], s_wa)
            split.load(sp)
            bias.load(sp)
            for b in range(1, NB):
                sp.dma_start(x_res[:, b * TB:(b + 1) * TB, :], xv[b]).then_inc(s_x, 16)
            rows(w_out, w["out_proj_w"], s_wo)
            load_later(sp)
            split.keep(sp)

        @block.gpsimd
        def _(pool):
            chain = Chain(pool, s_pool, 4)
            nc.gpsimd.memset(half[:], -0.5).then_inc(s_half, 1)
            nc.gpsimd.memset(eps[:], LN_EPS).then_inc(s_half, 1)
            pool.wait_ge(s_half, 2)
            chain.link(nc.gpsimd.memset(ident[:], 0.0))
            nc.gpsimd.affine_select(out=ident[:], in_=ident[:], compare_op=ALU.not_equal, fill=1.0, base=0,
                                    pattern=[[-1, P]], channel_multiplier=1).then_inc(s_id, 1)
            nc.gpsimd.memset(xc[:, :, 0:CT - 1], 0.0).then_inc(s_pad, 1)
            pool_chain = Chain(pool, s_pf, 6)

            def scales(b):
                pool_chain.begin(b)
                pool.wait_ge(s_var, b + 1)
                if not is_first(b):
                    pool.wait_ge(s_h, b)
                pool_chain.link(nc.gpsimd.tensor_tensor(ms[:], var[:], eps[:], ALU.add))
                pool_chain.link(nc.gpsimd.tensor_tensor(rstd[:], ms[:], half[:], ALU.pow))
                pool_chain.link(nc.gpsimd.tensor_tensor(ms[:], var[:], rstd[:], ALU.mult))
                pool_chain.link(nc.gpsimd.tensor_tensor(ms[:], ms[:], rstd[:], ALU.mult))
                pool_chain.link(nc.gpsimd.tensor_tensor(ms[:], ms[:], eps[:], ALU.add))
                pool_chain.link(nc.gpsimd.tensor_tensor(r2[:], ms[:], half[:], ALU.pow))
                nc.gpsimd.tensor_tensor(r2[:], r2[:], rstd[:], ALU.mult).then_inc(s_r2, 1)
                pool_chain.end()

            def residual(b, rows):
                pool.wait_ge(s_xn, b + 1)
                pool.wait_ge(s_h, b + 1)
                nc.gpsimd.tensor_tensor(rows, rows, xn[:], ALU.add).then_inc(s_res, 1)

            scales(0)
            residual(0, x_res[:, 0:TB, :])
            split.constants()
            nc.gpsimd.memset(bias.parts[:], 0.0).then_inc(bias.ready, 1)
            chain.link(nc.gpsimd.memset(sel[:], 0.0))
            for part in range(3):
                ins = nc.gpsimd.affine_select(out=sel[:], in_=sel[:], compare_op=ALU.not_equal, fill=1.0,
                                              base=-2 * NS * part, pattern=[[-1, 2 * NS], [0, P]],
                                              channel_multiplier=1)
                if part < 2:
                    chain.link(ins)
                if part == 0:
                    split.take_root(pool)
            ins.then_inc(s_sel, 1)
            chain.end()
            with pool.Fori(1, NB) as b:
                scales(b)
                residual(b, x_res[:, bass.ds(TB * b, TB), :])

        @block.tensor
        def _(pe):
            def transposes(b):
                pe.wait_ge(s_h, b + 1)
                for k in range(KD):
                    if is_first(b):
                        pass
                    elif is_second(b):
                        pe.wait_ge(s_spin, b)
                        pe.wait_ge(s_sz, KD * b)
                    else:
                        pe.wait_ge(s_xo, KD * (b - 1))
                    for t in range(TB):
                        mm = nc.tensor.transpose(front[(HT + k) % 2][:, t * P:(t + 1) * P],
                                                 h[:, t, k * P:(k + 1) * P], ident[:])
                    mm.then_inc(s_full, 1)

            def in_proj(b, m, use, col, read, count):
                pe.wait_ge(s_hT, KD * (b + 1))
                pe.wait_ge(read, count)
                if is_first(b):
                    pe.wait_ge(s_wi, 16)
                for k in range(KD):
                    mm = nc.tensor.matmul(front[use % 2][:], w_in[:, k, (col + m) * P:(col + m + 1) * P],
                                          hT[:, k, :], start=(k == 0), stop=(k == KD - 1))
                mm.then_inc(s_full, 1)

            def conv(b, m, half):
                if half == 0:
                    pe.wait_ge(s_xc, KD * (b + 1))
                if is_first(b):
                    pe.wait_ge(s_wc, 32)
                for j in range(2 * half, 2 * half + 2):
                    for k in range(KD):
                        mm = nc.tensor.matmul(front[(CV + m) % 2][:], w_conv[:, j, k, m * P:(m + 1) * P],
                                              xc[:, k, j:j + T], start=(j == 0 and k == 0),
                                              stop=(j == CT - 1 and k == KD - 1))
                if half == 1:
                    mm.then_inc(s_full, 1)

            def x_proj(b):
                pe.wait_ge(s_xs, KD * (b + 1))
                if is_first(b):
                    pe.wait_ge(s_wx, 16)
                for k in range(KD):
                    mm = nc.tensor.matmul(front[DBC % 2][0:R + 2 * NS, :], w_xp[:, k, :], xs[:, b % 2, k, :],
                                          start=(k == 0), stop=(k == KD - 1))
                mm.then_inc(s_full, 1)

            def dt_proj(b):
                pe.wait_ge(s_dlow, b + 1)
                pe.wait_ge(s_sz, KD * b + 1)
                if is_first(b):
                    pe.wait_ge(s_wd, 32)
                for m in range(KD):
                    if m == 1:
                        pe.wait_ge(s_bc3, b + 1)
                    nc.tensor.matmul(front[(DT + m) % 2][:], w_dt[:, m * P:(m + 1) * P], dlow[:], start=True,
                                     stop=True).then_inc(s_full, 1)

            pieces = {3: transposes,
                      4: lambda b: in_proj(b, 0, XC, 0, s_hT, KD * b + 1),
                      5: lambda b: in_proj(b, 1, XC + 1, 0, s_hT, KD * b + 2),
                      6: lambda b: conv(b, 0, 0), 7: lambda b: conv(b, 0, 1),
                      8: lambda b: conv(b, 1, 0), 9: lambda b: conv(b, 1, 1),
                      10: lambda b: in_proj(b, 0, Z[0], KD, s_xs, KD * b + 1), 11: x_proj, 13: dt_proj,
                      14: lambda b: in_proj(b, 1, Z[1], KD, s_spin, b + 1)}

            def broadcast_B(b, n):
                step = NS * b + n
                if not (is_first(b) and n < 2):
                    pe.wait_ge(s_bx, step - 1)
                nc.tensor.matmul(Bps[:, n % 2, :], sel[:, n, :], bc3[:, b % 2, :], start=True,
                                 stop=True).then_inc(s_B, 1)

            def broadcast_C(b, n):
                step = NS * b + n
                if not (is_first(b) and n < 2):
                    pe.wait_ge(s_hc, step - 1)
                nc.tensor.matmul(Cps[:, n % 2, :], sel[:, NS + n, :], bc3[:, b % 2, :], start=True,
                                 stop=True).then_inc(s_C, 1)

            def accumulate(b, n):
                step = NS * b + n
                pe.wait_ge(s_hc, step + 1)
                if n == 0 and not is_first(b):
                    pe.wait_ge(s_y2, b)
                for m in range(KD):
                    mm = nc.tensor.matmul(yps[:, m, :], ident[:], hc[:, (step % 3), m, :], start=(n == 0),
                                          stop=(n == NS - 1))
                mm.then_inc(s_hcu, 1)

            def out_proj(b, fronts):
                pe.wait_ge(s_g, b + 1)
                pe.wait_ge(s_spin, fronts)
                pe.wait_ge(s_sz, KD * fronts)
                for j in range(KD):
                    for t in range(2 * j, 2 * j + 2):
                        for k in range(KD):
                            mm = nc.tensor.matmul(front[1 - j][:, (t % 2) * D:(t % 2 + 1) * D],
                                                  g[:, k, t * P:(t + 1) * P], w_out[:, k, :],
                                                  start=(k == 0), stop=(k == KD - 1))
                    mm.then_inc(s_o, 1)

            def sequence(b, ahead):
                for n in range(NS):
                    if n + 2 < NS:
                        broadcast_B(b, n + 2)
                    elif ahead:
                        if n + 2 == NS:
                            pe.wait_ge(s_bc3, b + 2)
                        broadcast_B(b + 1, n + 2 - NS)
                    if ahead and n in pieces:
                        pieces[n](b + 1)
                    if n + 1 < NS:
                        broadcast_C(b, n + 1)
                    elif ahead:
                        broadcast_C(b + 1, 0)
                    if n >= 1:
                        accumulate(b, n - 1)
                    elif not is_first(b):
                        accumulate(b - 1, NS - 1)
                    if n == 1 and not is_first(b):
                        out_proj(b - 1, b + 1)
                if not ahead:
                    accumulate(b, NS - 1)
                    out_proj(b, NB)

            pe.wait_ge(s_id, 1)
            pe.wait_ge(s_pad, 1)
            for n, piece in pieces.items():
                if n == 8:
                    split.add_up(pe, Bps[:, 0, :])
                if n == 14:
                    pe.wait_ge(s_sel, 1)
                    broadcast_B(0, 0)
                    broadcast_B(0, 1)
                    broadcast_C(0, 0)
                piece(0)
            pe.wait_ge(s_wo, 16)
            sequence(0, True)
            with pe.Fori(1, NB - 1) as b:
                sequence(b, True)
            sequence(NB - 1, False)

        @block.scalar
        def _(act):
            def take_hT(b):
                if is_first(b):
                    act.wait_ge(s_wn, 16)
                for k in range(KD):
                    act.wait_ge(s_full, full(b, HT + k))
                    nc.scalar.activation(hT[:, k, :], front[(HT + k) % 2][:], ACT.Copy,
                                         scale=norm_w[:, k:k + 1]).then_inc(s_hT, 1)

            def take_xc(b, k):
                act.wait_ge(s_full, full(b, XC + k))
                nc.scalar.activation(xc[:, k, CT - 1:], front[(XC + k) % 2][:], ACT.Copy).then_inc(s_xc, 1)

            def take_z(b, k):
                act.wait_ge(s_full, full(b, Z[k]))
                nc.scalar.activation(sz[:, b % 2, k, :], front[Z[k] % 2][:], ACT.Silu).then_inc(s_sz, 1)

            def take_conv(b, k):
                if is_first(b):
                    act.wait_ge(s_wc, 32)
                act.wait_ge(s_full, full(b, CV + k))
                nc.scalar.activation(xs[:, b % 2, k, :], front[(CV + k) % 2][:], ACT.Silu,
                                     bias=conv_b[:, k:k + 1]).then_inc(s_xs, 1)

            def take_dlow(b):
                act.wait_ge(s_full, full(b, DBC))
                nc.scalar.activation(dlow[:], front[DBC % 2][0:R, :], ACT.Copy).then_inc(s_dlow, 1)

            def softplus(b):
                act.wait_ge(s_spin, b + 1)
                nc.scalar.activation(sp_e[:], sp_in[:], ACT.Exp).then_inc(s_spe, 1)
                act.wait_ge(s_spe, b + 1)
                nc.scalar.activation(sp_l[:], sp_e[:], ACT.Ln, bias=1.0).then_inc(s_spl, 1)

            pieces = {5: take_hT, 6: lambda b: take_xc(b, 0), 7: lambda b: take_xc(b, 1),
                      9: lambda b: take_conv(b, 0), 11: lambda b: (take_conv(b, 1), take_z(b, 0)),
                      13: take_dlow, 15: softplus}

            def sequence(b, ahead):
                for n in range(NS):
                    step = NS * b + n
                    if n == 0:
                        act.wait_ge(s_delta, b + 1)
                    if not (is_first(b) and n < 3):
                        act.wait_ge(s_scan, step - 2)
                    for m in range(KD):
                        ins = nc.scalar.activation(dA[:, step % 3, m, :], delta[:, b % 2, m, :], ACT.Exp,
                                                   scale=a_neg[:, m, n:n + 1])
                    ins.then_inc(s_dA, 1)
                    if n == 1:
                        take_z(b, 1)
                    if ahead and n in pieces:
                        pieces[n](b + 1)

            for n, piece in pieces.items():
                piece(0)
                if n == 7:
                    split.square(act)
                    split.high(act)
                if n == 13:
                    split.high_ssd(act)
            act.wait_ge(s_wa, 32)
            nc.scalar.activation(a_exp[:], a_log[:], ACT.Exp).then_inc(s_ae, 1)
            act.wait_ge(s_a, 1)
            sequence(0, True)
            with act.Fori(1, NB - 1) as b:
                sequence(b, True)
            sequence(NB - 1, False)

        @block.vector
        def _(dve):
            chain = Chain(dve, s_vf, 6)

            def statistics(b):
                chain.begin(b)
                dve.wait_ge(s_x0 if is_first(b) else s_x, 16 if is_first(b) else 16 * (NB - 1))
                if not is_first(b):
                    dve.wait_ge(s_h, b)
                for t in range(TB):
                    ins = nc.vector.bn_stats(stats[:, t, :], x_res[:, TB * b + t, :])
                    chain.link(ins) if t == TB - 1 else None
                nc.vector.memset(scrap[:], 0.0)
                for t in range(TB):
                    ins = nc.vector.bn_aggr(mv[:, t, :], stats[:, t, :])
                chain.link(ins)
                nc.vector.tensor_copy(var[:], mv[:, :, 1]).then_inc(s_var, 1)

            def normalise(b):
                dve.wait_ge(s_r2, b + 1)
                if not is_first(b):
                    dve.wait_ge(s_res, b)
                for t in range(TB):
                    ins = nc.vector.tensor_scalar(xn[:, t, :], x_res[:, TB * b + t, :], mv[:, t, 0:1],
                                                  rstd[:, t:t + 1], ALU.subtract, ALU.mult)
                ins.then_inc(s_xn, 1)
                if not is_first(b):
                    dve.wait_ge(s_full, full(b - 1, HT + KD - 1))
                for t in range(TB):
                    ins = nc.vector.tensor_scalar(h[:, t, :], x_res[:, TB * b + t, :], mv[:, t, 0:1],
                                                  r2[:, t:t + 1], ALU.subtract, ALU.mult)
                ins.then_inc(s_h, 1)

            def split_bc(b):
                dve.wait_ge(s_full, full(b, DBC))
                n = 2 * NS
                src = front[DBC % 2][R:R + n, :]
                chain.link(nc.vector.tensor_copy(bc3[0:n, b % 2, :], src))
                chain.link(nc.vector.tensor_tensor(rest[n:2 * n, :], src, bc3[0:n, b % 2, :], ALU.subtract))
                chain.link(nc.vector.tensor_copy(bc3[n:2 * n, b % 2, :], rest[n:2 * n, :]))
                nc.vector.tensor_tensor(bc3[2 * n:3 * n, b % 2, :], rest[n:2 * n, :], bc3[n:2 * n, b % 2, :],
                                        ALU.subtract).then_inc(s_bc3, 1)

            def softplus_in(b):
                if is_first(b):
                    dve.wait_ge(s_wd, 32)
                for m in range(KD):
                    dve.wait_ge(s_full, full(b, DT + m))
                    ins = nc.vector.tensor_scalar(delta[:, b % 2, m, :], front[(DT + m) % 2][:], dt_b[:, m:m + 1],
                                                  None, ALU.add)
                chain.link(ins)
                nc.vector.tensor_scalar(sp_in[:], delta[:, b % 2], 30.0, None, ALU.min).then_inc(s_spin, 1)

            def step_size(b):
                dve.wait_ge(s_spl, b + 1)
                nc.vector.tensor_tensor(delta[:, b % 2], delta[:, b % 2], sp_l[:], ALU.max).then_inc(s_delta, 1)
                dve.wait_ge(s_delta, b + 1)
                dve.wait_ge(s_xs, KD * (b + 1))
                nc.vector.tensor_tensor(u[:, b % 2], delta[:, b % 2], xs[:, b % 2], ALU.mult).then_inc(s_u, 1)
                chain.end()

            pieces = {0: statistics, 2: normalise, 12: split_bc, 13: softplus_in}

            def inject(b, n):
                step = NS * b + n
                if n == 0:
                    dve.wait_ge(s_u, b + 1)
                dve.wait_ge(s_B, step + 1)
                nc.vector.tensor_tensor(bx[:, n % 2], u[:, b % 2], bc_mid(Bps[:, n % 2, :], KD),
                                        ALU.mult).then_inc(s_bx, 1)

            def gate(b):
                dve.wait_ge(s_hcu, NS * (b + 1))
                for m in range(KD):
                    ins = nc.vector.scalar_tensor_tensor(y2[:, m, :], xs[:, b % 2, m, :], d_skip[:, m:m + 1],
                                                         yps[:, m, :], ALU.mult, ALU.add)
                ins.then_inc(s_y2, 1)
                dve.wait_ge(s_y2, b + 1)
                dve.wait_ge(s_sz, KD * (b + 1))
                nc.vector.tensor_tensor(g, y2[:], sz[:, b % 2], ALU.mult).then_inc(s_g, 1)

            def add_output(b):
                dve.wait_ge(s_res, b + 1)
                for j in range(KD):
                    dve.wait_ge(s_o, KD * b + j + 1)
                    rows = x_res[:, bass.ds(TB * b + 2 * j, 2), :]
                    nc.vector.tensor_tensor(rows, rows, front[1 - j][:].rearrange("p (t d) -> p t d", t=2),
                                            ALU.add).then_inc(s_xo, 1)

            def sequence(b, ahead):
                for n in range(NS):
                    step = NS * b + n
                    dve.wait_ge(s_dA, step + 1)
                    dve.wait_ge(s_bx, step + 1)
                    for m in range(KD):
                        ins = nc.vector.tensor_tensor_scan(hs[:, n % 2, m, :], dA[:, step % 3, m, :],
                                                           bx[:, n % 2, m, :], 0.0, ALU.mult, ALU.add)
                    ins.then_inc(s_scan, 1)
                    if n + 1 < NS:
                        inject(b, n + 1)
                    elif ahead:
                        step_size(b + 1)
                        inject(b + 1, 0)
                    dve.wait_ge(s_C, step + 1)
                    dve.wait_ge(s_scan, step + 1)
                    if not (is_first(b) and n < 3):
                        dve.wait_ge(s_hcu, step - 2)
                    nc.vector.tensor_tensor(hc[:, step % 3], hs[:, n % 2], bc_mid(Cps[:, n % 2, :], KD),
                                            ALU.mult).then_inc(s_hc, 1)
                    if n == 0 and not is_first(b):
                        gate(b - 1)
                    if n == 2 and not is_first(b):
                        add_output(b - 1)
                    if ahead and n in pieces:
                        pieces[n](b + 1)
                if not ahead:
                    gate(b)
                    add_output(b)

            statistics(0)
            normalise(0)
            split_bias(nc, dve, bias, s_bs)
            split.take_total(dve, Bps[:, 0, :])
            split.scales(dve)
            for j in range(len(split.signals.experts)):
                split.low(dve, j)
            split_bc(0)
            softplus_in(0)
            split.low_ssd(dve)
            step_size(0)
            inject(0, 0)
            dve.wait_ge(s_ae, 1)
            nc.vector.tensor_scalar(a_neg[:], a_exp[:], -1.0, None, ALU.mult).then_inc(s_a, 1)
            dve.wait_ge(s_wa, 32)
            sequence(0, True)
            with dve.Fori(1, NB - 1) as b:
                sequence(b, True)
            sequence(NB - 1, False)

class FfnBiases:

    def __init__(self, nc, ctx, w):
        E = w["router_w"].shape[1]
        self.w, self.E = w, E
        self.PB, self.RB = E * D, E * D + D
        self.n = E * D + D + E
        self.parts = ctx.enter_context(nc.sbuf_tensor("bias_parts", [96, self.n], BF16))
        self.loaded = ctx.enter_context(nc.semaphore("biases_loaded"))
        self.ready = ctx.enter_context(nc.semaphore("bias_parts_cleared"))
        self.whole = None

    def load(self, sp):
        w, PB, RB = self.w, self.PB, self.RB
        sp.dma_start(self.whole[0:1, 0:PB], w["expert_b"].rearrange("e d -> (e d)").unsqueeze(0)).then_inc(self.loaded, 16)
        sp.dma_start(self.whole[0:1, PB:RB], w["proj_b"].unsqueeze(0)).then_inc(self.loaded, 16)
        sp.dma_start(self.whole[0:1, RB:], w["router_b"].unsqueeze(0)).then_inc(self.loaded, 16)


def split_bias(nc, dve, bias, step):
    whole, parts = bias.whole, bias.parts
    dve.wait_ge(bias.loaded, 48)
    dve.wait_ge(bias.ready, 1)
    nc.vector.tensor_copy(parts[0:1], whole[0:1]).then_inc(step, 1)
    dve.wait_ge(step, 1)
    nc.vector.tensor_tensor(whole[32:33], whole[0:1], parts[0:1], ALU.subtract).then_inc(step, 1)
    dve.wait_ge(step, 2)
    nc.vector.tensor_copy(parts[32:33], whole[32:33]).then_inc(step, 1)
    dve.wait_ge(step, 3)
    nc.vector.tensor_tensor(parts[64:65], whole[32:33], parts[32:33], ALU.subtract)


class FfnSignals:
    EB = 2

    def __init__(self, nc, ctx, w):
        E = w["router_w"].shape[1]
        self.experts = [ctx.enter_context(nc.semaphore(f"experts_{j}_loaded")) for j in range(E // self.EB)]
        self.router = ctx.enter_context(nc.semaphore("router_loaded"))
        self.proj = ctx.enter_context(nc.semaphore("proj_loaded"))
        self.norm = ctx.enter_context(nc.semaphore("norm_loaded"))
        self.whole = ctx.enter_context(nc.semaphore("whole_weights_loaded"))
        self.split = ctx.enter_context(nc.semaphore("experts_split"))
        self.kept = ctx.enter_context(nc.semaphore("experts_kept"))


class Scales:
    NORM, Z_UP = 2.0 ** 14, 2.0 ** 10

    def __init__(self, nc, ctx):
        self.back = ctx.enter_context(nc.sbuf_tensor("scale_back", [P, 2], F32))
        self.bias_up = ctx.enter_context(nc.sbuf_tensor("scale_bias_up", [96, P], BF16))


class FfnWeights:

    def __init__(self, nc, ctx, w, signals, kept, turn):
        E, EB = w["router_w"].shape[1], signals.EB
        self.w, self.signals, self.kept, self.turn = w, signals, kept, turn

        def sb(name, shape, dt=F32):
            return ctx.enter_context(nc.sbuf_tensor(f"f{turn}_{name}", shape, dt))

        self.parts = sb("parts", [P, E // EB, 2, KD, EB * D], F16)
        self.w_r = sb("w_r", [P, KD, E])
        self.w_p = sb("w_p", [P, KD, D])
        self.norm_w = sb("norm_w", [P, D])

    def load(self, sp):
        w, signals = self.w, self.signals
        sp.dma_start(self.w_r[:], w["router_w"].rearrange("(k p) e -> p k e", p=P)).then_inc(signals.router, 16)
        if self.turn == 2:
            for j, loaded in enumerate(signals.experts):
                sp.dma_start(self.parts[:, j], self.kept[j]).then_inc(loaded, 16)
        sp.dma_start(self.w_p[:], w["proj_w"].rearrange("(k p) n -> p k n", p=P)).then_inc(signals.proj, 16)
        sp.dma_start(self.norm_w[:], w["norm_w"].partition_broadcast(P)).then_inc(signals.norm, 16)


class WeightSplit:

    def __init__(self, nc, ctx, weights, ssd, scale, bias):
        self.nc, self.weights, self.ssd, self.scale = nc, weights, ssd, scale
        self.signals, self.NB_ = weights.signals, len(weights.signals.experts)
        E, EB = bias.E, weights.signals.EB

        def sb(name, shape):
            return ctx.enter_context(nc.sbuf_tensor("split_" + name, shape, F32))

        def sem(name):
            return ctx.enter_context(nc.semaphore("split_" + name))

        self.whole = sb("whole", [P, E // EB, KD, EB, D])
        self.squares = sb("squares", [P, E // EB + KD])
        self.ones = sb("ones", [P, P])
        self.total = sb("total", [P, 2])
        self.root = sb("root", [P, 2])
        self.half = sb("half", [P, 2])
        self.up_short = ctx.enter_context(nc.sbuf_tensor("split_up_short", [P, 2], BF16))
        self.up = sb("up", [P, 2])
        self.up_all = sb("up_all", [P, 2])
        self.s_const = sem("constants_ready")
        self.s_sq = sem("squares_ready")
        self.s_sum = sem("sum_full")
        self.s_step = sem("vector_step")
        self.s_root = sem("root_ready")
        self.s_hi = sem("hi_ready")

    def load(self, sp):
        for j in range(self.NB_):
            for k in range(KD):
                e = slice(j * self.signals.EB, (j + 1) * self.signals.EB)
                sp.dma_start(self.whole[:, j, k], self.weights.w["expert_w"].rearrange(
                    "e (k p) n -> k p e n", p=P)[k, :, e]).then_inc(self.signals.whole, 16)
        for k in range(KD):
            sp.dma_start(self.ssd.whole[:, k], self.ssd.w["W_in"][k * P:(k + 1) * P, :]).then_inc(self.signals.whole, 16)

    def keep(self, sp):
        sp.wait_ge(self.signals.split, self.NB_)
        for j in range(self.NB_):
            sp.dma_start(self.weights.kept[j], self.weights.parts[:, j]).then_inc(self.signals.kept, 16)
        sp.wait_ge(self.signals.kept, 16 * self.NB_)

    def constants(self):
        self.nc.gpsimd.memset(self.ones[:], 1.0).then_inc(self.s_const, 1)
        self.nc.gpsimd.memset(self.half[:], -0.5).then_inc(self.s_const, 1)

    def square(self, act):
        act.wait_ge(self.signals.whole, 16 * (self.NB_ + 1) * KD)
        for k in range(KD):
            self.nc.scalar.activation(self.ssd.parts[:, k, 0], self.ssd.whole[:, k], ACT.Square,
                                      accum_out=self.squares[:, self.NB_ + k:self.NB_ + k + 1])
        for j in range(self.NB_):
            ins = self.nc.scalar.activation(
                self.weights.parts[:, j, 0].rearrange("p k n -> p (k n)"),
                self.whole[:, j].rearrange("p k e n -> p (k e n)"), ACT.Square, accum_out=self.squares[:, j:j + 1])
        ins.then_inc(self.s_sq, 1)

    def add_up(self, pe, bank):
        pe.wait_ge(self.s_const, 2)
        pe.wait_ge(self.s_sq, 1)
        self.nc.tensor.matmul(bank[:, 0:self.NB_ + KD], self.ones[:], self.squares[:], start=True,
                              stop=True).then_inc(self.s_sum, 1)

    def take_total(self, dve, bank):
        dve.wait_ge(self.s_sum, 1)
        self.nc.vector.tensor_reduce(self.total[:, 0:1], bank[:, 0:self.NB_], AX, ALU.add)
        self.nc.vector.tensor_reduce(self.total[:, 1:2], bank[:, self.NB_:self.NB_ + KD], AX,
                                     ALU.add).then_inc(self.s_step, 1)
        dve.wait_ge(self.s_step, 1)
        self.nc.vector.tensor_scalar(self.total[:], self.total[:], 1e-30, None, ALU.max).then_inc(self.s_step, 1)

    def take_root(self, pool):
        pool.wait_ge(self.s_const, 2)
        pool.wait_ge(self.s_step, 2)
        self.nc.gpsimd.tensor_tensor(self.root[:], self.total[:], self.half[:], ALU.pow).then_inc(self.s_root, 1)

    def scales(self, dve):
        norm, z_up = self.scale.NORM, self.scale.Z_UP
        dve.wait_ge(self.s_root, 1)
        self.nc.vector.tensor_scalar(self.up_short[:], self.root[:], norm, None, ALU.mult).then_inc(self.s_step, 1)
        dve.wait_ge(self.s_step, 3)
        self.nc.vector.tensor_copy(self.up[:], self.up_short[:])
        self.nc.vector.tensor_scalar(self.up_all[:], self.up_short[:], z_up, None, ALU.mult).then_inc(self.s_step, 1)
        dve.wait_ge(self.s_step, 4)
        self.nc.vector.reciprocal(self.scale.back[:], self.up_all[:])
        self.nc.vector.tensor_scalar(self.scale.bias_up[:], self.ones[0:96], self.up_all[0:96, 0:1], None, ALU.mult)

    def high(self, act):
        act.wait_ge(self.s_step, 4)
        for j in range(self.NB_):
            self.nc.scalar.activation(self.weights.parts[:, j, 0].rearrange("p k n -> p (k n)"),
                                      self.whole[:, j].rearrange("p k e n -> p (k e n)"), ACT.Copy,
                                      scale=self.up[:, 0:1]).then_inc(self.s_hi, 1)

    def low(self, dve, j):
        dve.wait_ge(self.s_hi, j + 1)
        self.nc.vector.scalar_tensor_tensor(
            self.weights.parts[:, j, 1].rearrange("p k n -> p (k n)"),
            self.whole[:, j].rearrange("p k e n -> p (k e n)"), self.up[:, 0:1],
            self.weights.parts[:, j, 0].rearrange("p k n -> p (k n)"), ALU.mult,
            ALU.subtract).then_inc(self.signals.split, 1)

    def high_ssd(self, act):
        for k in range(KD):
            self.nc.scalar.activation(self.ssd.parts[:, k, 0], self.ssd.whole[:, k], ACT.Copy,
                                      scale=self.up[:, 1:2]).then_inc(self.s_hi, 1)

    def low_ssd(self, dve):
        dve.wait_ge(self.s_hi, self.NB_ + KD)
        for k in range(KD):
            self.nc.vector.scalar_tensor_tensor(self.ssd.parts[:, k, 1], self.ssd.whole[:, k], self.up[:, 1:2],
                                                self.ssd.parts[:, k, 0], ALU.mult, ALU.subtract)


def phase_ffn(nc, x_res, ident, bias, weights, scale, load_now, tag, out=None):
    RMS_EPS = 1e-6
    E, EB = bias.E, weights.signals.EB
    signals, LOADED = weights.signals, 16 * weights.turn
    NBANK = E // EB
    used = []
    PB, RB, bias3 = bias.PB, bias.RB, bias.parts
    w_r, w_p, norm_w = weights.w_r, weights.w_p, weights.norm_w
    with ExitStack() as ctx:
        def sb(name, shape, dt=F32):
            return ctx.enter_context(nc.sbuf_tensor(tag + name, shape, dt))

        def ps(name, shape):
            return ctx.enter_context(nc.psum_tensor(tag + name, shape, F32))

        def sem(name):
            used.append(nc.alloc_semaphore(name=tag + name))
            return used[-1]

        ones = sb("ones", [96, P], BF16)
        before = sb("before", [P, E, E])
        half = sb("half", [P, TB])
        eps = sb("eps", [P, TB])
        rms_eps = sb("rms_eps", [P, 1])
        per_d = sb("per_d", [P, 1])

        stats = sb("stats", [P, TB, 6])
        scrap = sb("scrap", [P, 1])
        mv = sb("mv", [P, TB, 2])
        ve = sb("ve", [P, TB])
        rstd = sb("rstd", [P, TB])
        z = sb("z", [P, TB, D])
        zT = sb("zT", [P, 2, KD, P])
        zh = sb("zh", [P, 2, KD, P], F16)
        zl = sb("zl", [P, 2, KD, P], F16)
        lg = sb("lg", [P, 2, E])
        above = sb("above", [P, E, E])
        equal = sb("equal", [P, E, E])
        rank = sb("rank", [P, 2, E])
        picked = sb("picked", [P, E])
        mid = sb("mid", [P, 2])
        th = sb("th", [P, 2, E])
        wt = sb("wt", [P, E])
        gate = sb("gate", [P, 2, E])
        s = sb("s", [P, 2, E, D])
        acc = sb("acc", [P, 2, D])
        cT = sb("cT", [P, 2, KD, P])
        y = sb("y", [P, 2, D])
        sq = sb("sq", [P, D])
        ss = sb("ss", [P, 2])
        ms = sb("ms", [P, 2])
        rr = sb("rr", [P, 2])
        o = sb("o", [P, 2, D])

        hps = ps("hps", [P, NBANK, EB * D])
        zps = ps("zps", [P, KD, P])
        rps = ps("rps", [P, 2, E])
        cps = ps("cps", [P, KD, P])
        ops = ps("ops", [P, D])

        s_const = sem("constants_ready")
        s_var = sem("var_ready")
        s_rstd = sem("rstd_ready")
        s_pool = sem("pool_step")
        s_z = sem("z_ready")
        s_zt = sem("z_turned")
        s_zT = sem("zT_ready")
        s_zl = sem("zl_ready")
        s_r = sem("logits_full")
        s_v = sem("vector_step")
        s_route = sem("route_step")
        s_part = sem("combine_step")
        s_mid = sem("mid_ready")
        s_th = sem("tanh_ready")
        s_gate = sem("gate_ready")
        s_h = sem("experts_full")
        s_s = sem("silu_ready")
        s_acc = sem("combined_ready")
        s_ct = sem("combined_turned")
        s_cT = sem("cT_ready")
        s_o = sem("out_full")
        s_y = sem("y_ready")
        s_ss = sem("ss_ready")
        s_rr = sem("rr_ready")
        s_x = sem("x_updated")
        s_out = sem("out_stored")

        block = ctx.enter_context(nc.Block())

        def is_first(t):
            return isinstance(t, int) and t == 0

        @block.sync
        def _(sp):
            if load_now:
                weights.load(sp)
            if out is not None:
                rows = out.rearrange("b (t p) d -> p (b t) d", p=P)
                ends = (TB, 2 * TB, 3 * TB, NT - 1, NT)
                for first, end in zip((0,) + ends, ends):
                    sp.wait_ge(s_x, end)
                    sp.dma_start(rows[:, first:end], x_res[:, first:end, :]).then_inc(s_out, 16)
                sp.wait_ge(s_out, 16 * len(ends))

        @block.gpsimd
        def _(pool):
            nc.gpsimd.memset(half[:], -0.5).then_inc(s_const, 1)
            nc.gpsimd.memset(eps[:], LN_EPS).then_inc(s_const, 1)
            nc.gpsimd.memset(rms_eps[:], RMS_EPS).then_inc(s_const, 1)
            nc.gpsimd.memset(per_d[:], 1.0 / D).then_inc(s_const, 1)
            nc.gpsimd.memset(ones[:], 1.0).then_inc(s_const, 1)
            nc.gpsimd.memset(ss[:], 0.0).then_inc(s_const, 1)
            nc.gpsimd.memset(mid[:], 0.0).then_inc(s_const, 1)
            nc.gpsimd.memset(before[:], 1.0).then_inc(s_const, 1)
            pool.wait_ge(s_const, 8)
            nc.gpsimd.affine_select(out=before[:], in_=before[:], compare_op=ALU.is_gt, fill=0.0, base=0,
                                    pattern=[[1, E], [-1, E]], channel_multiplier=0).then_inc(s_const, 1)
            chain = Chain(pool, s_pool, 1 + 2 * TB)

            def scales(g):
                pool.wait_ge(s_var, g + 1)
                chain.link(nc.gpsimd.tensor_tensor(ve[:], mv[:, :, 1], eps[:], ALU.add))
                nc.gpsimd.tensor_tensor(rstd[:], ve[:], half[:], ALU.pow).then_inc(s_rstd, 1)

            def rms(tile, q):
                pool.wait_ge(s_ss, tile + 1)
                chain.link(nc.gpsimd.tensor_tensor(ms[:, q:q + 1], ss[:, q:q + 1], per_d[:], ALU.mult))
                chain.link(nc.gpsimd.tensor_tensor(ms[:, q:q + 1], ms[:, q:q + 1], rms_eps[:], ALU.add))
                nc.gpsimd.tensor_tensor(rr[:, q:q + 1], ms[:, q:q + 1], half[:, 0:1], ALU.pow).then_inc(s_rr, 1)

            def group(g, ahead):
                chain.begin(g)
                chain.base = 1 if is_first(g) else chain.base - 1
                for t in range(TB):
                    if t == TB - 2 and ahead:
                        scales(g + 1)
                    if not (is_first(g) and t == 0):
                        rms(TB * g + t - 1, (t - 1) % 2)
                if not ahead:
                    rms(TB * g + t, t % 2)

            chain.begin(0)
            scales(0)
            group(0, True)
            with pool.Fori(1, NB - 1) as g:
                group(g, True)
            group(NB - 1, False)

        @block.tensor
        def _(pe):
            def turn_z(tile, q):
                pe.wait_ge(s_z, tile + 1)
                if not is_first(tile):
                    pe.wait_ge(s_zT, tile)
                for k in range(KD):
                    mm = nc.tensor.transpose(zps[:, k, :], z[:, q, k * P:(k + 1) * P], ident[:])
                mm.then_inc(s_zt, 1)

            def router(tile, q):
                pe.wait_ge(s_zT, tile + 1)
                if is_first(tile):
                    pe.wait_ge(signals.router, LOADED)
                for k in range(KD):
                    nc.tensor.matmul(rps[:, q, :], zT[:, q, k, :], w_r[:, k, :], start=(k == 0), stop=False)
                nc.tensor.matmul(rps[:, q, :], ones[:], bias3[:, RB:], start=False, stop=True).then_inc(s_r, 1)

            def experts(tile, q, j):
                if not is_first(tile):
                    pe.wait_ge(s_s, NBANK * tile + j - NBANK + 1)
                else:
                    if load_now:
                        pe.wait_ge(signals.experts[j], 16)
                if j == 0:
                    pe.wait_ge(s_zl, tile + 1)
                cols = slice(EB * D * j, EB * D * (j + 1))
                for k in range(KD):
                    for z_part, w_part in ((zh, 0), (zh, 1), (zl, 0)):
                        nc.tensor.matmul(hps[:, j, :], z_part[:, q, k, :], weights.parts[:, j, w_part, k, :],
                                         start=(k == 0 and z_part is zh and w_part == 0), stop=False)
                nc.tensor.matmul(hps[:, j, :], scale.bias_up[:], bias3[:, cols], start=False, stop=True).then_inc(s_h, 1)

            def turn_combined(tile, q):
                pe.wait_ge(s_acc, tile + 1)
                for k in range(KD):
                    mm = nc.tensor.transpose(cps[:, k, :], acc[:, q, k * P:(k + 1) * P], ident[:])
                mm.then_inc(s_ct, 1)

            def project(tile, q):
                pe.wait_ge(s_cT, tile + 1)
                if not is_first(tile):
                    pe.wait_ge(s_y, tile)
                else:
                    pe.wait_ge(signals.proj, LOADED)
                for k in range(KD):
                    nc.tensor.matmul(ops[:], cT[:, q, k, :], w_p[:, k, :], start=(k == 0), stop=False)
                nc.tensor.matmul(ops[:], ones[:], bias3[:, PB:RB], start=False, stop=True).then_inc(s_o, 1)

            def group(g, last):
                for t in range(TB):
                    tile, q = TB * g + t, t % 2
                    started = not (is_first(g) and t == 0)
                    ahead = not (last and t == TB - 1)
                    for j in range(NBANK):
                        experts(tile, q, j)
                        if j == 1 and ahead:
                            turn_z(tile + 1, (t + 1) % TB)
                        if j == 2 and started:
                            turn_combined(tile - 1, (t - 1) % 2)
                        if j == 2 and ahead:
                            router(tile + 1, (t + 1) % 2)
                        if j == 3 and started:
                            project(tile - 1, (t - 1) % 2)
                if last:
                    turn_combined(tile, q)
                    project(tile, q)

            pe.wait_ge(s_const, 9)
            turn_z(0, 0)
            router(0, 0)
            group(0, False)
            with pe.Fori(1, NB - 1) as g:
                group(g, False)
            group(NB - 1, True)

        @block.scalar
        def _(act):
            def take_zT(tile, q):
                act.wait_ge(s_zt, tile + 1)
                nc.scalar.activation(zh[:, q], zps[:], ACT.Copy, scale=scale.Z_UP)
                nc.scalar.activation(zT[:, q], zps[:], ACT.Copy).then_inc(s_zT, 1)

            def tanh(tile, q):
                act.wait_ge(s_mid, tile + 1)
                nc.scalar.activation(th[:, q, :], lg[:, q, :], ACT.Tanh, bias=mid[:, q:q + 1],
                                     scale=-2.0).then_inc(s_th, 1)

            def silu(tile, q, j):
                act.wait_ge(s_h, NBANK * tile + j + 1)
                if not (isinstance(tile, int) and tile < 2):
                    act.wait_ge(s_acc, tile - 1)
                nc.scalar.activation(s[:, q, EB * j:EB * (j + 1), :].rearrange("p e n -> p (e n)"),
                                     hps[:, j, :], ACT.Silu, scale=scale.back[:, 0:1]).then_inc(s_s, 1)

            def take_cT(tile, q):
                act.wait_ge(s_ct, tile + 1)
                nc.scalar.activation(cT[:, q], cps[:], ACT.Copy).then_inc(s_cT, 1)

            def square(tile, q):
                act.wait_ge(s_y, tile + 1)
                if is_first(tile):
                    act.wait_ge(s_const, 9)
                nc.scalar.activation(sq[:], y[:, q, :], ACT.Square, accum_out=ss[:, q:q + 1]).then_inc(s_ss, 1)

            def group(g, last):
                for t in range(TB):
                    tile, q = TB * g + t, t % 2
                    started = not (is_first(g) and t == 0)
                    for j in range(NBANK):
                        silu(tile, q, j)
                        if j == 0:
                            tanh(tile, q)
                        if j == 1 and not (last and t == TB - 1):
                            take_zT(tile + 1, (t + 1) % 2)
                        if j == 2 and started:
                            take_cT(tile - 1, (t - 1) % 2)
                    if not (is_first(g) and t < 2):
                        square(tile - 2, q)
                if last:
                    take_cT(tile, q)
                    square(tile - 1, 1 - q)
                    square(tile, q)

            take_zT(0, 0)
            group(0, False)
            with act.Fori(1, NB - 1) as g:
                group(g, False)
            group(NB - 1, True)

        @block.vector
        def _(dve):
            chain = Chain(dve, s_v, TB + 1)
            routing = Chain(dve, s_route, TB * 6)
            parts = Chain(dve, s_part, TB * (E - 1))

            def statistics(g):
                for t in range(TB):
                    ins = nc.vector.bn_stats(stats[:, t, :], x_res[:, TB * g + t, :])
                chain.link(ins)
                nc.vector.memset(scrap[:], 0.0)
                for t in range(TB):
                    ins = nc.vector.bn_aggr(mv[:, t, :], stats[:, t, :])
                ins.then_inc(s_var, 1)

            def normalise(tile, t, g):
                if t == 0:
                    dve.wait_ge(s_rstd, g + 1)
                nc.vector.tensor_scalar(z[:, t, :], x_res[:, tile, :], mv[:, t, 0:1], rstd[:, t:t + 1],
                                        ALU.subtract, ALU.mult).then_inc(s_z, 1)

            def route(tile, q, step):
                other, own = bc_mid(lg[:, q, :], E), bc_last(lg[:, q, :], E)
                if step == 0:
                    dve.wait_ge(s_r, tile + 1)
                    if is_first(tile):
                        dve.wait_ge(s_const, 9)
                    routing.mark(nc.vector.tensor_scalar(lg[:, q, :], rps[:, q, :], -0.5, None, ALU.mult))
                else:
                    routing.wait()
                if step == 1:
                    nc.vector.tensor_tensor(above[:], other, own, ALU.is_lt)
                    routing.mark(nc.vector.tensor_tensor(equal[:], other, own, ALU.is_equal))
                if step == 2:
                    routing.mark(nc.vector.tensor_tensor(equal[:], equal[:], before[:], ALU.mult))
                if step == 3:
                    routing.mark(nc.vector.tensor_tensor(above[:], above[:], equal[:], ALU.add))
                if step == 4:
                    routing.mark(nc.vector.tensor_reduce(rank[:, q, :], above[:], AX, ALU.add))
                if step == 5:
                    nc.vector.scalar_tensor_tensor(picked[:], rank[:, q, :], 2.0, lg[:, q, :], ALU.is_lt, ALU.mult,
                                                   accum_out=mid[:, q:q + 1]).then_inc(s_mid, 1)

            def weigh(tile, q):
                dve.wait_ge(s_th, tile + 1)
                routing.link(nc.vector.tensor_scalar(wt[:], th[:, q, :], 0.5, 0.5, ALU.mult, ALU.add))
                nc.vector.scalar_tensor_tensor(gate[:, q, :], rank[:, q, :], 2.0, wt[:], ALU.is_lt,
                                               ALU.mult).then_inc(s_gate, 1)

            def rest_of_z(tile, q):
                dve.wait_ge(s_zT, tile + 1)
                nc.vector.scalar_tensor_tensor(zl[:, q], zT[:, q], scale.Z_UP, zh[:, q], ALU.mult,
                                               ALU.subtract).then_inc(s_zl, 1)

            def combine(tile, q, e):
                if e == 0:
                    if not (isinstance(tile, int) and tile < 2):
                        dve.wait_ge(s_ct, tile - 1)
                    dve.wait_ge(s_gate, tile + 1)
                else:
                    parts.wait()
                if e % EB == 0:
                    dve.wait_ge(s_s, NBANK * tile + e // EB + 1)
                if e == 0:
                    ins = nc.vector.tensor_scalar(acc[:, q, :], s[:, q, e, :], gate[:, q, e:e + 1], None, ALU.mult)
                else:
                    ins = nc.vector.scalar_tensor_tensor(acc[:, q, :], s[:, q, e, :], gate[:, q, e:e + 1],
                                                         acc[:, q, :], ALU.mult, ALU.add)
                if e < E - 1:
                    parts.mark(ins)
                else:
                    ins.then_inc(s_acc, 1)

            def add_input(tile, q, t):
                dve.wait_ge(s_o, tile + 1)
                nc.vector.tensor_tensor(y[:, q, :], ops[:], z[:, t, :], ALU.add).then_inc(s_y, 1)

            def finish(tile, q):
                dve.wait_ge(s_rr, tile + 1)
                if is_first(tile):
                    dve.wait_ge(signals.norm, LOADED)
                chain.link(nc.vector.scalar_tensor_tensor(o[:, q, :], y[:, q, :], rr[:, q:q + 1], norm_w[:],
                                                          ALU.mult, ALU.mult))
                nc.vector.tensor_tensor(x_res[:, tile, :], x_res[:, tile, :], o[:, q, :], ALU.add).then_inc(s_x, 1)

            def group(g, last):
                chain.begin(g)
                chain.base = 1 if is_first(g) else chain.base - 1
                routing.begin(g)
                routing.base = routing.base + 5
                parts.begin(g)
                for t in range(TB):
                    tile, q = TB * g + t, t % 2
                    ahead = not (last and t == TB - 1)
                    two_back = not (is_first(g) and t < 2)
                    if ahead:
                        normalise(tile + 1, (t + 1) % TB, g + (t + 1) // TB)
                    if t == TB - 2 and not last:
                        statistics(g + 1)
                    weigh(tile, q)
                    for e in range(E):
                        if e == 3 and ahead:
                            rest_of_z(tile + 1, 1 - q)
                        combine(tile, q, e)
                        if e == 0 and two_back:
                            add_input(tile - 2, q, (t - 2) % TB)
                        if e >= 3 and ahead:
                            route(tile + 1, 1 - q, e - 3)
                    if ahead:
                        route(tile + 1, 1 - q, 5)
                    if two_back:
                        finish(tile - 2, q)
                if last:
                    add_input(tile - 1, 1 - q, t - 1)
                    finish(tile - 1, 1 - q)
                    add_input(tile, q, t)
                    finish(tile, q)

            chain.begin(0)
            routing.begin(0)
            statistics(0)
            normalise(0, 0, 0)
            rest_of_z(0, 0)
            for step in range(6):
                route(0, 0, step)
            group(0, False)
            with dve.Fori(1, NB - 1) as g:
                group(g, False)
            group(NB - 1, True)

    return used


class SsdWeights:

    def __init__(self, nc, ctx, ctx_before, w):
        self.w = w
        H, DI, NS = w["A_log"].shape[0], w["W_out"].shape[0], w["B_norm_bias"].shape[1]
        n = w["W_in"].shape[1]
        self.parts = ctx.enter_context(nc.sbuf_tensor("s_w_in_parts", [P, KD, 2, n], F16))
        self.w_out = ctx.enter_context(nc.sbuf_tensor("s_w_out", [P, DI // P, D], F32))
        self.row = ctx.enter_context(nc.sbuf_tensor("s_row", [P, 2 * H + 2 * NS], F32))
        self.whole = ctx_before.enter_context(nc.sbuf_tensor("s_w_in", [P, KD, n], F32))
        self.H, self.NS = H, NS
        self.loaded = ctx.enter_context(nc.semaphore("s_weights_loaded"))
        self.n_loads = 5

    def load(self, sp):
        w, row, H, NS, loaded = self.w, self.row, self.H, self.NS, self.loaded
        for n, name in enumerate(("A_log", "dt_bias")):
            sp.dma_start(row[:, n * H:(n + 1) * H], w[name].partition_broadcast(P)).then_inc(loaded, 16)
        for n, name in enumerate(("B_norm_bias", "C_norm_bias")):
            sp.dma_start(row[:, 2 * H + n * NS:2 * H + (n + 1) * NS],
                         w[name].rearrange("g n -> (g n)").partition_broadcast(P)).then_inc(loaded, 16)
        sp.dma_start(self.w_out[:], w["W_out"].rearrange("(g p) n -> p g n", p=P)).then_inc(loaded, 16)


def phase_ssd(nc, x_res, ident, weights, scale, retired):
    w, w_in, w_out, row = weights.w, weights.parts, weights.w_out, weights.row
    Z_UP, back = scale.Z_UP, scale.back[:, 1:2]
    H = w["A_log"].shape[0]
    DI = w["W_out"].shape[0]
    HP = DI // H
    NS = w["B_norm_bias"].shape[1]
    NR = NS // 2
    Q = 32
    NC = P // Q
    NQ = P // Q
    HG = H // NQ
    NG = DI // P
    ST = NG
    REST = 2 * NS + 2 * H + NR
    BC, DT, LAM, TH = 0, 2 * NS, 2 * NS + H, 2 * NS + 2 * H
    RMS_EPS = 1e-6
    TWO_PI_HI, ROUND = 6.28125, 12582912.0
    TWO_PI_LO = 2 * np.pi - TWO_PI_HI
    with ExitStack() as ctx:
        def sb(name, shape, dt=F32):
            return ctx.enter_context(nc.sbuf_tensor("s_" + name, shape, dt))

        def ps(name, shape):
            return ctx.enter_context(nc.psum_tensor("s_" + name, shape, F32))

        def sem(name):
            return ctx.enter_context(nc.semaphore("s_" + name))

        a_exp = sb("a_exp", [P, H])
        a_neg = sb("a_neg", [P, H])
        nbias = row[:, 2 * H:]
        half_pi = sb("half_pi", [P, 1])
        half = sb("half", [P, 2 * TB])
        eps = sb("eps", [P, TB])
        rms_eps = sb("rms_eps", [P, 2 * TB])
        per_ns = sb("per_ns", [P, 2 * TB])
        ones = sb("ones", [P, P])
        tri = sb("tri", [P, P])
        tri_c = sb("tri_c", [P, NC, Q])
        after = sb("after", [P, NC, Q])
        shift = sb("shift", [P, P])
        carry = sb("carry", [P, P])
        rep = sb("rep", [H, DI])
        in_chunk = sb("in_chunk", [P, NC])
        mask_rs = sb("mask_rs", [P, Q])
        mask_st = sb("mask_st", [P, Q])

        stats = sb("stats", [P, TB, 6])
        scrap = sb("scrap", [P, 1])
        mv = sb("mv", [P, TB, 2])
        ve = sb("ve", [P, TB])
        rstd = sb("rstd", [P, TB])
        zn = sb("zn", [P, TB, D])
        zh = sb("zh", [P, KD, T], F16)
        zl = sb("zl", [P, KD, T], F16)
        rest = sb("rest", [P, TB, REST])
        v = sb("v", [P, TB, H])
        vm = sb("vm", [P, TB, H])
        le = sb("le", [P, TB, H])
        dt = sb("dt", [P, TB, H])
        dtm = sb("dtm", [P, TB])
        th = sb("th", [P, TB, NR])
        pp = sb("pp", [P, TB, H])
        qq = v
        dA = sb("dA", [P, TB, H])
        dA2 = sb("dA2", [P, 2, TB, H])
        bsq = sb("bsq", [P, TB * 2, NS])
        bss = sb("bss", [P, TB * 2])
        bms = sb("bms", [P, TB * 2])
        brr = sb("brr", [P, TB * 2])
        bn = bsq[:].rearrange("p (t a) n -> p t a n", t=TB)
        kk = sb("kk", [P, TB, NR])
        arg = sb("arg", [P, TB, NR])
        aarg = kk
        sn = sb("sn", [P, TB, NR])
        cs = th
        rt = zn[:].rearrange("p t (i r) -> p (t i r)", r=NR).rearrange("p (k t a r) -> p k t a r", k=4, t=TB, a=2)
        br = sb("br", [P, TB, 2, NS])
        cbd = sb("cbd", [P, TB])
        bT = sb("bT", [P, T])
        cT = sb("cT", [P, 2, T])
        cbm = sb("cbm", [P, 2, T])
        bm = sb("bm", [P, 2, TB, NC, NS])
        gw = sb("gw", [P, 2, TB, H])
        ww = sb("ww", [P, 2, TB, H])
        dl = sb("dl", [P, 2, TB, H])
        xg = sb("xg", [P, 2, TB, DI])
        szT = sb("szT", [P, 2, NG, T])
        ecs = sb("ecs", [P, 2, NG, T])

        mst = sb("mst", [P, 2, H, Q])
        xbd = sb("xbd", [P, 2, NC, HG, NQ, HP])
        xw = sb("xw", [P, 2, DI])
        xdl = sb("xdl", [P, 2, DI])
        e = sb("e", [P, ST, NG, P])
        st = sb("st", [P, NG, 2 * NC, NS])
        pT = sb("pT", [P, NC // 2, DI])
        y = sb("y", [P, NG, P])
        y2 = sb("y2", [P, NG, P])
        strict = y2[:, 0, :].rearrange("p (c t) -> p c t", t=Q)
        gT = sb("gT", [P, NG, P])
        ms = sb("ms", [P, 1])
        rr = sb("rr", [P, 1])

        dps = ps("dps", [P, 2, NG, P])
        yps = ps("yps", [P, NG, P])
        ops = ps("ops", [P, NG, P])
        sps = ps("sps", [P, 2, NC, NS])
        mps = ps("mps", [P, T])
        fps = [ps(f"fps{i}", [P, T]) for i in range(2)]

        s_half = sem("half_ready")
        s_const = sem("constants_ready")
        s_mask = sem("masks_ready")
        s_ae = sem("a_exp_ready")
        s_var = sem("var_ready")
        s_pool = sem("pool_step")
        s_rstd = sem("rstd_ready")
        s_v = sem("vector_front_step")
        s_zn = sem("zn_ready")
        s_f = sem("front_full")
        s_zh = sem("zh_ready")
        s_zl = sem("zl_ready")
        s_rest = sem("rest_ready")
        s_vm = sem("vm_ready")
        s_act = sem("scalar_front_step")
        s_vl = sem("vl_ready")
        s_qq = sem("qq_ready")
        s_bss = sem("bss_ready")
        s_brr = sem("brr_ready")
        s_arg = sem("arg_ready")
        s_trig = sem("trig_ready")
        s_g = sem("g_ready")
        s_br = sem("br_ready")
        s_bT = sem("bT_ready")
        s_cbm = sem("cbm_ready")
        s_dcs = sem("dcs_ready")
        s_xg = sem("xg_ready")
        s_hcs = sem("head_decay_ready")
        s_sz = sem("sz_ready")
        s_ecs = sem("ecs_ready")
        s_front = sem("front_weights_ready")
        s_bm = sem("bm_ready")
        s_mst = sem("mst_ready")
        s_prep = sem("x_scaled")
        s_d = sem("d_full")
        s_e = sem("e_ready")
        s_em = sem("e_masked")
        s_Y = sem("y_added")
        s_S = sem("states_full")
        s_rs = sem("state_step")
        s_z0 = sem("state_cleared")
        s_pt = sem("prev_turned")
        s_pT = sem("prev_ready")
        s_yo = sem("y_off_full")
        s_t1 = sem("t1_ready")
        s_y = sem("y_ready")
        s_gT = sem("gT_ready")
        s_y2 = sem("y2_ready")
        s_half_fold = sem("y2_halved")
        s_fold = sem("y2_summed")
        s_tail = sem("tail_full")
        s_ms = sem("ms_ready")
        s_rr = sem("rr_ready")
        s_x = sem("x_updated")

        NCONST = 24
        ZT, RE, XP, CUM, QS, WC, BCT, CBT, HC, EC = 0, 2, 6, 11, 12, 13, 17, 18, 19, 20
        ZP = (10, 14, 15, 16)
        NF = 24
        was_read = ([(s_zl, KD, k + 1) for k in range(KD)] + [(s_rest, TB, t + 1) for t in range(TB)] +
                    [(s_xg, TB, t + 1) for t in range(TB)] + [(s_sz, NG, 1), (s_arg, 1, 1), (s_g, 1, 1), (s_dcs, 1, 1)] +
                    [(s_sz, NG, g + 1) for g in range(1, NG)] + [(s_bT, 4, 4), (s_cbm, 1, 1), (s_hcs, 1, 1)] +
                    [(s_ecs, NG, g + 1) for g in range(NG)])
        assert len(was_read) == NF
        nc.clear_and_free_semaphores(retired)
        block = ctx.enter_context(nc.Block())

        def is_first(n):
            return isinstance(n, int) and n == 0

        def full(b, use):
            return b * NF + use + 1

        def front(use):
            return fps[use % 2]

        def heads(ap, n=HP):
            return bc_last(ap, n)

        @block.gpsimd
        def _(pool):
            done = [0]

            def step(ins):
                done[0] += 1
                ins.then_inc(s_const, 1)

            def select(out, op, base, pattern, channel, fill=0.0):
                pool.wait_ge(s_const, done[0])
                step(nc.gpsimd.affine_select(out=out, in_=out, compare_op=op, fill=fill, base=base,
                                             pattern=pattern, channel_multiplier=channel))

            chain = Chain(pool, s_pool, 3)

            def scales(b):
                chain.begin(b)
                pool.wait_ge(s_var, b + 1)
                chain.link(nc.gpsimd.tensor_tensor(ve[:], mv[:, :, 1], eps[:], ALU.add))
                nc.gpsimd.tensor_tensor(rstd[:], ve[:], half[:, 0:TB], ALU.pow).then_inc(s_rstd, 1)

            def bc_scales(b):
                pool.wait_ge(s_bss, b + 1)
                chain.link(nc.gpsimd.tensor_tensor(bms[:], bss[:], per_ns[:], ALU.mult))
                chain.link(nc.gpsimd.tensor_tensor(bms[:], bms[:], rms_eps[:], ALU.add))
                nc.gpsimd.tensor_tensor(brr[:], bms[:], half[:], ALU.pow).then_inc(s_brr, 1)

            def spread_b(b):
                pool.wait_ge(s_br, b + 1)
                for t in range(TB):
                    ins = nc.gpsimd.tensor_tensor(bm[:, b % 2, t], bc_mid(br[:, t, 0, :], NC),
                                                  bc_last(in_chunk[:], NS), ALU.mult)
                ins.then_inc(s_bm, 1)

            def decay_operand(b, t):
                tile = TB * b + t
                pool.wait_ge(s_qq, b + 1)
                if not (isinstance(tile, int) and tile < 2):
                    pool.wait_ge(s_d, ST * tile - ST)
                nc.gpsimd.tensor_tensor(mst[:, t % 2], bc_last(dA2[:, b % 2, t, :], Q), bc_mid(mask_rs[:], H),
                                        ALU.mult).then_inc(s_mst, 1)

            def rms(tile):
                pool.wait_ge(s_ms, tile + 1)
                nc.gpsimd.tensor_tensor(rr[:], ms[:], half[:, 0:1], ALU.pow).then_inc(s_rr, 1)

            def fold(tile):
                pool.wait_ge(s_y2, tile + 1)
                nc.gpsimd.tensor_tensor(y2[:, 0:2], y2[:, 0:2], y2[:, 2:4], ALU.add).then_inc(s_half_fold, 1)
                pool.wait_ge(s_half_fold, tile + 1)
                nc.gpsimd.tensor_tensor(y2[:, 0], y2[:, 0], y2[:, 1], ALU.add).then_inc(s_fold, 1)

            def sequence(b, ahead):
                for t in range(TB):
                    tile = TB * b + t
                    if t > 1 or not is_first(b):
                        rms(tile - 2)
                    if t + 1 < TB:
                        decay_operand(b, t + 1)
                    if ahead and t == 0:
                        scales(b + 1)
                    if ahead and t == 1:
                        bc_scales(b + 1)
                    if ahead and t == 3:
                        spread_b(b + 1)
                        decay_operand(b + 1, 0)
                    if t > 0 or not is_first(b):
                        fold(tile - 1)
                if not ahead:
                    rms(tile - 1)
                    fold(tile)
                    rms(tile)

            nc.gpsimd.memset(half[:], -0.5).then_inc(s_half, 1)
            nc.gpsimd.memset(eps[:], LN_EPS).then_inc(s_half, 1)
            pool.wait_ge(s_half, 2)
            scales(0)
            for tile_, value in ((rms_eps, RMS_EPS), (per_ns, 1.0 / NS), (half_pi, np.pi / 2), (ones, 1.0),
                                 (tri, 1.0), (tri_c, 1.0), (after, 1.0), (shift, 0.0), (carry, 0.0),
                                 (in_chunk, 1.0), (xbd, 0.0), (rep, 1.0), (cT, 0.0)):
                step(nc.gpsimd.memset(tile_[:], float(value)))
            select(tri[:], ALU.is_ge, 0, [[1, P]], -1)
            select(tri_c[:], ALU.is_ge, 0, [[Q, NC], [1, Q]], -1)
            select(tri_c[:], ALU.is_ge, 0, [[-Q, NC], [0, Q]], 1)
            select(after[:], ALU.is_gt, 0, [[-Q, NC], [-1, Q]], 1)
            select(after[:], ALU.is_gt, Q, [[Q, NC], [0, Q]], -1)
            select(shift[:], ALU.not_equal, 1, [[1, P]], -1, 1.0)
            select(carry[:], ALU.not_equal, 1 - P, [[1, P]], P, 1.0)
            select(in_chunk[:], ALU.is_ge, 0, [[-Q, NC]], 1)
            select(in_chunk[:], ALU.is_ge, Q - 1, [[Q, NC]], -1)
            select(rep[:], ALU.is_ge, 0, [[1, DI]], -HP)
            select(rep[:], ALU.is_ge, HP - 1, [[-1, DI]], HP)
            assert done[0] == NCONST, done[0]
            pool.wait_ge(s_const, NCONST)
            pool.wait_ge(s_mask, 3)
            bc_scales(0)
            decay_operand(0, 0)
            spread_b(0)
            sequence(0, True)
            with pool.Fori(1, NB - 1) as b:
                sequence(b, True)
            sequence(NB - 1, False)

        @block.tensor
        def _(pe):
            PRODUCTS = [(k, z_part, part) for k in range(KD) for z_part, part in ((zh, 0), (zh, 1), (zl, 0))]

            def claim(b, use):
                if use >= 2:
                    read, per, count = was_read[use - 2]
                    pe.wait_ge(read, per * b + count)
                elif not is_first(b):
                    pe.wait_ge(s_ecs, NG * b)
                return front(use)

            def turn_zn(b, k):
                pe.wait_ge(s_zn, b + 1)
                bank = claim(b, ZT + k)
                for t in range(TB):
                    mm = nc.tensor.transpose(bank[:, t * P:(t + 1) * P], zn[:, t, k * P:(k + 1) * P], ident[:])
                mm.then_inc(s_f, 1)

            def token_proj(b, t, use, cols):
                bank = claim(b, use)
                for n, (k, z_part, part) in enumerate(PRODUCTS):
                    mm = nc.tensor.matmul(bank[:, 0:cols.stop - cols.start], z_part[:, k, t * P:(t + 1) * P],
                                          w_in[:, k, part, cols], start=(n == 0), stop=(n == len(PRODUCTS) - 1))
                mm.then_inc(s_f, 1)

            def project_rest(b, t):
                if t == 0:
                    pe.wait_ge(s_zl, KD * (b + 1))
                token_proj(b, t, RE + t, slice(2 * DI, 2 * DI + REST))

            def project_x(b, t):
                token_proj(b, t, XP + t, slice(DI, 2 * DI))

            def project_z(b, g):
                bank = claim(b, ZP[g])
                for n, (k, z_part, part) in enumerate(PRODUCTS):
                    mm = nc.tensor.matmul(bank[:], w_in[:, k, part, g * P:(g + 1) * P], z_part[:, k, :],
                                          start=(n == 0), stop=(n == len(PRODUCTS) - 1))
                mm.then_inc(s_f, 1)

            def sum_angles(b):
                pe.wait_ge(s_qq, b + 1)
                cum = claim(b, CUM)[:, 0:TB * NR].rearrange("p (t n) -> p t n", t=TB)
                nc.tensor.matmul(cum, tri[:], th[:], start=True, stop=False, skip_group_check=True)
                for j in range(TB - 1):
                    mm = nc.tensor.matmul(cum[:, j + 1:, :], ones[:], bc_mid(th[:, j, :], TB - 1 - j),
                                          start=False, stop=(j == TB - 2), skip_group_check=True)
                mm.then_inc(s_f, 1)

            def next_token(b):
                nxt = claim(b, QS)[:, 0:TB * H].rearrange("p (t h) -> p t h", t=TB)
                nc.tensor.matmul(nxt, shift[:], qq[:], start=True, stop=False, skip_group_check=True)
                nc.tensor.matmul(nxt[:, 0:TB - 1, :], carry[:], qq[:, 1:TB, :], start=False, stop=True,
                                 skip_group_check=True).then_inc(s_f, 1)

            def following_decay(b):
                nc.tensor.matmul(claim(b, WC)[:, 0:TB * H], after[:].rearrange("p c t -> p (c t)"),
                                 dA[:].rearrange("p t h -> p (t h)"), start=True, stop=True).then_inc(s_f, 1)

            def turn_bc(b):
                pe.wait_ge(s_br, b + 1)
                bank = claim(b, BCT)
                for t in range(TB):
                    mm = nc.tensor.transpose(bank[:, t * P:(t + 1) * P], br[:, t].rearrange("p a n -> p (a n)"),
                                             ident[:])
                mm.then_inc(s_f, 1)

            def c_dot_b(b):
                pe.wait_ge(s_bT, 4 * (b + 1))
                bank = claim(b, CBT)
                for t in range(TB):
                    mm = nc.tensor.matmul(bank[:, t * P:(t + 1) * P], bT[:, t * P:(t + 1) * P],
                                          cT[:, b % 2, t * P:(t + 1) * P], start=(t == 0), stop=(t == TB - 1),
                                          skip_group_check=True)
                mm.then_inc(s_f, 1)

            def running_decay(b):
                bank = claim(b, HC)
                for t in range(TB):
                    mm = nc.tensor.matmul(bank[0:H, t * P:(t + 1) * P], dA[:, t, :],
                                          tri_c[:].rearrange("p c t -> p (c t)"), start=(t == 0),
                                          stop=(t == TB - 1), skip_group_check=True)
                mm.then_inc(s_f, 1)

            def spread_decay(b, g):
                if g == 0:
                    pe.wait_ge(s_hcs, b + 1)
                nc.tensor.matmul(claim(b, EC + g)[:], rep[:, g * P:(g + 1) * P], bT[0:H, :], start=True,
                                 stop=True).then_inc(s_f, 1)

            pieces = {(2, 1): lambda b: turn_zn(b, 0), (3, 0): lambda b: turn_zn(b, 1),
                      (4, 0): lambda b: (project_rest(b, 0), project_rest(b, 1)),
                      (4, 1): lambda b: (project_rest(b, 2), project_rest(b, 3)),
                      (5, 0): lambda b: project_x(b, 0), (5, 1): lambda b: project_x(b, 1),
                      (6, 1): lambda b: project_x(b, 2), (7, 0): lambda b: project_x(b, 3),
                      (7, 1): lambda b: project_z(b, 0), (8, 0): sum_angles, (8, 1): next_token,
                      (9, 0): following_decay, (9, 1): lambda b: project_z(b, 1),
                      (10, 0): lambda b: project_z(b, 2), (10, 1): lambda b: project_z(b, 3),
                      (12, 0): turn_bc, (12, 1): lambda b: (c_dot_b(b), running_decay(b)),
                      (13, 1): lambda b: spread_decay(b, 0), (14, 0): lambda b: spread_decay(b, 1),
                      (14, 1): lambda b: spread_decay(b, 2), (15, 0): lambda b: spread_decay(b, 3)}

            def decays(tile, t, j):
                step = ST * tile + j
                if j == 0:
                    pe.wait_ge(s_mst, tile + 1)
                if not (isinstance(step, int) and step < 2):
                    pe.wait_ge(s_e, step - 1)
                for i in range(NG):
                    hg = NG * j + i
                    mm = nc.tensor.matmul(dps[:, j % 2, i, :],
                                          mst[:, t % 2, hg * NQ:(hg + 1) * NQ, :].rearrange("p h s -> p (h s)"),
                                          tri_c[:].rearrange("p c t -> p (c t)"), start=(i == 0),
                                          stop=(i == NG - 1), skip_group_check=True)
                mm.then_inc(s_d, 1)

            def own_token(tile, t):
                if not is_first(tile):
                    pe.wait_ge(s_y, tile)
                for g in range(NG):
                    nc.tensor.matmul(yps[:, g, :], xdl[:, t % 2, g * P:(g + 1) * P], ident[:],
                                     start=(g == 0), stop=False, skip_group_check=True)

            def earlier_tokens(tile, t, j):
                pe.wait_ge(s_em, ST * tile + j + 1)
                for i in range(NG):
                    for c in range(NC):
                        mm = nc.tensor.matmul(yps[i * Q:(i + 1) * Q, j, c * Q:(c + 1) * Q],
                                              xbd[:, t % 2, c, NG * j + i].rearrange("p h q -> p (h q)"),
                                              e[:, j, i, c * Q:(c + 1) * Q], start=False,
                                              stop=(j == ST - 1 and c == NC - 1), skip_group_check=True)
                mm.then_inc(s_Y, 1)

            def chunk_states(b, tile, t, pair):
                if pair == 0:
                    pe.wait_ge(s_prep, tile + 1)
                if pair == 0 and t == 0:
                    pe.wait_ge(s_bm, b + 1)
                if pair == 1 or not is_first(tile):
                    pe.wait_ge(s_rs, 2 * NC * (2 * tile + pair))
                for i in range(2):
                    g = 2 * pair + i
                    mm = nc.tensor.matmul(sps[:, i].rearrange("p c n -> p (c n)"), xw[:, t % 2, g * P:(g + 1) * P],
                                          bm[:, b % 2, t].rearrange("p c n -> p (c n)"), start=(i == 0),
                                          stop=(i == 1), skip_group_check=True)
                mm.then_inc(s_S, 1)

            def turn_prev(tile, t, pair):
                if pair == 0:
                    pe.wait_ge(s_rs, 4 * NC * tile + 2 * NC + 2)
                    if not (isinstance(tile, int) and tile < 2):
                        pe.wait_ge(s_x, tile - 1)
                else:
                    pe.wait_ge(s_rs, 4 * NC * (tile + 1))
                    if not is_first(tile):
                        pe.wait_ge(s_t1, tile)
                out = (mps, ops[:].rearrange("p g t -> p (g t)"))[pair]
                slot = NC * (t % 2) + 2 * pair
                for g in range(NG):
                    mm = nc.tensor.transpose(out[:, g * P:(g + 1) * P],
                                             st[:, g, slot:slot + 2, :].rearrange("p c n -> p (c n)"), ident[:])
                mm.then_inc(s_pt, 1)

            def earlier_chunks(b, tile, t):
                pe.wait_ge(s_pT, 2 * (tile + 1))
                for g in range(NG):
                    for pair in range(2):
                        at, n = t * P + pair * 2 * Q, 2 * Q
                        mm = nc.tensor.matmul(ops[:, g, pair * n:(pair + 1) * n], pT[:, pair, g * P:(g + 1) * P],
                                              cT[:, b % 2, at:at + n], start=(g == 0 and pair == 0),
                                              stop=(g == NG - 1 and pair == 1), skip_group_check=True)
                mm.then_inc(s_yo, 1)

            def tail(tile):
                pe.wait_ge(s_fold, tile + 1)
                nc.tensor.matmul(mps[:, D:D + 1], y2[:, 0, :], ones[:, 0:1], start=True, stop=True)
                pe.wait_ge(s_gT, tile + 1)
                for g in range(NG):
                    mm = nc.tensor.matmul(mps[:, 0:D], gT[:, g, :], w_out[:, g, :], start=(g == 0),
                                          stop=(g == NG - 1))
                mm.then_inc(s_tail, 1)

            def sequence(b, ahead):
                for t in range(TB):
                    tile = TB * b + t
                    started = not (is_first(b) and t == 0)
                    for j in range(ST):
                        piece = [pieces.get((ST * t + j, i)) if ahead else None for i in range(2)]
                        if j + 1 < ST:
                            decays(tile, t, j + 1)
                        elif t + 1 < TB or ahead:
                            decays(tile + 1, (t + 1) % TB, 0)
                        if j == 0:
                            chunk_states(b, tile, t, 0)
                            if started:
                                earlier_chunks(b if t else b - 1, tile - 1, (t - 1) % TB)
                        if j == 1:
                            chunk_states(b, tile, t, 1)
                        if piece[0]:
                            piece[0](b + 1)
                        if j >= 2:
                            turn_prev(tile, t, j - 2)
                        if j == 0 and started:
                            earlier_tokens(tile - 1, (t - 1) % TB, ST - 1)
                        if j == 2:
                            own_token(tile, t)
                            earlier_tokens(tile, t, 0)
                            earlier_tokens(tile, t, 1)
                        if j == 3:
                            earlier_tokens(tile, t, 2)
                        if j == 3 and started:
                            pe.wait_ge(s_pT, 2 * tile + 1)
                            tail(tile - 1)
                        if piece[1]:
                            piece[1](b + 1)
                if not ahead:
                    earlier_tokens(tile, t, ST - 1)
                    earlier_chunks(b, tile, t)
                    tail(tile)

            pe.wait_ge(weights.loaded, 16 * weights.n_loads)
            for piece in pieces.values():
                if piece is sum_angles:
                    pe.wait_ge(s_const, NCONST)
                if piece is turn_bc:
                    decays(0, 0, 0)
                piece(0)
            sequence(0, True)
            with pe.Fori(1, NB - 1) as b:
                sequence(b, True)
            sequence(NB - 1, False)

        @block.scalar
        def _(act):
            chain = Chain(act, s_act, 2)

            def take_zT(b, k):
                act.wait_ge(s_f, full(b, ZT + k))
                nc.scalar.activation(zh[:, k, :], front(ZT + k)[:], ACT.Copy, scale=Z_UP).then_inc(s_zh, 1)

            def take_rest(b, t):
                act.wait_ge(s_f, full(b, RE + t))
                if t == 0 and not is_first(b):
                    act.wait_ge(s_trig, b)
                nc.scalar.activation(rest[:, t, :], front(RE + t)[:, 0:REST], ACT.Copy,
                                     scale=back).then_inc(s_rest, 1)

            def exps(b):
                act.wait_ge(s_vm, b + 1)
                chain.link(nc.scalar.activation(vm[:], vm[:], ACT.Exp))
                nc.scalar.activation(vm[:], vm[:], ACT.Ln, bias=1.0).then_inc(s_vl, 1)

            def tanh(b):
                chain.begin(b)
                act.wait_ge(s_rest, TB * (b + 1))
                nc.scalar.activation(le[:], rest[:, :, LAM:LAM + H], ACT.Tanh, scale=0.5)

            def take_x(b, t):
                act.wait_ge(s_f, full(b, XP + t))
                nc.scalar.activation(xg[:, b % 2, t, :], front(XP + t)[:], ACT.Silu, scale=back).then_inc(s_xg, 1)

            def trig(b):
                act.wait_ge(s_arg, b + 1)
                nc.scalar.activation(sn[:], arg[:], ACT.Sin)
                chain.link(nc.scalar.activation(aarg[:], arg[:], ACT.Abs))
                nc.scalar.activation(cs[:], aarg[:], ACT.Sin, bias=half_pi[:], scale=-1.0).then_inc(s_trig, 1)

            def chunk_decay(b):
                act.wait_ge(s_f, full(b, WC))
                nc.scalar.activation(ww[:, b % 2].rearrange("p t h -> p (t h)"), front(WC)[:, 0:TB * H],
                                     ACT.Exp).then_inc(s_dcs, 1)

            def take_z(b, g):
                act.wait_ge(s_f, full(b, ZP[g]))
                nc.scalar.activation(szT[:, b % 2, g, :], front(ZP[g])[:], ACT.Silu,
                                     scale=back).then_inc(s_sz, 1)

            def take_bc(b):
                act.wait_ge(s_f, full(b, BCT))
                bank = front(BCT)
                for i in range(2):
                    half_ = slice(i * NS, (i + 1) * NS)
                    nc.scalar.activation(bT[half_, :], bank[0:NS, :], ACT.Copy).then_inc(s_bT, 1)
                    nc.scalar.activation(cT[half_, b % 2, :].rearrange("p (c i t) -> p c i t", i=2, t=Q)[:, :, i],
                                         bank[NS:2 * NS, :].rearrange("p (c i t) -> p c i t", i=2, t=Q)[:, :, i],
                                         ACT.Copy).then_inc(s_bT, 1)

            def take_head_decay(b):
                act.wait_ge(s_f, full(b, HC))
                nc.scalar.activation(bT[0:H, :], front(HC)[0:H, :], ACT.Exp).then_inc(s_hcs, 1)

            def take_decay(b, g):
                act.wait_ge(s_f, full(b, EC + g))
                nc.scalar.activation(ecs[:, b % 2, g, :], front(EC + g)[:], ACT.Copy).then_inc(s_ecs, 1)

            pieces = {(2, 1): lambda b: take_zT(b, 0), (3, 0): lambda b: take_zT(b, 1),
                      (4, 0): lambda b: (take_rest(b, 0), take_rest(b, 1)),
                      (4, 1): lambda b: (take_rest(b, 2), take_rest(b, 3)),
                      (5, 0): lambda b: (tanh(b), take_x(b, 0)), (5, 1): lambda b: take_x(b, 1),
                      (6, 0): exps, (6, 1): lambda b: take_x(b, 2), (7, 0): lambda b: take_x(b, 3),
                      (7, 1): lambda b: take_z(b, 0), (9, 0): chunk_decay,
                      (9, 1): lambda b: (trig(b), take_z(b, 1)),
                      (10, 0): lambda b: take_z(b, 2), (10, 1): lambda b: take_z(b, 3),
                      (12, 0): take_bc, (13, 0): take_head_decay,
                      (13, 1): lambda b: take_decay(b, 0), (14, 0): lambda b: take_decay(b, 1),
                      (14, 1): lambda b: take_decay(b, 2), (15, 0): lambda b: take_decay(b, 3)}

            def decay(tile, j):
                step = ST * tile + j
                act.wait_ge(s_d, step + 1)
                if not is_first(tile):
                    act.wait_ge(s_Y, step - ST + 1)
                nc.scalar.activation(e[:, j].rearrange("p g t -> p (g t)"),
                                     dps[:, j % 2].rearrange("p g t -> p (g t)"), ACT.Exp).then_inc(s_e, 1)

            def take_prev(tile, pair):
                act.wait_ge(s_pt, 2 * tile + pair + 1)
                if pair == 0 and not is_first(tile):
                    act.wait_ge(s_yo, tile)
                src = (mps, ops[:].rearrange("p g t -> p (g t)"))[pair]
                nc.scalar.activation(pT[:, pair, :], src[:], ACT.Copy).then_inc(s_pT, 1)

            def square(tile):
                act.wait_ge(s_y, tile + 1)
                if not is_first(tile):
                    act.wait_ge(s_tail, tile)
                nc.scalar.activation(y2[:], y[:], ACT.Square).then_inc(s_y2, 1)

            def sequence(b, ahead):
                for t in range(TB):
                    tile = TB * b + t
                    started = not (is_first(b) and t == 0)
                    for j in range(ST):
                        piece = [pieces.get((ST * t + j, i)) if ahead else None for i in range(2)]
                        decay(tile, j)
                        if piece[0]:
                            piece[0](b + 1)
                        if j >= 2:
                            take_prev(tile, j - 2)
                        if j == 2 and started:
                            square(tile - 1)
                        if piece[1]:
                            piece[1](b + 1)
                if not ahead:
                    square(tile)

            act.wait_ge(weights.loaded, 16 * weights.n_loads)
            nc.scalar.activation(a_exp[:], row[:, 0:H], ACT.Exp).then_inc(s_ae, 1)
            for piece in pieces.values():
                if piece is chunk_decay:
                    act.wait_ge(s_const, NCONST)
                piece(0)
            sequence(0, True)
            with act.Fori(1, NB - 1) as b:
                sequence(b, True)
            sequence(NB - 1, False)

        @block.vector
        def _(dve):
            chain = Chain(dve, s_v, 16)

            def statistics(b):
                chain.begin(b)
                for t in range(TB):
                    ins = nc.vector.bn_stats(stats[:, t, :], x_res[:, TB * b + t, :])
                chain.link(ins)
                nc.vector.memset(scrap[:], 0.0)
                for t in range(TB):
                    ins = nc.vector.bn_aggr(mv[:, t, :], stats[:, t, :])
                ins.then_inc(s_var, 1)

            def normalise(b):
                dve.wait_ge(s_rstd, b + 1)
                for t in range(TB):
                    ins = nc.vector.tensor_scalar(zn[:, t, :], x_res[:, TB * b + t, :], mv[:, t, 0:1],
                                                  rstd[:, t:t + 1], ALU.subtract, ALU.mult)
                ins.then_inc(s_zn, 1)

            def rest_of_z(b, k):
                dve.wait_ge(s_zh, KD * b + k + 1)
                nc.vector.scalar_tensor_tensor(zl[:, k, :], front(ZT + k)[:], Z_UP, zh[:, k, :], ALU.mult,
                                               ALU.subtract).then_inc(s_zl, 1)

            def raw(b):
                dve.wait_ge(s_rest, TB * (b + 1))
                chain.link(nc.vector.tensor_tensor(v[:], rest[:, :, DT:DT + H], bc_mid(row[:, H:2 * H], TB), ALU.add))
                nc.vector.tensor_scalar(vm[:], v[:], 30.0, None, ALU.min).then_inc(s_vm, 1)
                bc = rest[:, :, 0:2 * NS]
                chain.link(nc.vector.tensor_tensor(bsq[:].rearrange("p (t a) n -> p t (a n)", t=TB), bc, bc, ALU.mult))
                nc.vector.tensor_reduce(bss[:], bsq[:], AX, ALU.add).then_inc(s_bss, 1)

            def rates(b):
                dve.wait_ge(s_vl, b + 1)
                nc.vector.tensor_tensor(dt[:], v[:], vm[:], ALU.max)
                chain.link(nc.vector.tensor_scalar(le[:], le[:], 0.5, 0.5, ALU.mult, ALU.add))
                chain.link(nc.vector.tensor_scalar(dt[:], dt[:], 1e-4, 0.5, ALU.max, ALU.min))
                nc.vector.tensor_tensor(dA[:], dt[:], bc_mid(a_neg[:], TB), ALU.mult)
                nc.vector.tensor_reduce(dtm[:], dt[:], AX, ALU.add)
                chain.link(nc.vector.tensor_tensor(pp[:], dt[:], le[:], ALU.mult))
                nc.vector.tensor_scalar(dtm[:], dtm[:], -1.0 / H, None, ALU.mult)
                chain.link(nc.vector.tensor_copy(dA2[:, b % 2], dA[:]))
                nc.vector.tensor_tensor(th[:], rest[:, :, TH:TH + NR], bc_last(dtm[:], NR), ALU.mult)
                nc.vector.tensor_tensor(qq[:], dt[:], pp[:], ALU.subtract).then_inc(s_qq, 1)
                dve.wait_ge(s_brr, b + 1)
                chain.link(nc.vector.tensor_tensor(
                    bn, rest[:, :, 0:2 * NS].rearrange("p t (a n) -> p t a n", a=2),
                    brr[:].rearrange("p (t a) -> p t a", t=TB).unsqueeze(3).to_broadcast([P, TB, 2, NS]), ALU.mult))
                chain.link(nc.vector.tensor_tensor(
                    bn.rearrange("p t a n -> p t (a n)"), bn.rearrange("p t a n -> p t (a n)"),
                    bc_mid(nbias, TB), ALU.mult))

            def angles(b):
                dve.wait_ge(s_f, full(b, CUM))
                cum = front(CUM)[:, 0:TB * NR].rearrange("p (t n) -> p t n", t=TB)
                chain.link(nc.vector.tensor_scalar(kk[:], cum, float(1 / (2 * np.pi)), ROUND, ALU.mult, ALU.add))
                chain.link(nc.vector.tensor_scalar(kk[:], kk[:], ROUND, None, ALU.subtract))
                chain.link(nc.vector.scalar_tensor_tensor(arg[:], kk[:], -TWO_PI_HI, cum, ALU.mult, ALU.add))
                chain.link(nc.vector.scalar_tensor_tensor(arg[:], kk[:], -TWO_PI_LO, arg[:], ALU.mult, ALU.add))
                nc.vector.tensor_scalar(arg[:], arg[:], 3.1415925, -3.1415925, ALU.min, ALU.max).then_inc(s_arg, 1)

            def seen_later(b):
                dve.wait_ge(s_f, full(b, QS))
                nc.vector.tensor_tensor(gw[:, b % 2], pp[:],
                                        front(QS)[:, 0:TB * H].rearrange("p (t h) -> p t h", t=TB), ALU.add).then_inc(s_g, 1)

            def rotate(b):
                dve.wait_ge(s_trig, b + 1)
                x1, x2 = bn[:, :, :, 0:NR], bn[:, :, :, NR:]
                cosb = cs[:].unsqueeze(2).to_broadcast([P, TB, 2, NR])
                sinb = sn[:].unsqueeze(2).to_broadcast([P, TB, 2, NR])
                nc.vector.tensor_tensor(rt[:, 0], x1, cosb, ALU.mult)
                nc.vector.tensor_tensor(rt[:, 1], x2, sinb, ALU.mult)
                nc.vector.tensor_tensor(rt[:, 2], x1, sinb, ALU.mult)
                chain.link(nc.vector.tensor_tensor(rt[:, 3], x2, cosb, ALU.mult))
                nc.vector.tensor_tensor(br[:, :, :, 0:NR], rt[:, 0], rt[:, 1], ALU.subtract)
                nc.vector.tensor_tensor(br[:, :, :, NR:], rt[:, 2], rt[:, 3], ALU.add).then_inc(s_br, 1)
                dve.wait_ge(s_br, b + 1)
                dve.wait_ge(s_dcs, b + 1)
                nc.vector.tensor_tensor(ww[:, b % 2], ww[:, b % 2], gw[:, b % 2], ALU.mult)
                chain.link(nc.vector.tensor_tensor(bsq[:, 0:TB, :], br[:, :, 0, :], br[:, :, 1, :], ALU.mult))
                chain.link(nc.vector.tensor_reduce(cbd[:], bsq[:, 0:TB, :], AX, ALU.add))
                nc.vector.tensor_tensor(dl[:, b % 2], pp[:], bc_last(cbd[:], H), ALU.mult).then_inc(s_front, 1)

            def mask_cb(b):
                dve.wait_ge(s_f, full(b, CBT))
                for c in range(NC):
                    rows = slice(c * Q, (c + 1) * Q)
                    for i in range(NQ):
                        ins = nc.vector.tensor_tensor(
                            cbm[i * Q:(i + 1) * Q, b % 2, :].rearrange("p (k t) -> p k t", t=P)[:, :, rows],
                            front(CBT)[rows, :].rearrange("p (k t) -> p k t", t=P)[:, :, rows],
                            bc_mid(mask_st[rows], TB), ALU.mult)
                ins.then_inc(s_cbm, 1)
                chain.end()

            def prepare(b, tile, t):
                if t == 0:
                    dve.wait_ge(s_front, b + 1)
                    dve.wait_ge(s_xg, TB * (b + 1))
                if not (isinstance(tile, int) and tile < 2):
                    dve.wait_ge(s_Y, ST * tile - ST)
                x = xg[:, b % 2, t, :].rearrange("p (h q) -> p h q", q=HP)
                for c in range(NC):
                    for i in range(NQ):
                        src = slice(c * Q, (c + 1) * Q)
                        nc.vector.tensor_tensor(
                            xbd[i * Q:(i + 1) * Q, t % 2, c, :, i, :],
                            x[src].rearrange("p (g i) q -> p i g q", i=NQ)[:, i],
                            heads(gw[src, b % 2, t, :].rearrange("p (g i) -> p i g", i=NQ)[:, i]), ALU.mult)
                nc.vector.tensor_tensor(xw[:, t % 2, :].rearrange("p (h q) -> p h q", q=HP), x,
                                        heads(ww[:, b % 2, t, :]), ALU.mult)
                nc.vector.tensor_tensor(xdl[:, t % 2, :].rearrange("p (h q) -> p h q", q=HP), x,
                                        heads(dl[:, b % 2, t, :]), ALU.mult).then_inc(s_prep, 1)

            def mask(b, tile, t, j):
                dve.wait_ge(s_e, ST * tile + j + 1)
                if t == 0 and j == 0:
                    dve.wait_ge(s_cbm, b + 1)
                nc.vector.tensor_tensor(e[:, j], e[:, j], bc_mid(cbm[:, b % 2, t * P:(t + 1) * P], NG),
                                        ALU.mult).then_inc(s_em, 1)

            def carry_states(b, tile, t, pair):
                if t == 0 and pair == 0:
                    if not is_first(b):
                        dve.wait_ge(s_pt, 2 * tile)
                    nc.vector.memset(st[:, :, 0, :], 0.0).then_inc(s_z0, 1)
                    dve.wait_ge(s_z0, b + 1)
                    dve.wait_ge(s_ecs, NG * (b + 1))
                elif pair == 0:
                    dve.wait_ge(s_pt, 2 * tile)
                dve.wait_ge(s_S, 2 * tile + pair + 1)
                base = 4 * NC * tile + 2 * NC * pair
                for c in range(NC):
                    for i in range(2):
                        g, n = 2 * pair + i, 2 * c + i
                        if c > 0:
                            dve.wait_ge(s_rs, base + n - 1)
                        slot = NC * (t % 2) + c
                        at = t * P + c * Q + Q - 1
                        nc.vector.scalar_tensor_tensor(st[:, g, (slot + 1) % (2 * NC), :], st[:, g, slot, :],
                                                       ecs[:, b % 2, g, at:at + 1], sps[:, i, c, :], ALU.mult,
                                                       ALU.add).then_inc(s_rs, 1)

            def combine(b, tile, t):
                dve.wait_ge(s_yo, tile + 1)
                nc.vector.tensor_tensor(y[:], ops[:], ecs[:, b % 2, :, t * P:(t + 1) * P],
                                        ALU.mult).then_inc(s_t1, 1)
                dve.wait_ge(s_t1, tile + 1)
                dve.wait_ge(s_Y, ST * (tile + 1))
                if not is_first(tile):
                    dve.wait_ge(s_tail, tile)
                nc.vector.tensor_tensor(y[:], yps[:], y[:], ALU.add).then_inc(s_y, 1)
                dve.wait_ge(s_y, tile + 1)
                dve.wait_ge(s_sz, NG * (b + 1))
                nc.vector.tensor_tensor(gT[:], y[:], szT[:, b % 2, :, t * P:(t + 1) * P], ALU.mult).then_inc(s_gT, 1)

            def mean_square(tile):
                dve.wait_ge(s_tail, tile + 1)
                nc.vector.tensor_scalar(ms[:], mps[:, D:D + 1], 1.0 / DI, RMS_EPS, ALU.mult, ALU.add).then_inc(s_ms, 1)

            def update(tile):
                dve.wait_ge(s_rr, tile + 1)
                nc.vector.scalar_tensor_tensor(x_res[:, tile, :], mps[:, 0:D], rr[:], x_res[:, tile, :], ALU.mult,
                                               ALU.add).then_inc(s_x, 1)

            pieces = {(0, 1): statistics, (1, 1): normalise,
                      (3, 0): lambda b: rest_of_z(b, 0), (3, 1): lambda b: rest_of_z(b, 1), (5, 0): raw, (7, 1): rates,
                      (8, 1): lambda b: (angles(b), seen_later(b)), (11, 1): rotate, (12, 1): mask_cb}

            def sequence(b, ahead):
                for t in range(TB):
                    tile = TB * b + t
                    for j in range(ST):
                        piece = [pieces.get((ST * t + j, i)) if ahead else None for i in range(2)]
                        two_back = not (is_first(b) and t < 2)
                        if j == 0 and two_back:
                            mean_square(tile - 2)
                        if j == 1 and two_back:
                            update(tile - 2)
                        if piece[0]:
                            piece[0](b + 1)
                        if j == 1 and not (is_first(b) and t == 0):
                            combine(b if t else b - 1, tile - 1, (t - 1) % TB)
                        if j < 2:
                            carry_states(b, tile, t, j)
                        mask(b, tile, t, j)
                        if piece[1]:
                            piece[1](b + 1)
                        if j == 2 and (t + 1 < TB or ahead):
                            prepare(b if t + 1 < TB else b + 1, tile + 1, (t + 1) % TB)
                if not ahead:
                    mean_square(tile - 1)
                    update(tile - 1)
                    combine(b, tile, t)
                    mean_square(tile)
                    update(tile)

            statistics(0)
            normalise(0)
            rest_of_z(0, 0)
            rest_of_z(0, 1)
            dve.wait_ge(weights.loaded, 16 * weights.n_loads)
            dve.wait_ge(s_const, NCONST)
            nc.vector.tensor_tensor(strict.rearrange("p c t -> p (c t)"), tri_c[:].rearrange("p c t -> p (c t)"),
                                    ident[:], ALU.subtract).then_inc(s_mask, 1)
            dve.wait_ge(s_mask, 1)
            nc.vector.tensor_reduce(mask_st[:], strict.rearrange("p c t -> p t c"), AX, ALU.add).then_inc(s_mask, 1)
            nc.vector.tensor_reduce(mask_rs[:], after[:].rearrange("p c t -> p t c"), AX, ALU.add).then_inc(s_mask, 1)
            nc.vector.tensor_scalar(nbias[:, NS:], nbias[:, NS:], float(NS) ** -0.5, None, ALU.mult)
            dve.wait_ge(s_ae, 1)
            nc.vector.tensor_scalar(a_neg[:], a_exp[:], -1.0, None, ALU.mult).then_inc(s_mask, 1)
            dve.wait_ge(s_mask, 4)
            for (n, _), piece in pieces.items():
                if n > 3:
                    piece(0)
            prepare(0, 0, 0)
            sequence(0, True)
            with dve.Fori(1, NB - 1) as b:
                sequence(b, True)
            sequence(NB - 1, False)


def hybrid_block(nc, ins, kept, out):
    with ExitStack() as ctx:
        x_res = ctx.enter_context(nc.sbuf_tensor("x_res", [P, NT, D], F32))
        ident = ctx.enter_context(nc.sbuf_tensor("ident", [P, P], F32))
        a = {n[len("L0_attn_a_"):]: v for n, v in ins.items() if n.startswith("L0_attn_a_")}
        s = {n[len("L0_attn_b_"):]: v for n, v in ins.items() if n.startswith("L0_attn_b_")}
        f = {n[len("L0_ffn_"):]: v for n, v in ins.items() if n.startswith("L0_ffn_")}
        bias = FfnBiases(nc, ctx, f)
        signals = FfnSignals(nc, ctx, f)
        scale = Scales(nc, ctx)
        with ExitStack() as before_ffn2:
            with ExitStack() as before_ssd:
                ssd = SsdWeights(nc, before_ffn2, before_ssd, s)
                ffn1 = FfnWeights(nc, before_ssd, f, signals, kept, 1)

                def load_later(sp):
                    ffn1.load(sp)
                    ssd.load(sp)

                with ExitStack() as first:
                    split = WeightSplit(nc, first, ffn1, ssd, scale, bias)
                    phase_mamba(nc, x_res, ident, a, a["x"], load_later, bias, split)
                retired = phase_ffn(nc, x_res, ident, bias, ffn1, scale, False, "f1_")
            phase_ssd(nc, x_res, ident, ssd, scale, retired)
        ffn2 = FfnWeights(nc, ctx, f, signals, kept, 2)
        phase_ffn(nc, x_res, ident, bias, ffn2, scale, True, "f2_", out)


_TURNED = ("L0_attn_a_in_proj_w", "L0_attn_a_x_proj_w", "L0_attn_a_dt_proj_w", "L0_attn_a_out_proj_w")


def kernel(**inputs):
    import numpy as np
    import concourse.bacc as bacc
    from concourse import mybir as mb
    from concourse.bass_utils import run_bass_kernel_spmd

    nc = bacc.Bacc("TRN2", target_bir_lowering=False, num_devices=1)
    arrays, aps = {}, {}
    for name, value in inputs.items():
        a = np.asarray(value)
        a = np.ascontiguousarray(a.T if name in _TURNED else a)
        arrays["in_" + name] = a
        aps[name] = nc.dram_tensor("in_" + name, a.shape, mb.dt.from_np(a.dtype), kind="ExternalInput").ap()
    out = nc.dram_tensor("out_x", (NB, T, D), F32, kind="ExternalOutput").ap()
    E = inputs["L0_ffn_expert_w"].shape[0]
    kept = nc.dram_tensor("kept", (E // FfnSignals.EB, P, 2, KD, FfnSignals.EB * D), F16, kind="Internal").ap()
    hybrid_block(nc, aps, kept, out)
    r = run_bass_kernel_spmd(nc, [arrays], core_ids=[0])
    return r.results[0]["out_x"]
```
